# Optimizing a Trainium2 kernel written in Bass

```python
import numpy as np
import jax
import jax.numpy as jnp

def _softmax(x, axis=-1):
    return jax.nn.softmax(x, axis=axis)

def _gelu(x):
    return jax.nn.gelu(x, approximate=True)

def _silu(x):
    return jax.nn.silu(x)

def _sigmoid(x):
    return jax.nn.sigmoid(x)

def _layernorm(x, axis=-1, eps=1e-05):
    m = jnp.mean(x, axis=axis, keepdims=True)
    v = jnp.var(x, axis=axis, keepdims=True)
    return (x - m) / jnp.sqrt(v + eps)

def _scatter_add(tgt, idx, src, axis=0):
    return tgt.at[idx].add(src)

def _segment_sum(src, seg, n):
    return jax.ops.segment_sum(src, seg, n)
kernel_name = 'mk_adaln_ffn_d4_seqx_r4_2ff9f0'

def setup_inputs(seed: int=0):
    np.random.seed(seed)
    _w = jnp.asarray

    def _rec_inputs():
        import jax
        import jax.numpy as jnp
        _rk = jax.random.key(seed)
        x = -0.0002928 + 1 * jax.random.normal(jax.random.fold_in(_rk, 1), (4, 512, 256), jnp.float32)
        _lenS = 512 - jax.random.randint(jax.random.fold_in(_rk, 7), (4,), 0, max(1, 512 // 4) + 1, jnp.int32)
        _lenS2 = 512 - jax.random.randint(jax.random.fold_in(_rk, 8), (4,), 0, max(1, 512 // 4) + 1, jnp.int32)
        cond_1024 = -0.00356592 + 0.997978 * jax.random.normal(jax.random.fold_in(_rk, 11), (4, 256), jnp.float32)
        return (x, cond_1024)
    x, cond_1024 = _rec_inputs()

    def _L0_cond_setup():
        import jax, jax.numpy as jnp
        import numpy as np
        B, T, D = (128, 32, 256)
        ADA, INTER, RANK = (256, 256, 8)
        LN_EPS = 1e-05

        def _layernorm(x, g, b):
            mu = jnp.mean(x, axis=-1, keepdims=True)
            var = jnp.var(x, axis=-1, keepdims=True)
            return (x - mu) * jax.lax.rsqrt(var + LN_EPS) * g + b
        key = jax.random.key(seed)
        ks = jax.random.split(key, 9)
        return {'x': jax.random.normal(ks[0], (B, T, D), dtype=jnp.float32), 'ada_emb': jax.random.normal(ks[1], (B, ADA), dtype=jnp.float32), 'base_layer': jax.random.normal(ks[2], (D, D), dtype=jnp.float32), 'w1': jax.random.normal(ks[3], (ADA, INTER), dtype=jnp.float32) * 0.02, 'b1': jnp.zeros((INTER,), dtype=jnp.float32), 'w2': jax.random.normal(ks[4], (INTER, 2 * D * RANK), dtype=jnp.float32) * 0.02, 'b2': jnp.zeros((2 * D * RANK,), dtype=jnp.float32), 'ln_g': jnp.ones((ADA,), dtype=jnp.float32), 'ln_b': jnp.zeros((ADA,), dtype=jnp.float32)}
    _L0_cond_all = _L0_cond_setup()
    _L0_cond_in = {k: v for k, v in _L0_cond_all.items() if k in ('base_layer', 'w1', 'b1', 'w2', 'b2', 'ln_g', 'ln_b')}
    del _L0_cond_all

    def _L0_ffn_setup():
        import jax, jax.numpy as jnp
        import numpy as np
        D_MODEL = 256
        N_EXPERTS = 8
        TOP_K = 2
        BOTTLENECK = 64
        B, S = (2, 1024)
        ADAPTER_SCALE = 0.5

        def _moe_forward(x, w_gate, w_noise, Wd, bd, Wu, bu):
            b, s, d = x.shape
            xf = x.reshape(-1, d)
            T = xf.shape[0]
            clean_logits = xf @ w_gate
            logits = clean_logits
            k1 = min(TOP_K + 1, N_EXPERTS)
            top_logits, top_idx = jax.lax.top_k(logits, k1)
            top_k_logits = top_logits[:, :TOP_K]
            top_k_idx = top_idx[:, :TOP_K]
            top_k_gates = jax.nn.softmax(top_k_logits, axis=-1)
            rows = jnp.arange(T)[:, None]
            gates = jnp.zeros((T, N_EXPERTS), dtype=top_k_gates.dtype)
            gates = gates.at[rows, top_k_idx].set(top_k_gates)
            h = jax.nn.relu(jnp.einsum('td,edb->teb', xf, Wd) + bd[None, :, :])
            y = jnp.einsum('teb,ebd->ted', h, Wu) + bu[None, :, :]
            y = ADAPTER_SCALE * y
            out = jnp.einsum('te,ted->td', gates, y)
            return out.reshape(b, s, d)
        key = jax.random.key(seed)
        ks = jax.random.split(key, 8)
        sd = 0.02
        x = jax.random.normal(ks[0], (B, S, D_MODEL), dtype=jnp.float32)
        w_gate = jax.random.normal(ks[1], (D_MODEL, N_EXPERTS), dtype=jnp.float32) * sd
        w_noise = jax.random.normal(ks[2], (D_MODEL, N_EXPERTS), dtype=jnp.float32) * sd
        Wd = jax.random.normal(ks[3], (N_EXPERTS, D_MODEL, BOTTLENECK), dtype=jnp.float32) * sd
        bd = jnp.zeros((N_EXPERTS, BOTTLENECK), dtype=jnp.float32)
        Wu = jax.random.normal(ks[4], (N_EXPERTS, BOTTLENECK, D_MODEL), dtype=jnp.float32) * sd
        bu = jnp.zeros((N_EXPERTS, D_MODEL), dtype=jnp.float32)
        return {'x': x, 'w_gate': w_gate, 'w_noise': w_noise, 'Wd': Wd, 'bd': bd, 'Wu': Wu, 'bu': bu}
    _L0_ffn_all = _L0_ffn_setup()
    _L0_ffn_in = {k: v for k, v in _L0_ffn_all.items() if k in ('w_gate', 'w_noise', 'Wd', 'bd', 'Wu', 'bu')}
    del _L0_ffn_all

    def _L1_cond_setup():
        import jax, jax.numpy as jnp
        import numpy as np
        D = 256
        H = 256
        key = jax.random.key(seed)
        k1, k2, k3, k4 = jax.random.split(key, 4)
        x = jax.random.normal(k1, (32, 128, D), dtype=jnp.float32)
        h0 = jax.random.normal(k2, (32, H), dtype=jnp.float32)
        Wx = jax.random.normal(k3, (D, 4 * H), dtype=jnp.float32) / jnp.sqrt(float(D))
        Wh = jax.random.normal(k4, (H, 4 * H), dtype=jnp.float32) / jnp.sqrt(float(H))
        b = jnp.zeros((4 * H,), dtype=jnp.float32)
        return {'x': x, 'h0': h0, 'Wx': Wx, 'Wh': Wh, 'b': b}
    _L1_cond_all = _L1_cond_setup()
    _L1_cond_in = {k: v for k, v in _L1_cond_all.items() if k in ('Wx', 'Wh', 'b')}
    del _L1_cond_all

    def _L1_ffn_setup():
        import jax, jax.numpy as jnp
        import numpy as np
        B, T, C = (2, 256, 256)
        H = 1024
        E_R, E_S, K = (8, 2, 2)

        def _rmsnorm(x, g):
            eps = jnp.finfo(x.dtype).eps
            return x * jax.lax.rsqrt(jnp.mean(x * x, axis=-1, keepdims=True) + eps) * g

        def _experts_mlp(x, g, W1, b1, W2, b2):
            xn = _rmsnorm(x, g)
            h = jnp.einsum('btc,ech->bteh', xn, W1) + b1
            h = jax.nn.gelu(h, approximate=False)
            return jnp.einsum('bteh,ehc->btec', h, W2) + b2
        key = jax.random.key(seed)
        ks = jax.random.split(key, 12)
        s = 0.02
        return {'u': jax.random.normal(ks[0], (B, T, C), dtype=jnp.float32), 'g_shared': jnp.ones((C,), jnp.float32), 'W1_s': jax.random.normal(ks[1], (E_S, C, H), jnp.float32) * s, 'b1_s': jax.random.normal(ks[2], (E_S, H), jnp.float32) * s, 'W2_s': jax.random.normal(ks[3], (E_S, H, C), jnp.float32) * s, 'b2_s': jax.random.normal(ks[4], (E_S, C), jnp.float32) * s, 'g_routed': jnp.ones((C,), jnp.float32), 'W1_r': jax.random.normal(ks[5], (E_R, C, H), jnp.float32) * s, 'b1_r': jax.random.normal(ks[6], (E_R, H), jnp.float32) * s, 'W2_r': jax.random.normal(ks[7], (E_R, H, C), jnp.float32) * s, 'b2_r': jax.random.normal(ks[8], (E_R, C), jnp.float32) * s, 'centroids': jax.random.normal(ks[9], (C, E_R), jnp.float32) * s}
    _L1_ffn_all = _L1_ffn_setup()
    _L1_ffn_in = {k: v for k, v in _L1_ffn_all.items() if k in ('g_shared', 'W1_s', 'b1_s', 'W2_s', 'b2_s', 'g_routed', 'W1_r', 'b1_r', 'W2_r', 'b2_r', 'centroids')}
    del _L1_ffn_all

    def _L2_cond_setup():
        import jax, jax.numpy as jnp
        import numpy as np
        B, S, I, H = (16, 512, 256, 256)
        key = jax.random.key(seed)
        ks = jax.random.split(key, 6)
        scale_ih = 1.0 / np.sqrt(I)
        scale_hh = 1.0 / np.sqrt(H)
        return {'x': jax.random.normal(ks[0], (B, S, I), dtype=jnp.float32), 'hx': jax.random.normal(ks[1], (B, H), dtype=jnp.float32), 'W_ih': jax.random.normal(ks[2], (H, I), dtype=jnp.float32) * scale_ih, 'W_hh': jax.random.normal(ks[3], (H, H), dtype=jnp.float32) * scale_hh, 'b_ih': jax.random.normal(ks[4], (H,), dtype=jnp.float32) * scale_ih, 'b_hh': jax.random.normal(ks[5], (H,), dtype=jnp.float32) * scale_hh}
    _L2_cond_all = _L2_cond_setup()
    _L2_cond_in = {k: v for k, v in _L2_cond_all.items() if k in ('W_ih', 'W_hh', 'b_ih', 'b_hh')}
    del _L2_cond_all

    def _L2_ffn_setup():
        import jax, jax.numpy as jnp
        import numpy as np
        B, S, D, O, E, K = (4, 512, 256, 256, 8, 2)
        key = jax.random.key(seed)
        ks = jax.random.split(key, 5)
        scale_in = 1.0 / np.sqrt(D)
        x = jax.random.normal(ks[0], (B, S, D), dtype=jnp.float32)
        gate_w = jax.random.uniform(ks[1], (E, D), jnp.float32, -scale_in, scale_in)
        gate_b = jax.random.uniform(ks[2], (E,), jnp.float32, -scale_in, scale_in)
        expert_w = jax.random.uniform(ks[3], (E, D, O), jnp.float32, -scale_in, scale_in)
        expert_b = jax.random.uniform(ks[4], (E, O), jnp.float32, -scale_in, scale_in)
        return {'x': x, 'gate_w': gate_w, 'gate_b': gate_b, 'expert_w': expert_w, 'expert_b': expert_b}
    _L2_ffn_all = _L2_ffn_setup()
    _L2_ffn_in = {k: v for k, v in _L2_ffn_all.items() if k in ('gate_w', 'gate_b', 'expert_w', 'expert_b')}
    del _L2_ffn_all

    def _L3_cond_setup():
        import jax, jax.numpy as jnp
        import numpy as np
        RANK = 8
        LN_EPS = 1e-05
        key = jax.random.key(seed)
        ks = jax.random.split(key, 8)
        B, T, D = (16, 256, 256)
        A = 256
        I = 256
        OUT = D * RANK * 4
        s = 0.02
        return {'x': jax.random.normal(ks[0], (B, T, D), jnp.float32), 'ada_emb': jax.random.normal(ks[1], (B, A), jnp.float32), 'base_up': jax.random.normal(ks[2], (D, D), jnp.float32) * s, 'base_down': jax.random.normal(ks[3], (D, D), jnp.float32) * s, 'ln_gamma': jnp.ones((A,), jnp.float32), 'ln_beta': jnp.zeros((A,), jnp.float32), 'W1': jax.random.normal(ks[4], (A, I), jnp.float32) / np.sqrt(A), 'bias1': jnp.zeros((I,), jnp.float32), 'W2': jax.random.normal(ks[5], (I, OUT), jnp.float32) / np.sqrt(I), 'bias2': jnp.zeros((OUT,), jnp.float32)}
    _L3_cond_all = _L3_cond_setup()
    _L3_cond_in = {k: v for k, v in _L3_cond_all.items() if k in ('base_up', 'base_down', 'ln_gamma', 'ln_beta', 'W1', 'bias1', 'W2', 'bias2')}
    del _L3_cond_all

    def _L3_ffn_setup():
        import jax, jax.numpy as jnp
        import numpy as np
        EPS = 1e-05

        def _ln(x, g, b):
            mu = jnp.mean(x, axis=-1, keepdims=True)
            var = jnp.mean(jnp.square(x - mu), axis=-1, keepdims=True)
            return (x - mu) * jax.lax.rsqrt(var + EPS) * g + b

        def _forward(x, index_b, index_t, sw1, sb1, sw2, sb2, sw3, sb3, s_ln_g, s_ln_b, sg_w, sg_b, eg_w, eg_b, exp_bias, ew1, eb1, ew2, eb2, ew3, eb3, sel_ln_g, sel_ln_b):
            x1 = jnp.einsum('btd,hd->bth', x, sw1) + sb1
            x2 = jnp.einsum('btd,hd->bth', x, sw2) + sb2
            sh = _ln(jax.nn.silu(x1) * x2, s_ln_g, s_ln_b)
            shared_out = jnp.einsum('bth,dh->btd', sh, sw3) + sb3
            x_moe = x[index_b, index_t]
            shared_scores = jax.nn.sigmoid(x_moe @ sg_w.T + sg_b)
            expert_scores = jax.nn.sigmoid(x_moe @ eg_w.T + eg_b)
            top1_idx = jnp.argmax(expert_scores + exp_bias, axis=-1)
            top1_score = jnp.take_along_axis(expert_scores, top1_idx[:, None], axis=-1)
            weights = jax.nn.softmax(jnp.concatenate([shared_scores, top1_score], axis=-1), axis=-1)
            shared_w, expert_w = (weights[:, 0], weights[:, 1])
            shared_moe_out = shared_out[index_b, index_t] * shared_w[:, None]
            h1 = jnp.einsum('md,ehd->meh', x_moe, ew1) + eb1
            h2 = jnp.einsum('md,ehd->meh', x_moe, ew2) + eb2
            z = _ln(jax.nn.silu(h1) * h2, sel_ln_g, sel_ln_b)
            out_all = jnp.einsum('meh,edh->med', z, ew3) + eb3
            expert_out = jnp.take_along_axis(out_all, top1_idx[:, None, None], axis=1)[:, 0]
            expert_moe_out = expert_out * expert_w[:, None]
            final_out = shared_out.at[index_b, index_t].set(shared_moe_out + expert_moe_out)
            return final_out
        B, T, D, E, H, M = (2, 512, 256, 8, 128, 512)
        key = jax.random.key(seed)
        ks = jax.random.split(key, 24)
        s = 0.02
        inp = {}
        inp['x'] = jax.random.normal(ks[0], (B, T, D), jnp.float32)
        flat = jnp.arange(M, dtype=jnp.int32) * 2
        inp['index_b'] = flat // T
        inp['index_t'] = flat % T
        inp['sw1'] = jax.random.normal(ks[1], (H, D), jnp.float32) * s
        inp['sb1'] = jnp.zeros((H,), jnp.float32)
        inp['sw2'] = jax.random.normal(ks[2], (H, D), jnp.float32) * s
        inp['sb2'] = jnp.zeros((H,), jnp.float32)
        inp['sw3'] = jax.random.normal(ks[3], (D, H), jnp.float32) * s
        inp['sb3'] = jnp.zeros((D,), jnp.float32)
        inp['s_ln_g'] = jnp.ones((H,), jnp.float32)
        inp['s_ln_b'] = jnp.zeros((H,), jnp.float32)
        inp['sg_w'] = jax.random.normal(ks[4], (1, D), jnp.float32) * s
        inp['sg_b'] = jnp.zeros((1,), jnp.float32)
        inp['eg_w'] = jax.random.normal(ks[5], (E, D), jnp.float32) * s
        inp['eg_b'] = jnp.zeros((E,), jnp.float32)
        inp['exp_bias'] = jnp.zeros((E,), jnp.float32)
        inp['ew1'] = jax.random.normal(ks[6], (E, H, D), jnp.float32) * s
        inp['eb1'] = jnp.zeros((E, H), jnp.float32)
        inp['ew2'] = jax.random.normal(ks[7], (E, H, D), jnp.float32) * s
        inp['eb2'] = jnp.zeros((E, H), jnp.float32)
        inp['ew3'] = jax.random.normal(ks[8], (E, D, H), jnp.float32) * s
        inp['eb3'] = jnp.zeros((E, D), jnp.float32)
        inp['sel_ln_g'] = jnp.ones((H,), jnp.float32)
        inp['sel_ln_b'] = jnp.zeros((H,), jnp.float32)
        return inp
    _L3_ffn_all = _L3_ffn_setup()
    _L3_ffn_in = {k: v for k, v in _L3_ffn_all.items() if k in ('index_b', 'index_t', 'sw1', 'sb1', 'sw2', 'sb2', 'sw3', 'sb3', 's_ln_g', 's_ln_b', 'sg_w', 'sg_b', 'eg_w', 'eg_b', 'exp_bias', 'ew1', 'eb1', 'ew2', 'eb2', 'ew3', 'eb3', 'sel_ln_g', 'sel_ln_b')}
    del _L3_ffn_all
    return {'x': x, 'cond_1024': cond_1024, 'L0_cond_base_layer': _L0_cond_in['base_layer'], 'L0_cond_w1': _L0_cond_in['w1'], 'L0_cond_b1': _L0_cond_in['b1'], 'L0_cond_w2': _L0_cond_in['w2'], 'L0_cond_b2': _L0_cond_in['b2'], 'L0_cond_ln_g': _L0_cond_in['ln_g'], 'L0_cond_ln_b': _L0_cond_in['ln_b'], 'L0_ffn_w_gate': _L0_ffn_in['w_gate'], 'L0_ffn_w_noise': _L0_ffn_in['w_noise'], 'L0_ffn_Wd': _L0_ffn_in['Wd'], 'L0_ffn_bd': _L0_ffn_in['bd'], 'L0_ffn_Wu': _L0_ffn_in['Wu'], 'L0_ffn_bu': _L0_ffn_in['bu'], 'L1_cond_Wx': _L1_cond_in['Wx'], 'L1_cond_Wh': _L1_cond_in['Wh'], 'L1_cond_b': _L1_cond_in['b'], 'L1_ffn_g_shared': _L1_ffn_in['g_shared'], 'L1_ffn_W1_s': _L1_ffn_in['W1_s'], 'L1_ffn_b1_s': _L1_ffn_in['b1_s'], 'L1_ffn_W2_s': _L1_ffn_in['W2_s'], 'L1_ffn_b2_s': _L1_ffn_in['b2_s'], 'L1_ffn_g_routed': _L1_ffn_in['g_routed'], 'L1_ffn_W1_r': _L1_ffn_in['W1_r'], 'L1_ffn_b1_r': _L1_ffn_in['b1_r'], 'L1_ffn_W2_r': _L1_ffn_in['W2_r'], 'L1_ffn_b2_r': _L1_ffn_in['b2_r'], 'L1_ffn_centroids': _L1_ffn_in['centroids'], 'L2_cond_W_ih': _L2_cond_in['W_ih'], 'L2_cond_W_hh': _L2_cond_in['W_hh'], 'L2_cond_b_ih': _L2_cond_in['b_ih'], 'L2_cond_b_hh': _L2_cond_in['b_hh'], 'L2_ffn_gate_w': _L2_ffn_in['gate_w'], 'L2_ffn_gate_b': _L2_ffn_in['gate_b'], 'L2_ffn_expert_w': _L2_ffn_in['expert_w'], 'L2_ffn_expert_b': _L2_ffn_in['expert_b'], 'L3_cond_base_up': _L3_cond_in['base_up'], 'L3_cond_base_down': _L3_cond_in['base_down'], 'L3_cond_ln_gamma': _L3_cond_in['ln_gamma'], 'L3_cond_ln_beta': _L3_cond_in['ln_beta'], 'L3_cond_W1': _L3_cond_in['W1'], 'L3_cond_bias1': _L3_cond_in['bias1'], 'L3_cond_W2': _L3_cond_in['W2'], 'L3_cond_bias2': _L3_cond_in['bias2'], 'L3_ffn_index_b': _L3_ffn_in['index_b'], 'L3_ffn_index_t': _L3_ffn_in['index_t'], 'L3_ffn_sw1': _L3_ffn_in['sw1'], 'L3_ffn_sb1': _L3_ffn_in['sb1'], 'L3_ffn_sw2': _L3_ffn_in['sw2'], 'L3_ffn_sb2': _L3_ffn_in['sb2'], 'L3_ffn_sw3': _L3_ffn_in['sw3'], 'L3_ffn_sb3': _L3_ffn_in['sb3'], 'L3_ffn_s_ln_g': _L3_ffn_in['s_ln_g'], 'L3_ffn_s_ln_b': _L3_ffn_in['s_ln_b'], 'L3_ffn_sg_w': _L3_ffn_in['sg_w'], 'L3_ffn_sg_b': _L3_ffn_in['sg_b'], 'L3_ffn_eg_w': _L3_ffn_in['eg_w'], 'L3_ffn_eg_b': _L3_ffn_in['eg_b'], 'L3_ffn_exp_bias': _L3_ffn_in['exp_bias'], 'L3_ffn_ew1': _L3_ffn_in['ew1'], 'L3_ffn_eb1': _L3_ffn_in['eb1'], 'L3_ffn_ew2': _L3_ffn_in['ew2'], 'L3_ffn_eb2': _L3_ffn_in['eb2'], 'L3_ffn_ew3': _L3_ffn_in['ew3'], 'L3_ffn_eb3': _L3_ffn_in['eb3'], 'L3_ffn_sel_ln_g': _L3_ffn_in['sel_ln_g'], 'L3_ffn_sel_ln_b': _L3_ffn_in['sel_ln_b']}

def reference(x, cond_1024, L0_cond_base_layer, L0_cond_w1, L0_cond_b1, L0_cond_w2, L0_cond_b2, L0_cond_ln_g, L0_cond_ln_b, L0_ffn_w_gate, L0_ffn_w_noise, L0_ffn_Wd, L0_ffn_bd, L0_ffn_Wu, L0_ffn_bu, L1_cond_Wx, L1_cond_Wh, L1_cond_b, L1_ffn_g_shared, L1_ffn_W1_s, L1_ffn_b1_s, L1_ffn_W2_s, L1_ffn_b2_s, L1_ffn_g_routed, L1_ffn_W1_r, L1_ffn_b1_r, L1_ffn_W2_r, L1_ffn_b2_r, L1_ffn_centroids, L2_cond_W_ih, L2_cond_W_hh, L2_cond_b_ih, L2_cond_b_hh, L2_ffn_gate_w, L2_ffn_gate_b, L2_ffn_expert_w, L2_ffn_expert_b, L3_cond_base_up, L3_cond_base_down, L3_cond_ln_gamma, L3_cond_ln_beta, L3_cond_W1, L3_cond_bias1, L3_cond_W2, L3_cond_bias2, L3_ffn_index_b, L3_ffn_index_t, L3_ffn_sw1, L3_ffn_sb1, L3_ffn_sw2, L3_ffn_sb2, L3_ffn_sw3, L3_ffn_sb3, L3_ffn_s_ln_g, L3_ffn_s_ln_b, L3_ffn_sg_w, L3_ffn_sg_b, L3_ffn_eg_w, L3_ffn_eg_b, L3_ffn_exp_bias, L3_ffn_ew1, L3_ffn_eb1, L3_ffn_ew2, L3_ffn_eb2, L3_ffn_ew3, L3_ffn_eb3, L3_ffn_sel_ln_g, L3_ffn_sel_ln_b):
    import jax
    import jax.numpy as jnp

    def _L0_cond_ref(x, ada_emb, base_layer, w1, b1, w2, b2, ln_g, ln_b):
        import jax, jax.numpy as jnp
        import numpy as np
        B, T, D = (128, 32, 256)
        ADA, INTER, RANK = (256, 256, 8)
        LN_EPS = 1e-05

        def _layernorm(x, g, b):
            mu = jnp.mean(x, axis=-1, keepdims=True)
            var = jnp.var(x, axis=-1, keepdims=True)
            return (x - mu) * jax.lax.rsqrt(var + LN_EPS) * g + b
        b, t, d = x.shape
        ae = _layernorm(ada_emb, ln_g, ln_b)
        h = jax.nn.gelu(ae @ w1 + b1, approximate=False)
        xw = h @ w2 + b2
        x_a, x_b = jnp.split(xw, 2, axis=-1)
        x_a = x_a.reshape(b, d, RANK)
        x_b = x_b.reshape(b, d, RANK)
        layer = base_layer[None, :, :] + jnp.einsum('bdr,bkr->bdk', x_a, x_b)
        out = jnp.einsum('btc,bco->bto', x, layer)
        return x + out

    def _L0_ffn_ref(x, w_gate, w_noise, Wd, bd, Wu, bu):
        import jax, jax.numpy as jnp
        import numpy as np
        D_MODEL = 256
        N_EXPERTS = 8
        TOP_K = 2
        BOTTLENECK = 64
        B, S = (2, 1024)
        ADAPTER_SCALE = 0.5

        def _moe_forward(x, w_gate, w_noise, Wd, bd, Wu, bu):
            b, s, d = x.shape
            xf = x.reshape(-1, d)
            T = xf.shape[0]
            clean_logits = xf @ w_gate
            logits = clean_logits
            k1 = min(TOP_K + 1, N_EXPERTS)
            top_logits, top_idx = jax.lax.top_k(logits, k1)
            top_k_logits = top_logits[:, :TOP_K]
            top_k_idx = top_idx[:, :TOP_K]
            top_k_gates = jax.nn.softmax(top_k_logits, axis=-1)
            rows = jnp.arange(T)[:, None]
            gates = jnp.zeros((T, N_EXPERTS), dtype=top_k_gates.dtype)
            gates = gates.at[rows, top_k_idx].set(top_k_gates)
            h = jax.nn.relu(jnp.einsum('td,edb->teb', xf, Wd) + bd[None, :, :])
            y = jnp.einsum('teb,ebd->ted', h, Wu) + bu[None, :, :]
            y = ADAPTER_SCALE * y
            out = jnp.einsum('te,ted->td', gates, y)
            return out.reshape(b, s, d)
        return _moe_forward(x, w_gate, w_noise, Wd, bd, Wu, bu)

    def _L1_cond_ref(x, h0, Wx, Wh, b):
        import jax, jax.numpy as jnp
        import numpy as np
        D = 256
        H = 256
        Hdim = h0.shape[1]
        x_proj = jnp.einsum('ntd,df->ntf', x, Wx) + b

        def step(carry, xp_t):
            prev_h, prev_c = carry
            h_bar = xp_t + prev_h @ Wh
            i = jax.nn.sigmoid(h_bar[:, 0:Hdim])
            f = jax.nn.sigmoid(h_bar[:, Hdim:2 * Hdim])
            o = jax.nn.sigmoid(h_bar[:, 2 * Hdim:3 * Hdim])
            g = jnp.tanh(h_bar[:, 3 * Hdim:4 * Hdim])
            next_c = f * prev_c + i * g
            next_h = o * jnp.tanh(next_c)
            return ((next_h, next_c), next_h)
        c0 = jnp.zeros_like(h0)
        xs = jnp.swapaxes(x_proj, 0, 1)
        _, hs = jax.lax.scan(step, (h0, c0), xs)
        return jnp.swapaxes(hs, 0, 1)

    def _L1_ffn_ref(u, g_shared, W1_s, b1_s, W2_s, b2_s, g_routed, W1_r, b1_r, W2_r, b2_r, centroids):
        import jax, jax.numpy as jnp
        import numpy as np
        B, T, C = (2, 256, 256)
        H = 1024
        E_R, E_S, K = (8, 2, 2)

        def _rmsnorm(x, g):
            eps = jnp.finfo(x.dtype).eps
            return x * jax.lax.rsqrt(jnp.mean(x * x, axis=-1, keepdims=True) + eps) * g

        def _experts_mlp(x, g, W1, b1, W2, b2):
            xn = _rmsnorm(x, g)
            h = jnp.einsum('btc,ech->bteh', xn, W1) + b1
            h = jax.nn.gelu(h, approximate=False)
            return jnp.einsum('bteh,ehc->btec', h, W2) + b2
        h_s = _experts_mlp(u, g_shared, W1_s, b1_s, W2_s, b2_s).sum(axis=-2)
        scores = jax.nn.sigmoid(u @ centroids)
        gpk, i_topk = jax.lax.top_k(scores, K)
        gk = gpk / scores.sum(axis=-1, keepdims=True)
        routed_all = _experts_mlp(u, g_routed, W1_r, b1_r, W2_r, b2_r)
        routed_topk = jnp.take_along_axis(routed_all, i_topk[..., None], axis=2)
        h_r = (gk[..., None] * routed_topk).sum(axis=-2)
        return u + h_s + h_r

    def _L2_cond_ref(x, hx, W_ih, W_hh, b_ih, b_hh):
        import jax, jax.numpy as jnp
        import numpy as np
        B, S, I, H = (16, 512, 256, 256)
        h_term = hx @ W_hh.T + b_hh + b_ih
        x_term = jnp.einsum('bsi,hi->bsh', x, W_ih)
        out = jnp.tanh(x_term + h_term[:, None, :])
        return out

    def _L2_ffn_ref(x, gate_w, gate_b, expert_w, expert_b):
        import jax, jax.numpy as jnp
        import numpy as np
        B, S, D, O, E, K = (4, 512, 256, 256, 8, 2)
        logits = jnp.einsum('bsd,ed->bse', x, gate_w) + gate_b
        if K < E:
            topv, topi = jax.lax.top_k(logits, K)
            keep = jax.nn.one_hot(topi, E, dtype=jnp.float32).sum(axis=-2)
            logits = jnp.where(keep > 0, logits, -jnp.inf)
        gate_score = jax.nn.softmax(logits, axis=-1)
        expert_out = jnp.einsum('bsd,edo->bseo', x, expert_w) + expert_b
        out = jnp.einsum('bseo,bse->bso', expert_out, gate_score)
        return out

    def _L3_cond_ref(x, ada_emb, base_up, base_down, ln_gamma, ln_beta, W1, bias1, W2, bias2):
        import jax, jax.numpy as jnp
        import numpy as np
        RANK = 8
        LN_EPS = 1e-05
        B, T, D = x.shape
        R = RANK
        mu = jnp.mean(ada_emb, axis=-1, keepdims=True)
        var = jnp.mean(jnp.square(ada_emb - mu), axis=-1, keepdims=True)
        c = (ada_emb - mu) / jnp.sqrt(var + LN_EPS) * ln_gamma + ln_beta
        h = jax.nn.gelu(c @ W1 + bias1, approximate=False)
        w = h @ W2 + bias2
        a1, b1, a2, b2 = [t.reshape(B, D, R) for t in jnp.split(w, 4, axis=-1)]
        u = jnp.einsum('btd,bdr->btr', x, a2)
        mid = jnp.einsum('btd,dl->btl', x, base_down) + jnp.einsum('btr,blr->btl', u, b2)
        mid = jax.nn.gelu(mid, approximate=False)
        v = jnp.einsum('blr,btl->btr', b1, mid)
        out = jnp.einsum('btl,kl->btk', mid, base_up) + jnp.einsum('bkr,btr->btk', a1, v)
        return x + out

    def _L3_ffn_ref(x, index_b, index_t, sw1, sb1, sw2, sb2, sw3, sb3, s_ln_g, s_ln_b, sg_w, sg_b, eg_w, eg_b, exp_bias, ew1, eb1, ew2, eb2, ew3, eb3, sel_ln_g, sel_ln_b):
        import jax, jax.numpy as jnp
        import numpy as np
        EPS = 1e-05

        def _ln(x, g, b):
            mu = jnp.mean(x, axis=-1, keepdims=True)
            var = jnp.mean(jnp.square(x - mu), axis=-1, keepdims=True)
            return (x - mu) * jax.lax.rsqrt(var + EPS) * g + b

        def _forward(x, index_b, index_t, sw1, sb1, sw2, sb2, sw3, sb3, s_ln_g, s_ln_b, sg_w, sg_b, eg_w, eg_b, exp_bias, ew1, eb1, ew2, eb2, ew3, eb3, sel_ln_g, sel_ln_b):
            x1 = jnp.einsum('btd,hd->bth', x, sw1) + sb1
            x2 = jnp.einsum('btd,hd->bth', x, sw2) + sb2
            sh = _ln(jax.nn.silu(x1) * x2, s_ln_g, s_ln_b)
            shared_out = jnp.einsum('bth,dh->btd', sh, sw3) + sb3
            x_moe = x[index_b, index_t]
            shared_scores = jax.nn.sigmoid(x_moe @ sg_w.T + sg_b)
            expert_scores = jax.nn.sigmoid(x_moe @ eg_w.T + eg_b)
            top1_idx = jnp.argmax(expert_scores + exp_bias, axis=-1)
            top1_score = jnp.take_along_axis(expert_scores, top1_idx[:, None], axis=-1)
            weights = jax.nn.softmax(jnp.concatenate([shared_scores, top1_score], axis=-1), axis=-1)
            shared_w, expert_w = (weights[:, 0], weights[:, 1])
            shared_moe_out = shared_out[index_b, index_t] * shared_w[:, None]
            h1 = jnp.einsum('md,ehd->meh', x_moe, ew1) + eb1
            h2 = jnp.einsum('md,ehd->meh', x_moe, ew2) + eb2
            z = _ln(jax.nn.silu(h1) * h2, sel_ln_g, sel_ln_b)
            out_all = jnp.einsum('meh,edh->med', z, ew3) + eb3
            expert_out = jnp.take_along_axis(out_all, top1_idx[:, None, None], axis=1)[:, 0]
            expert_moe_out = expert_out * expert_w[:, None]
            final_out = shared_out.at[index_b, index_t].set(shared_moe_out + expert_moe_out)
            return final_out
        return _forward(x, index_b, index_t, sw1, sb1, sw2, sb2, sw3, sb3, s_ln_g, s_ln_b, sg_w, sg_b, eg_w, eg_b, exp_bias, ew1, eb1, ew2, eb2, ew3, eb3, sel_ln_g, sel_ln_b)
    x = x + _L0_ffn_ref(_L0_cond_ref(x, cond_1024, L0_cond_base_layer, L0_cond_w1, L0_cond_b1, L0_cond_w2, L0_cond_b2, L0_cond_ln_g, L0_cond_ln_b), L0_ffn_w_gate, L0_ffn_w_noise, L0_ffn_Wd, L0_ffn_bd, L0_ffn_Wu, L0_ffn_bu)
    x = x + _L1_ffn_ref(_L1_cond_ref(x, cond_1024, L1_cond_Wx, L1_cond_Wh, L1_cond_b), L1_ffn_g_shared, L1_ffn_W1_s, L1_ffn_b1_s, L1_ffn_W2_s, L1_ffn_b2_s, L1_ffn_g_routed, L1_ffn_W1_r, L1_ffn_b1_r, L1_ffn_W2_r, L1_ffn_b2_r, L1_ffn_centroids)
    x = x + _L2_ffn_ref(_L2_cond_ref(x, cond_1024, L2_cond_W_ih, L2_cond_W_hh, L2_cond_b_ih, L2_cond_b_hh), L2_ffn_gate_w, L2_ffn_gate_b, L2_ffn_expert_w, L2_ffn_expert_b)
    x = x + _L3_ffn_ref(_L3_cond_ref(x, cond_1024, L3_cond_base_up, L3_cond_base_down, L3_cond_ln_gamma, L3_cond_ln_beta, L3_cond_W1, L3_cond_bias1, L3_cond_W2, L3_cond_bias2), L3_ffn_index_b, L3_ffn_index_t, L3_ffn_sw1, L3_ffn_sb1, L3_ffn_sw2, L3_ffn_sb2, L3_ffn_sw3, L3_ffn_sb3, L3_ffn_s_ln_g, L3_ffn_s_ln_b, L3_ffn_sg_w, L3_ffn_sg_b, L3_ffn_eg_w, L3_ffn_eg_b, L3_ffn_exp_bias, L3_ffn_ew1, L3_ffn_eb1, L3_ffn_ew2, L3_ffn_eb2, L3_ffn_ew3, L3_ffn_eb3, L3_ffn_sel_ln_g, L3_ffn_sel_ln_b)
    return x

_drawn_inputs = setup_inputs


def setup_inputs(seed=0):
    import zlib

    import numpy as np

    out = dict(_drawn_inputs(seed))
    spreads = {'L0_cond_b1': (0.0, 0.521),
     'L0_cond_b2': (0.0, 0.1),
     'L0_cond_ln_g': (1.0, 0.6),
     'L0_cond_ln_b': (0.0, 0.772),
     'L0_ffn_bd': (0.0, 0.431),
     'L0_ffn_bu': (0.0, 0.1),
     'L1_cond_b': (0.0, 0.1),
     'L1_ffn_g_shared': (1.0, 0.2),
     'L1_ffn_g_routed': (1.0, 0.6),
     'L3_cond_ln_gamma': (1.0, 0.2),
     'L3_cond_ln_beta': (0.0, 0.1),
     'L3_cond_bias1': (0.0, 0.1),
     'L3_cond_bias2': (0.0, 0.1),
     'L3_ffn_sb1': (0.0, 0.8),
     'L3_ffn_sb2': (0.0, 0.8),
     'L3_ffn_sb3': (0.0, 0.1),
     'L3_ffn_s_ln_g': (1.0, 0.2),
     'L3_ffn_s_ln_b': (0.0, 0.426),
     'L3_ffn_eg_b': (0.0, 0.8),
     'L3_ffn_exp_bias': (0.0, 0.1),
     'L3_ffn_eb1': (0.0, 0.8),
     'L3_ffn_eb2': (0.0, 0.8),
     'L3_ffn_eb3': (0.0, 0.277),
     'L3_ffn_sel_ln_g': (1.0, 0.6),
     'L3_ffn_sel_ln_b': (0.0, 0.8)}
    factors = {'L1_ffn_b1_r': 7.659,
     'L1_ffn_b2_r': 3.615,
     'L3_cond_base_up': 5.654,
     'L3_cond_base_down': 7.406}
    for name, (base, spread) in spreads.items():
        noise = np.random.default_rng([zlib.crc32(name.encode()), seed]).standard_normal(out[name].shape)
        drawn = base * np.exp(spread * noise) if base else spread * noise
        out[name] = jnp.asarray(drawn.astype(out[name].dtype))
    for name, factor in factors.items():
        out[name] = (out[name] * factor).astype(out[name].dtype)
    return out
```

```python
from contextlib import ExitStack

import concourse.bass as bass
from concourse import mybir

F32 = mybir.dt.float32
F16 = mybir.dt.float16
I32 = mybir.dt.int32
U32 = mybir.dt.uint32
ALU = mybir.AluOpType
ACT = mybir.ActivationFunctionType
AX = mybir.AxisListType

P = 128
B = 4
T = 512
D = 256
C = D // P
TB = 128
NBLK = T // TB
NT = B * TB
E = 8
R = 8
H1 = 1024
M1 = H1 // P
NE1 = 10
NEW = NE1 + 2
RU = 1024
UPS = 4
GATES = 4 * D
GC = GATES // P
S = 64.0
IS = 1.0 / S
LN_EPS = 1e-5
RMS_EPS = 1.1920928955078125e-07

RESIDENT = [("Wh_ifo", C * 768), ("Wh_g", C * 256), ("Wx", C * GATES), ("ew3", E * D), ("Wd", C * 512),
            ("Wu", 4 * D), ("Wih", C * D), ("sw12", C * D), ("sw3", D), ("wgate", C * E), ("gatew", C * E),
            ("egsg", C * (E + 1))]
OFF = {}
_at = 0
for _n, _w in RESIDENT:
    OFF[_n] = _at
    _at += _w
RES_COLS = _at
RES_UNITS = [(a, min(RU, 1536 - a), S / 2) for a in range(0, 1536, RU)] + \
            [(a, min(RU, RES_COLS - a), S) for a in range(1536, RES_COLS, RU)]
NFACT = 6
F_UNITS = NFACT * C * 2
SETUP_UNITS = F_UNITS + len(RES_UNITS) + UPS
assert SETUP_UNITS % 2 == 0

COLS = [("lstm_b", GC), ("g0", C), ("be0", C), ("b1_0", C), ("g3", C), ("be3", C), ("b1_3", C), ("bih", C), ("bhh", C),
        ("s_g", 1), ("s_b", 1), ("sel_g", 1), ("sel_b", 1), ("fb", NFACT * C * R), ("condT", C * B), ("idx_b", 0)]
ROWS = [("bd", 512), ("gate_b", E), ("egsg_b", E + 1), ("exp_bias", E)]
TMPW = [("w1_0", C * D), ("w1_3", C * D), ("base0", C * D), ("base_down", C * D), ("base_upT", C * D), ("WhhT", C * D),
        ("cent", C * E)]


def offsets(table):
    at, out = 0, {}
    for name, n in table:
        out[name] = at
        at += n
    return out, at


CO, NCOLS = offsets(COLS)
RO, NROWS = offsets(ROWS)
TO, NTMP = offsets(TMPW)

DSTAGES = [("xT", 2), ("y0T", 2), ("log0", 1), ("g0T", 1), ("h0", 8), ("out0", 4), ("x1T", 2),
           ("log1", 4), ("uT", 4), ("xnT", 2), ("g1T", 2), ("bias1", 4), ("down", NE1 * 4), ("x2T", 2), ("log2", 1),
           ("g2T", 2), ("bias2", 4), ("exp2", 16), ("x3T", 2), ("y3T", 2), ("log3", 1), ("g3T", 2),
           ("hid3", 24), ("out3", 24)]
ASTAGES = [("xp", GC), ("up", NE1 * M1), ("z2", 2), ("mid", 2), ("nT", 2)]
DI, ND = offsets(DSTAGES)
AI, NA = offsets(ASTAGES)
DB, AB = 4, 2
assert ND % DB == 0 and NA % AB == 0
DSPLITS = [("xT", 2), ("y0T", 2), ("h0T", 4), ("x1T", 2), ("xnT", 2), ("x2T", 2), ("x3T", 2)]
HI, NH = offsets(DSPLITS)


H0_AT, H0T_AT = (0, 1, 3, 5), (2, 4, 6, 7)


def dpos(stage, i):
    if stage == "h0":
        return DI["h0"] + H0_AT[i]
    if stage == "h0T":
        return DI["h0"] + H0T_AT[i]
    return DI[stage] + i


def adaln_lstm_moe(nc, a, out):
    with ExitStack() as ctx:
        def sb(name, shape, dt=F32):
            return ctx.enter_context(nc.sbuf_tensor(name, shape, dt))

        def sem(name):
            return ctx.enter_context(nc.semaphore(name))

        WH, WL = sb("WH", [P, RES_COLS], F16), sb("WL", [P, RES_COLS], F16)
        EH = [sb(f"EH{i}", [P, 4 * RU], F16) for i in range(2)]
        EL = [sb(f"EL{i}", [P, 4 * RU], F16) for i in range(2)]
        RAW = [sb(f"RAW{i}", [P, RU]) for i in range(2)]
        PARS = sb("PARS", [P, (NE1 + 3) * (C + M1)])
        PARB = [sb(f"PARB{i}", [P, C + M1]) for i in range(2)]
        PG = [sb(f"PG{i}", [P, C]) for i in range(2)]
        DWH = sb("DWH", [P, 3 * C * B * D], F16)
        DWL = sb("DWL", [P, 3 * C * B * D], F16)
        GH, GL = sb("GH", [P, M1 * NT], F16), sb("GL", [P, M1 * NT], F16)
        XP = sb("XP", [P, TB * GC * 2 * B], F16)
        TMP = XP[:, :].bitcast(F32)
        QH, QL = sb("QH", [P, C * NT], F16), sb("QL", [P, C * NT], F16)
        ZH, ZL = sb("ZH", [P, C * NT], F16), sb("ZL", [P, C * NT], F16)
        KH, KL = sb("KH", [P, 4 * 4 * P], F16), sb("KL", [P, 4 * 4 * P], F16)
        RES = sb("RES", [P, B * D])
        HT = sb("HT", [P, C * NT])
        UT = sb("UT", [P, B * D])
        YF = sb("YF", [P, C * NT])
        TT = [sb(f"TT{i}", [P, NT]) for i in range(2)]
        HB = [sb(f"HB{i}", [P, 512]) for i in range(2)]
        JUNK = GH[:, :].bitcast(F32)
        COL = sb("COL", [P, NCOLS])
        ROW = sb("ROW", [P, NROWS])
        RB = sb("RB", [16, 1536])
        GTT = sb("GTT", [16, 2 * NT])
        CENT = sb("CENT", [P, C * E])
        IDF, IDH = sb("IDF", [P, P]), sb("IDH", [P, P], F16)
        IOTA = sb("IOTA", [P, T])
        EQT, EQB = GL[:, 0:4 * T], sb("EQB", [P, 4 * B], F16)
        INSET = sb("INSET", [P, NBLK * B])
        IN = sb("IN", [P, B])
        IDXI = sb("IDXI", [P, 8], I32)
        IDXF, IDXG = sb("IDXF", [P, 8]), sb("IDXG", [P, 8])
        LB0 = sb("LB0", [P, GC])
        HBT = sb("HBT", [P, C * B])
        L = sb("L", [P, B * 9])
        SC = sb("SC", [P, B * 9])
        SB_ = sb("SB_", [P, B * E])
        MX = sb("MX", [P, B * 8])
        IX = sb("IX", [P, B * 8], U32)
        IXF = sb("IXF", [P, B * 8])
        GA = sb("GA", [P, B * 8])
        GT = sb("GT", [P, B * NE1])
        GT2 = sb("GT2", [P, B * NE1])
        GE = sb("GE", [P, NE1 * B])
        GCUR = [sb(f"GCUR{i}", [P, B]) for i in range(2)]
        SM = sb("SM", [P, 64])
        ST = sb("ST", [P, 64])
        PW = sb("PW", [P, 8])
        NTM = sb("NTM", [P, 2 * B * P])
        LNX = sb("LNX", [B, D])
        HID = sb("HID", [P, 2 * C * B])
        FV = sb("FV", [P, B * R])
        FT = GH[0:R, :].bitcast(F32)
        HC = sb("HC", [P, 2 * C * B])
        PRE = sb("PRE", [P, GC * B])
        TG = sb("TG", [P, (GC + C) * B])
        WK = sb("WK", [P, 2 * C * B])
        DC = sb("DC", [P, C * B])
        TC = sb("TC", [P, C * B])
        HF = [sb(f"HF{i}", [P, C * B]) for i in range(2)]
        H16 = [sb(f"H16{i}", [P, C * 2 * B], F16) for i in range(2)]

        DP = [ctx.enter_context(nc.psum_tensor(f"DP{i}", [P, 512], F32)) for i in range(DB)]
        AP_ = [ctx.enter_context(nc.psum_tensor(f"AP{i}", [P, 512], F32)) for i in range(AB)]
        GP = [ctx.enter_context(nc.psum_tensor(f"GP{i}", [P, 512], F32)) for i in range(2)]

        s_const = sem("s_const")
        s_tmpw = sem("s_tmpw")
        s_idx = sem("s_idx")
        s_gen = sem("s_gen")
        raw_in = [sem(f"raw_in{i}") for i in range(2)]
        raw_free = sem("raw_free")
        w_hi = sem("w_hi")
        pg_ready = sem("pg_ready")
        ew_lo = sem("ew_lo")
        res_lo = sem("res_lo")
        ew_free = sem("ew_free")
        f_fill, f_evac, ft_fill, ft_evac = sem("f_fill"), sem("f_evac"), sem("ft_fill"), sem("ft_evac")
        dw_fill, dw_sum, dw_hi, dw_lo = sem("dw_fill"), sem("dw_sum"), sem("dw_hi"), sem("dw_lo")
        s_ln, s_lnp, s_lnT, s_ae, s_hc, s_h = (sem(n) for n in ("s_ln", "s_lnp", "s_lnT", "s_ae", "s_hc", "s_h"))
        s_eq, s_in, s_misc, s_hbt, s_h0, s_base = (sem(n) for n in ("s_eq", "s_in", "s_misc", "s_hbt", "s_h0", "s_base"))
        d_fill, d_free = sem("d_fill"), sem("d_free")
        a_fill, a_free = sem("a_fill"), sem("a_free")
        dh, ah, al = sem("dh"), sem("ah"), sem("al")
        x_in = sem("x_in")
        s_mark = sem("s_mark")
        blk_done = sem("blk_done")
        st_out = sem("st_out")
        g_diff, g_tanh = sem("g_diff"), sem("g_tanh")
        g_mat, gt_copy = sem("g_mat"), sem("gt_copy")
        r_row = sem("r_row")
        h_row, k_used = sem("h_row"), sem("k_used")
        p_in, p_out = sem("p_in"), sem("p_out")
        sq = sem("sq")
        xn_row = sem("xn_row")
        x3f = sem("x3f")
        yf, yh, yl = sem("yf"), sem("yh"), sem("yl")
        hs_row, hs_tanh, n_row = sem("hs_row"), sem("hs_tanh"), sem("n_row")
        l_in, l_pe, l_pre, l_tg, l_w, l_d, l_c, l_tc, l_hi, l_h, l_lo, l_copy = (
            sem(n) for n in ("l_in", "l_pe", "l_pre", "l_tg", "l_w", "l_d", "l_c", "l_tc", "l_hi", "l_h", "l_lo", "l_copy"))

        V, A_, PE, G = nc.vector, nc.scalar, nc.tensor, nc.gpsimd
        block = ctx.enter_context(nc.Block())

        def col(name, n=1, i=0):
            return COL[:, CO[name] + i:CO[name] + i + n]

        def row(name, n):
            return ROW[:, RO[name]:RO[name] + n]

        def tmp(name, n, i=0):
            return TMP[:, TO[name] + i:TO[name] + i + n]

        def res(name, at, n):
            o = OFF[name] + at
            return WH[:, o:o + n], WL[:, o:o + n]

        def pair(hi, lo, at, n):
            return hi[:, at:at + n], lo[:, at:at + n]

        def dwp(which, b, c, at, n):
            o = ((which * B + b) * C + c) * D + at
            return DWH[:, o:o + n], DWL[:, o:o + n]

        def dbank(stage, i):
            return DP[dpos(stage, i) % DB]

        def abank(stage, i):
            return AP_[(AI[stage] + i) % AB]

        RBO = {"bu": 0, "b2": 256, "eb": 512, "eb12": 768, "b3": 1280}

        @block.sync
        def _(sp):
            for dst, src in ((COL[:, :], a["cols"]), (ROW[:, :], a["rows"]), (RB[:, :], a["rb"]), (PARS[:, :], a["par"]),
                             (CENT[:, :], a["tmpw"][:, TO["cent"]:TO["cent"] + C * E])):
                sp.dma_start(dst, src).then_inc(s_const, 16)
            sp.dma_start(LNX[:, :], a["cond"]).then_inc(s_const, 16)
            sp.dma_start(TMP[:, 0:NTMP], a["tmpw"]).then_inc(s_tmpw, 16)
            sp.dma_start(IDXI[:, :], a["idx"]).then_inc(s_idx, 16)

            def load(n, slot, src, width):
                sp.wait_ge(raw_free, n + 1)
                sp.dma_start(RAW[slot][:, 0:width], src).then_inc(raw_in[slot], 16)

            n = 0
            for f in range(F_UNITS):
                load(n, n % 2, a["factors"][f], RU)
                n += 1
            for at, w, _ in RES_UNITS:
                load(n, n % 2, a["resident"][:, at:at + w], w)
                n += 1
            for u in range(UPS):
                load(n, n % 2, a["stream"][0, :, u * RU:(u + 1) * RU], RU)
                n += 1
            with sp.Fori(0, NBLK) as k:
                with sp.Fori(0, NEW // 2) as p:
                    for j in range(2):
                        e = 2 * p + j
                        for u in range(UPS):
                            load(k * (NEW * UPS) + e * UPS + u + SETUP_UNITS, u % 2,
                                 a["stream"][bass.ds(e + 1, 1), :, u * RU:(u + 1) * RU].squeeze(0), RU)
            for i in range(2):
                sp.wait_ge(raw_in[i], 16 * (SETUP_UNITS // 2 + NBLK * NEW * UPS // 2))
            sp.wait_ge(st_out, 16 * NBLK * B)

        @block.gpsimd
        def _(g):
            g.sem_inc(l_copy, 2)
            G.memset(IDF[:, :], 0.0).then_inc(s_gen, 1)
            G.memset(IDH[:, :], 0.0).then_inc(s_gen, 1)
            G.memset(PW[:, :], -0.5).then_inc(s_gen, 1)
            G.iota(IOTA[:, :], [[1, T]], base=0, channel_multiplier=0,
                   allow_small_or_imprecise_dtypes=True).then_inc(s_gen, 1)
            g.wait_ge(s_gen, 4)
            G.affine_select(out=IDF[:, :], in_=IDF[:, :], compare_op=ALU.not_equal, fill=1.0, base=0,
                            pattern=[[-1, P]], channel_multiplier=1).then_inc(s_gen, 1)
            G.affine_select(out=IDH[:, :], in_=IDH[:, :], compare_op=ALU.not_equal, fill=1.0, base=0,
                            pattern=[[-1, P]], channel_multiplier=1).then_inc(s_gen, 1)
            g.wait_ge(s_ln, 1)
            G.tensor_tensor(SM[0:B, 2:3], SM[0:B, 1:2], PW[0:B, 0:1], ALU.pow).then_inc(s_lnp, 1)
            with g.Fori(0, NBLK) as k:
                g.wait_ge(blk_done, k + 1)
                g.dma_start(RES[:, :].rearrange("p (b c) -> p b c", b=B),
                            a["x"][:, bass.ds(k * TB, TB), :].rearrange("b p c -> p b c")).then_inc(x_in, 16)
                with g.Fori(0, TB // 2) as i:
                    for j in range(2):
                        s = i * 2 + j
                        g.wait_ge(l_h, k * TB + s + 1)
                        G.tensor_copy(HT[:, :].rearrange("p (q s) -> p q s", s=TB)[:, :, bass.ds(s, 1)],
                                      HF[j][:, :].rearrange("p (q o) -> p q o", o=1)).then_inc(l_copy, 1)
                g.wait_ge(p_in, k * 5 + 1)
                G.tensor_tensor(SM[:, 8:12], SM[:, 4:8], PW[:, 0:4], ALU.pow).then_inc(p_out, 1)
                for j in range(B):
                    g.wait_ge(p_in, k * 5 + 2 + j)
                    G.tensor_tensor(SM[:, 24 + 2 * j:26 + 2 * j], SM[:, 16 + 2 * j:18 + 2 * j], PW[:, 0:2],
                                    ALU.pow).then_inc(p_out, 1)
                for j in range(B):
                    g.wait_ge(r_row, k * (4 * B) + 3 * B + j + 1)
                    g.sem_inc(s_mark, 1)
                    g.dma_start(out[j, bass.ds(k * TB, TB), :], RES[:, j * D:(j + 1) * D]).then_inc(st_out, 16)
                g.wait_ge(st_out, k * (16 * B) + 16 * B)
                g.sem_inc(s_mark, 1)

        @block.scalar
        def _(act):
            act.wait_ge(s_const, 16 * 6)
            act.wait_ge(s_lnT, 1)
            for c in range(C):
                A_.activation(HC[:, c * B:(c + 1) * B], DP[0][:, c * B:(c + 1) * B], ACT.Identity,
                              scale=col("g0", 1, c), bias=col("be0", 1, c)).then_inc(s_ae, 1)
                A_.activation(HC[:, (C + c) * B:(C + c + 1) * B], DP[0][:, c * B:(c + 1) * B], ACT.Identity,
                              scale=col("g3", 1, c), bias=col("be3", 1, c)).then_inc(s_ae, 1)
            act.wait_ge(s_hc, 1)
            for w in range(2):
                for m in range(C):
                    A_.activation(HID[:, (w * C + m) * B:(w * C + m + 1) * B],
                                  DP[1][:, (w * C + m) * B:(w * C + m + 1) * B], ACT.Gelu,
                                  bias=col("b1_3" if w else "b1_0", 1, m)).then_inc(s_h, 1)
            for t in range(12):
                act.wait_ge(dw_sum, t + 1)
                A_.activation(DWH[:, t * 2 * D:(t + 1) * 2 * D], TT[t % 2][:, :], ACT.Copy, scale=S).then_inc(dw_hi, 1)

            for i, (at, w, sc) in enumerate(RES_UNITS):
                n = F_UNITS + i
                act.wait_ge(raw_in[n % 2], 16 * (n // 2 + 1))
                A_.activation(WH[:, at:at + w], RAW[n % 2][:, 0:w], ACT.Copy, scale=sc).then_inc(w_hi, 1)

            def stream_unit(par, u, count_in, scale):
                act.wait_ge(raw_in[u % 2], count_in)
                if scale is None:
                    A_.activation(EH[par][:, u * RU:(u + 1) * RU], RAW[u % 2][:, :], ACT.Identity,
                                  scale=PG[par][:, u:u + 1]).then_inc(w_hi, 1)
                else:
                    A_.activation(EH[par][:, u * RU:(u + 1) * RU], RAW[u % 2][:, :], ACT.Copy,
                                  scale=scale).then_inc(w_hi, 1)

            def stream_set(q, par, expert):
                act.wait_ge(ew_free, q + 1)
                if expert:
                    act.wait_ge(pg_ready, q + 1)
                for u in range(UPS):
                    stream_unit(par, u, (q * (UPS // 2) + (SETUP_UNITS - UPS) // 2 + u // 2 + 1) * 16,
                                None if expert and u < C else S)

            stream_set(0, 0, True)

            def d_hi(k, stage, i, dst, scale=1.0):
                act.wait_ge(d_fill, k * ND + dpos(stage, i) + 1)
                A_.activation(dst, dbank(stage, i)[:, :], ACT.Copy, scale=scale).then_inc(dh, 1)

            def a_split(k, idx, par, evac, hi_dst):
                act.wait_ge(a_fill, k * NA + idx + 1)
                act.wait_ge(al, k * NA + idx + 1)
                evac(TT[par])
                act.wait_ge(a_free, k * NA + idx + 1 + AB)
                return A_.activation(hi_dst, TT[par][:, :], ACT.Copy).then_inc(ah, 1)

            with act.Fori(0, NBLK) as k:
                for c in range(C):
                    d_hi(k, "xT", c, QH[:, c * NT:(c + 1) * NT])
                for m in range(C):
                    d_hi(k, "y0T", m, ZH[:, m * NT:(m + 1) * NT], IS)
                act.wait_ge(g_diff, k * 5 + 1)
                A_.activation(SM[:, 36:40], SM[:, 32:36], ACT.Tanh, scale=0.5).then_inc(g_tanh, 1)
                for j in range(B):
                    d_hi(k, "h0T", j, KH[:, j * 512:(j + 1) * 512])
                for c in range(C):
                    d_hi(k, "x1T", c, QH[:, c * NT:(c + 1) * NT])
                for m in range(GC):
                    f = 2.0 if m >= 6 else 1.0

                    def evac(t, m=m, f=f):
                        A_.activation(t[:, :], abank("xp", m)[:, :], ACT.Identity, scale=f,
                                      bias=LB0[:, m:m + 1]).then_inc(a_free, 1)
                    dst = XP[:, :].rearrange("p (s q b) -> p b s q", q=2 * GC, b=B)[:, :, :, 2 * m]
                    act.wait_ge(a_fill, k * NA + AI["xp"] + m + 1)
                    act.wait_ge(al, k * NA + AI["xp"] + m + 1)
                    evac(TT[m % 2])
                    act.wait_ge(a_free, k * NA + AI["xp"] + m + 1 + AB)
                    A_.activation(dst, TT[m % 2][:, :].rearrange("p (b s) -> p b s", b=B), ACT.Copy).then_inc(ah, 1)

                with act.Fori(0, TB // 2) as i:
                    for j in range(2):
                        n = k * TB + i * 2 + j + 1
                        act.wait_ge(l_pre, n)
                        A_.activation(TG[:, 0:GC * B], PRE[:, :], ACT.Tanh, scale=1.0 / 128).then_inc(l_tg, 1)
                        act.wait_ge(l_d, n)
                        A_.activation(TC[:, :], DC[:, :], ACT.Tanh, scale=0.5).then_inc(l_tc, 1)

                act.wait_ge(g_diff, k * 5 + 2)
                A_.activation(SC[:, 0:B * E], L[:, 0:B * E], ACT.Tanh, scale=0.5).then_inc(g_tanh, 1)
                for j in range(B):
                    act.wait_ge(d_fill, k * ND + DI["uT"] + j + 1)
                    A_.activation(JUNK[:, j * D:(j + 1) * D], dbank("uT", j)[:, 0:D], ACT.Square, scale=0.5,
                                  accum_out=SM[:, j:j + 1]).then_inc(sq, 1)
                for c in range(C):
                    d_hi(k, "xnT", c, QH[:, c * NT:(c + 1) * NT])

                with act.Fori(0, NE1 // 2) as p:
                    for j in range(2):
                        e = 2 * p + j
                        q = k * NEW + e + 1
                        act.wait_ge(ew_free, q + 1)
                        act.wait_ge(pg_ready, q + 1)
                        for u in range(UPS):
                            stream_unit((j + 1) % 2, u, (q * (UPS // 2) + ((SETUP_UNITS - UPS) // 2 + u // 2 + 1)) * 16,
                                        None if u < C else S)
                        for m in range(M1):
                            def evac(t, m=m, j=j):
                                A_.activation(t[:, :], abank("up", m)[:, :], ACT.Gelu, scale=IS,
                                              bias=PARB[j][:, C + m:C + m + 1]).then_inc(a_free, 1)
                            a_split(k, e * M1 + (AI["up"] + m), m % 2, evac, GH[:, m * NT:(m + 1) * NT])

                def skip_set(q, par):
                    act.wait_ge(ew_free, q + 1)
                    for u in range(UPS):
                        stream_unit(par, u, (q * (UPS // 2) + ((SETUP_UNITS - UPS) // 2 + u // 2 + 1)) * 16, S)

                skip_set(k * NEW + NE1 + 1, 1)
                for c in range(C):
                    d_hi(k, "x2T", c, QH[:, c * NT:(c + 1) * NT])
                for m in range(C):
                    def evac(t, m=m):
                        for b in range(B):
                            ins = A_.activation(t[:, b * TB:(b + 1) * TB], abank("z2", m)[:, b * TB:(b + 1) * TB],
                                                ACT.Tanh, scale=IS, bias=HBT[:, m * B + b:m * B + b + 1])
                        ins.then_inc(a_free, 1)
                    a_split(k, AI["z2"] + m, m % 2, evac, ZH[:, m * NT:(m + 1) * NT])
                act.wait_ge(g_diff, k * 5 + 3)
                A_.activation(SM[:, 36:40], SM[:, 32:36], ACT.Tanh, scale=0.5).then_inc(g_tanh, 1)

                q = (k + 1) * NEW
                act.wait_ge(ew_free, q + 1)
                act.wait_ge(pg_ready, q + 1)
                for u in range(UPS):
                    stream_unit(0, u, (q * (UPS // 2) + ((SETUP_UNITS - UPS) // 2 + u // 2 + 1)) * 16,
                                None if u < C else S)
                for c in range(C):
                    act.wait_ge(d_fill, k * ND + DI["x3T"] + c + 1)
                    A_.activation(YF[:, c * NT:(c + 1) * NT], dbank("x3T", c)[:, :], ACT.Copy).then_inc(x3f, 1)
                    d_hi(k, "x3T", c, QH[:, c * NT:(c + 1) * NT])
                for m in range(C):
                    def evac(t, m=m):
                        A_.activation(t[:, :], abank("mid", m)[:, :], ACT.Gelu, scale=IS).then_inc(a_free, 1)
                    a_split(k, AI["mid"] + m, m % 2, evac, ZH[:, m * NT:(m + 1) * NT])
                for m in range(C):
                    act.wait_ge(yf, k * C + m + 1)
                    A_.activation(QH[:, m * NT:(m + 1) * NT], YF[:, m * NT:(m + 1) * NT], ACT.Copy).then_inc(yh, 1)
                act.wait_ge(g_diff, k * 5 + 4)
                A_.activation(SC[:, :], L[:, :], ACT.Tanh, scale=0.5).then_inc(g_tanh, 1)
                act.wait_ge(g_diff, k * 5 + 5)
                A_.activation(SM[:, 36:40], SM[:, 32:36], ACT.Tanh, scale=0.5).then_inc(g_tanh, 1)
                for j in range(B):
                    act.wait_ge(hs_row, k * B + j + 1)
                    hv = HB[j % 2][:, :].rearrange("p (v w h) -> p v w h", v=2, w=2)
                    A_.activation(TT[0][:, (j % 2) * 256:(j % 2) * 256 + 256].rearrange("p (v h) -> p v h", v=2),
                                  hv[:, :, 0, :], ACT.Tanh, scale=0.5).then_inc(hs_tanh, 1)
                for v in range(2):
                    def evac(t, v=v):
                        A_.activation(t[:, :], abank("nT", v)[:, :], ACT.Identity,
                                      scale=col("s_g" if v else "sel_g"), bias=col("s_b" if v else "sel_b")).then_inc(a_free, 1)
                    a_split(k, AI["nT"] + v, v % 2, evac, ZH[:, v * NT:(v + 1) * NT])

        @block.vector
        def _(dve):
            def done(sem_, n=1):
                V.drain().then_inc(sem_, n)

            done(raw_free, 2)
            done(l_c)
            done(d_free, DB)
            done(al, 2)
            done(blk_done, 1)
            dve.wait_ge(s_const, 16 * 6)
            V.bn_stats(ST[0:B, 0:6], LNX[:, :])
            V.drain()
            V.bn_aggr(SM[0:B, 0:2], ST[0:B, 0:6])
            V.drain()
            V.tensor_scalar(SM[0:B, 1:2], SM[0:B, 1:2], LN_EPS, None, ALU.add).then_inc(s_ln, 1)
            V.tensor_scalar(LB0[:, 0:6], col("lstm_b", 6), S, None, ALU.mult)
            V.tensor_scalar(LB0[:, 6:8], col("lstm_b", 2, 6), 2 * S, None, ALU.mult)
            V.memset(TG[:, GC * B:(GC + C) * B], 0.0)
            V.tensor_scalar(HF[1][:, :], col("condT", C * B), 2.0, None, ALU.mult)
            V.drain()
            h0v = H16[0][:, :].rearrange("p (c v b) -> p c v b", c=C, v=2)
            hfv = [HF[i][:, :].rearrange("p (c b) -> p c b", c=C) for i in range(2)]
            V.tensor_copy(h0v[:, :, 0, :], hfv[1])
            V.drain()
            V.tensor_tensor(h0v[:, :, 1, :], hfv[1], h0v[:, :, 0, :], ALU.subtract)
            done(l_hi)
            done(l_lo)
            dve.wait_ge(s_lnp, 1)
            V.tensor_scalar(LNX[:, :], LNX[:, :], SM[0:B, 0:1], SM[0:B, 2:3], ALU.subtract, ALU.mult)
            done(s_ln)
            dve.wait_ge(s_gen, 6)
            dve.wait_ge(s_idx, 16)
            V.tensor_copy(IDXF[:, :], IDXI[:, :])
            V.drain()
            V.tensor_scalar(IDXG[:, 0:4], IDXF[:, 0:4], 0.0, float(B), ALU.is_lt, ALU.mult)
            V.tensor_scalar(IDXG[:, 4:8], IDXF[:, 4:8], 0.0, float(T), ALU.is_lt, ALU.mult)
            V.drain()
            V.tensor_tensor(IDXF[:, :], IDXF[:, :], IDXG[:, :], ALU.add)
            V.drain()
            for i in range(4):
                V.tensor_scalar(EQB[:, i * B:(i + 1) * B], IOTA[:, 0:B], IDXF[:, i:i + 1], None, ALU.is_equal)
                V.tensor_scalar(EQT[:, i * T:(i + 1) * T], IOTA[:, :], IDXF[:, 4 + i:5 + i], None, ALU.is_equal)
            done(s_eq)
            dve.wait_ge(s_in, 1)
            V.tensor_scalar(INSET[:, :], DP[3][:, 0:NBLK * B], 1.0, None, ALU.min)
            dve.wait_ge(s_hbt, 1)
            for m in range(C):
                V.tensor_scalar(HBT[:, m * B:(m + 1) * B], DP[2][:, m * B:(m + 1) * B], col("bhh", 1, m),
                                col("bih", 1, m), ALU.add, ALU.add)
            dve.wait_ge(s_tmpw, 16)
            for c in range(C):
                o = TO["base0"] + c * D + c * P
                V.tensor_tensor(TMP[:, o:o + P], TMP[:, o:o + P], IDF[:, :], ALU.add)
            V.drain()
            for f in range(F_UNITS // 2):
                which, c = f // C, f % C
                for half in range(2):
                    n = 2 * f + half
                    dve.wait_ge(f_fill, n + 1)
                    for b in range(B):
                        o = (which * C + c) * R + half * 4
                        V.tensor_tensor(FV[:, b * R + half * 4:b * R + half * 4 + 4],
                                        DP[0][:, 0:16].rearrange("p (r b) -> p b r", b=B)[:, b, :],
                                        col("fb", 4, o), ALU.add)
                    V.drain().then_inc(raw_free, 1)
                    done(f_evac)
                dve.wait_ge(ft_fill, f + 1)
                ftv = FT[:, :].rearrange("r (w b d) -> r w b d", w=2, b=B)
                V.tensor_copy(ftv[:, which % 2, :, c * P:(c + 1) * P],
                              DP[1][0:R, :].rearrange("r (b d) -> r b d", b=B))
                done(ft_evac)
                if f % 4 == 3:
                    w3 = f // 4
                    base = ("base0", "base_down", "base_upT")[w3]
                    for b in range(B):
                        t = w3 * 4 + b
                        dve.wait_ge(dw_fill, t + 1)
                        if t >= 2:
                            dve.wait_ge(dw_hi, t - 1)
                        V.tensor_tensor(TT[t % 2][:, :], DP[2 + t % 2][:, :], tmp(base, C * D), ALU.add).then_inc(dw_sum, 1)
                        dve.wait_ge(dw_hi, t + 1)
                        V.scalar_tensor_tensor(DWL[:, t * 2 * D:(t + 1) * 2 * D], TT[t % 2][:, :], S,
                                               DWH[:, t * 2 * D:(t + 1) * 2 * D], ALU.mult, ALU.subtract).then_inc(dw_lo, 1)
                    V.drain()
            for i, (at, w, sc) in enumerate(RES_UNITS):
                n = F_UNITS + i
                dve.wait_ge(w_hi, i + 1)
                V.scalar_tensor_tensor(WL[:, at:at + w], RAW[n % 2][:, 0:w], sc, WH[:, at:at + w],
                                       ALU.mult, ALU.subtract).then_inc(raw_free, 1)
            done(res_lo)

            def gains(par, e):
                V.tensor_copy(PARB[par][:, :], PARS[:, e * (C + M1):(e + 1) * (C + M1)] if isinstance(e, int)
                              else PARS[:, bass.ds(e * (C + M1), C + M1)])
                V.drain()
                V.tensor_scalar(PG[par][:, :], PARB[par][:, 0:C], S, None, ALU.mult)
                done(pg_ready)

            def stream_lo(q, par, expert):
                for u in range(UPS):
                    dve.wait_ge(w_hi, q * UPS + (len(RES_UNITS) + u + 1))
                    V.scalar_tensor_tensor(EL[par][:, u * RU:(u + 1) * RU], RAW[u % 2][:, :],
                                           PG[par][:, u:u + 1] if expert and u < C else S,
                                           EH[par][:, u * RU:(u + 1) * RU], ALU.mult, ALU.subtract).then_inc(raw_free, 1)
                done(ew_lo)

            gains(0, 0)
            stream_lo(0, 0, True)

            def d_lo(k, stage, i, hi, dst, scale=1.0):
                dve.wait_ge(dh, k * NH + HI[stage] + i + 1)
                V.scalar_tensor_tensor(dst, dbank(stage, i)[:, :], scale, hi, ALU.mult, ALU.subtract).then_inc(d_free, 1)

            def a_lo(k, idx, par, hi, dst, src=None):
                dve.wait_ge(ah, k * NA + idx + 1)
                V.tensor_tensor(dst, TT[par][:, :] if src is None else src, hi, ALU.subtract).then_inc(al, 1)

            def filled(k, stage, i):
                dve.wait_ge(d_fill, k * ND + dpos(stage, i) + 1)

            def top2(src, n=E):
                for j in range(B):
                    V.max(MX[:, j * 8:(j + 1) * 8], src[:, j * n:j * n + E])
                V.drain()
                for j in range(B):
                    V.max_index(IX[:, j * 8:(j + 1) * 8], MX[:, j * 8:(j + 1) * 8], src[:, j * n:j * n + E])
                V.drain()
                V.tensor_copy(IXF[:, :], IX[:, :])
                mxv = MX[:, :].rearrange("p (j e) -> p j e", j=B)
                V.tensor_tensor(SM[:, 32:36], mxv[:, :, 0], mxv[:, :, 1], ALU.subtract)

            def softmax2(k, g_index, scale):
                dve.wait_ge(g_tanh, k * 5 + g_index)
                V.tensor_scalar(SM[:, 40:44], SM[:, 36:40], 0.5 * scale, 0.5 * scale, ALU.mult, ALU.add)
                V.tensor_scalar(SM[:, 44:48], SM[:, 36:40], -0.5 * scale, 0.5 * scale, ALU.mult, ALU.add)
                V.drain()
                for j in range(B):
                    V.tensor_scalar(GA[:, j * 8:(j + 1) * 8], IOTA[:, 0:E], IXF[:, j * 8:j * 8 + 1],
                                    SM[:, 40 + j:41 + j], ALU.is_equal, ALU.mult)
                    V.tensor_scalar(GT[:, j * 8:(j + 1) * 8], IOTA[:, 0:E], IXF[:, j * 8 + 1:j * 8 + 2],
                                    SM[:, 44 + j:45 + j], ALU.is_equal, ALU.mult)
                V.drain()
                V.tensor_tensor(GT[:, 0:B * E], GT[:, 0:B * E], GA[:, :], ALU.add)
                V.drain()

            with dve.Fori(0, NBLK) as k:
                for c in range(C):
                    d_lo(k, "xT", c, QH[:, c * NT:(c + 1) * NT], QL[:, c * NT:(c + 1) * NT])
                for m in range(C):
                    d_lo(k, "y0T", m, ZH[:, m * NT:(m + 1) * NT], ZL[:, m * NT:(m + 1) * NT], IS)
                filled(k, "log0", 0)
                V.tensor_scalar(L[:, 0:B * E], dbank("log0", 0)[:, 0:B * E], IS, None, ALU.mult).then_inc(d_free, 1)
                V.drain()
                top2(L)
                done(g_diff)
                softmax2(k, 1, 0.5)
                done(g_mat)
                filled(k, "g0T", 0)
                V.tensor_scalar(GTT[0:E, 0:NT], dbank("g0T", 0)[0:E, :], S, None, ALU.mult).then_inc(d_free, 1)
                done(gt_copy)
                for j in range(B):
                    filled(k, "h0", j)
                    hb = HB[j % 2]
                    if j >= 2:
                        filled(k, "h0T", j - 2)
                    V.scalar_tensor_tensor(hb[:, :], dbank("h0", j)[:, :], IS, row("bd", 512), ALU.mult, ALU.add).then_inc(d_free, 1)
                    V.drain()
                    V.scalar_tensor_tensor(hb[:, :].rearrange("p (e h) -> p e h", e=E),
                                           hb[:, :].rearrange("p (e h) -> p e h", e=E), 0.0,
                                           GT[:, j * E:(j + 1) * E].unsqueeze(2).to_broadcast([P, E, 64]),
                                           ALU.max, ALU.mult)
                    done(h_row)
                    if j >= 1:
                        d_lo(k, "h0T", j - 1, KH[:, (j - 1) * 512:j * 512], KL[:, (j - 1) * 512:j * 512])
                d_lo(k, "h0T", 3, KH[:, 3 * 512:4 * 512], KL[:, 3 * 512:4 * 512])
                for j in range(B):
                    filled(k, "out0", j)
                    r = RES[:, j * D:(j + 1) * D]
                    V.scalar_tensor_tensor(r, dbank("out0", j)[:, 0:D], IS, r, ALU.mult, ALU.add).then_inc(d_free, 1)
                    done(r_row)
                for c in range(C):
                    d_lo(k, "x1T", c, QH[:, c * NT:(c + 1) * NT], QL[:, c * NT:(c + 1) * NT])
                for m in range(GC):
                    xv = XP[:, :].rearrange("p (s q b) -> p b s q", q=2 * GC, b=B)
                    dve.wait_ge(ah, k * NA + AI["xp"] + m + 1)
                    V.tensor_tensor(xv[:, :, :, 2 * m + 1], TT[m % 2][:, :].rearrange("p (b s) -> p b s", b=B),
                                    xv[:, :, :, 2 * m], ALU.subtract).then_inc(al, 1)

                with dve.Fori(0, TB // 2) as i:
                    for j in range(2):
                        n = k * TB + i * 2 + j + 1
                        h16 = H16[(j + 1) % 2][:, :].rearrange("p (c v b) -> p c v b", c=C, v=2)
                        dve.wait_ge(l_pe, n)
                        V.tensor_reduce(PRE[:, :].rearrange("p (c b) -> p c b", c=GC),
                                        GP[j][:, 0:GC * 2 * B].rearrange("p (c v b) -> p c b v", v=2, b=B),
                                        AX.X, ALU.add).then_inc(l_pre, 1)
                        dve.wait_ge(l_tg, n)
                        V.scalar_tensor_tensor(WK[:, :], TG[:, 0:16], 1.0, TG[:, 24:40], ALU.add, ALU.mult).then_inc(l_w, 1)
                        dve.wait_ge(l_w, n)
                        V.tensor_tensor(DC[:, :], WK[:, 0:8], WK[:, 8:16], ALU.add).then_inc(l_d, 1)
                        dve.wait_ge(l_d, n)
                        V.tensor_scalar(TG[:, 32:40], DC[:, :], 0.5, None, ALU.mult).then_inc(l_c, 1)
                        dve.wait_ge(l_tc, n)
                        tov = TG[:, 16:24].rearrange("p (c b) -> p c b", c=C)
                        tcv = TC[:, :].rearrange("p (c b) -> p c b", c=C)
                        V.scalar_tensor_tensor(h16[:, :, 0, :], tov, 1.0, tcv, ALU.add, ALU.mult).then_inc(l_hi, 1)
                        dve.wait_ge(l_copy, n)
                        V.scalar_tensor_tensor(hfv[j], tov, 1.0, tcv, ALU.add, ALU.mult).then_inc(l_h, 1)
                        dve.wait_ge(l_hi, n + 1)
                        dve.wait_ge(l_h, n)
                        V.tensor_tensor(h16[:, :, 1, :], hfv[j], h16[:, :, 0, :], ALU.subtract).then_inc(l_lo, 1)

                for j in range(B):
                    filled(k, "log1", j)
                    V.tensor_scalar(L[:, j * E:(j + 1) * E], dbank("log1", j)[:, 0:E], 0.5, None, ALU.mult).then_inc(d_free, 1)
                done(g_diff)
                for j in range(B):
                    filled(k, "uT", j)
                    dve.wait_ge(sq, k * B + j + 1)
                    V.tensor_scalar(UT[:, j * D:(j + 1) * D], dbank("uT", j)[:, 0:D], 0.5, None, ALU.mult).then_inc(d_free, 1)
                V.tensor_scalar(SM[:, 4:8], SM[:, 0:4], 1.0 / D, RMS_EPS, ALU.mult, ALU.add)
                V.drain()
                V.tensor_tensor(RES[:, :], RES[:, :], UT[:, :], ALU.add)
                done(p_in)
                dve.wait_ge(g_tanh, k * 5 + 2)
                V.tensor_scalar(SC[:, 0:B * E], SC[:, 0:B * E], 0.5, 0.5, ALU.mult, ALU.add)
                V.drain()
                top2(SC)
                V.reduce_sum(SM[:, 48:52], SC[:, 0:B * E].rearrange("p (j e) -> p j e", j=B), AX.X)
                V.drain()
                V.reciprocal(SM[:, 52:56], SM[:, 48:52])
                V.memset(GT[:, :], 1.0)
                for j in range(B):
                    V.tensor_scalar(GA[:, j * 8:(j + 1) * 8], IOTA[:, 0:E], IXF[:, j * 8:j * 8 + 1], None, ALU.is_equal)
                V.drain()
                for j in range(B):
                    V.scalar_tensor_tensor(GA[:, j * 8:(j + 1) * 8], IOTA[:, 0:E], IXF[:, j * 8 + 1:j * 8 + 2],
                                           GA[:, j * 8:(j + 1) * 8], ALU.is_equal, ALU.add)
                V.drain()
                for j in range(B):
                    V.scalar_tensor_tensor(GT[:, j * NE1 + 2:(j + 1) * NE1], SC[:, j * E:(j + 1) * E], SM[:, 52 + j:53 + j],
                                           GA[:, j * 8:(j + 1) * 8], ALU.mult, ALU.mult)
                V.drain()
                V.tensor_scalar(GE[:, :].rearrange("p (e j) -> p j e", j=B), GT[:, :].rearrange("p (j e) -> p j e", j=B),
                                IS, None, ALU.mult)
                done(g_mat)
                dve.wait_ge(p_out, k * 5 + 1)
                for j in range(B):
                    V.tensor_scalar(UT[:, j * D:(j + 1) * D], UT[:, j * D:(j + 1) * D], SM[:, 8 + j:9 + j], None, ALU.mult)
                done(xn_row)
                for c in range(C):
                    d_lo(k, "xnT", c, QH[:, c * NT:(c + 1) * NT], QL[:, c * NT:(c + 1) * NT])
                for h in range(2):
                    filled(k, "g1T", h)
                    V.tensor_copy(GTT[0:NE1, h * 256:(h + 1) * 256], dbank("g1T", h)[0:NE1, 0:256]).then_inc(d_free, 1)
                done(gt_copy)
                for j in range(B):
                    filled(k, "bias1", j)
                    r = RES[:, j * D:(j + 1) * D]
                    V.tensor_tensor(r, dbank("bias1", j)[:, 0:D], r, ALU.add).then_inc(d_free, 1)
                with dve.Fori(0, NE1 // 2) as p:
                    for j2 in range(2):
                        e = 2 * p + j2
                        q = k * NEW + e + 1
                        par = (j2 + 1) % 2
                        V.tensor_copy(GCUR[j2][:, :], GE[:, bass.ds(e * B, B)])
                        gains(par, e + 1)
                        stream_lo(q, par, True)
                        for m in range(M1):
                            a_lo(k, e * M1 + (AI["up"] + m), m % 2, GH[:, m * NT:(m + 1) * NT], GL[:, m * NT:(m + 1) * NT])
                        for j in range(B):
                            dve.wait_ge(d_fill, k * ND + e * B + (DI["down"] + j + 1))
                            r = RES[:, j * D:(j + 1) * D]
                            V.scalar_tensor_tensor(r, dbank("down", j)[:, 0:D], GCUR[j2][:, j:j + 1], r,
                                                   ALU.mult, ALU.add).then_inc(d_free, 1)
                done(r_row, B)

                gains(1, NE1 + 1)
                stream_lo(k * NEW + NE1 + 1, 1, False)
                for c in range(C):
                    d_lo(k, "x2T", c, QH[:, c * NT:(c + 1) * NT], QL[:, c * NT:(c + 1) * NT])
                for m in range(C):
                    a_lo(k, AI["z2"] + m, m % 2, ZH[:, m * NT:(m + 1) * NT], ZL[:, m * NT:(m + 1) * NT])
                filled(k, "log2", 0)
                for j in range(B):
                    ins = V.scalar_tensor_tensor(L[:, j * E:(j + 1) * E], dbank("log2", 0)[:, j * E:(j + 1) * E], IS,
                                                 row("gate_b", E), ALU.mult, ALU.add)
                ins.then_inc(d_free, 1)
                V.drain()
                top2(L)
                done(g_diff)
                softmax2(k, 3, 1.0)
                V.tensor_scalar(GT2[:, 0:B * E], GT[:, 0:B * E], IS, None, ALU.mult)
                done(g_mat)
                for h in range(2):
                    filled(k, "g2T", h)
                    V.tensor_copy(GTT[0:E, h * 256:(h + 1) * 256], dbank("g2T", h)[0:E, 0:256]).then_inc(d_free, 1)
                done(gt_copy)
                for j in range(B):
                    filled(k, "bias2", j)
                    r = RES[:, j * D:(j + 1) * D]
                    V.tensor_tensor(r, dbank("bias2", j)[:, 0:D], r, ALU.add).then_inc(d_free, 1)
                for j in range(B):
                    for w in range(4):
                        V.drain()
                        filled(k, "exp2", j * 4 + w)
                        r = RES[:, j * D:(j + 1) * D]
                        for h in range(2):
                            if h:
                                V.drain()
                            e = 2 * w + h
                            ins = V.scalar_tensor_tensor(r, dbank("exp2", j * 4 + w)[:, h * D:(h + 1) * D],
                                                         GT2[:, j * E + e:j * E + e + 1], r, ALU.mult, ALU.add)
                        ins.then_inc(d_free, 1)
                done(r_row, B)

                gains(0, NEW)
                stream_lo((k + 1) * NEW, 0, True)
                for c in range(C):
                    d_lo(k, "x3T", c, QH[:, c * NT:(c + 1) * NT], QL[:, c * NT:(c + 1) * NT])
                for m in range(C):
                    a_lo(k, AI["mid"] + m, m % 2, ZH[:, m * NT:(m + 1) * NT], ZL[:, m * NT:(m + 1) * NT])
                dve.wait_ge(x3f, k * C + C)
                for m in range(C):
                    filled(k, "y3T", m)
                    y = YF[:, m * NT:(m + 1) * NT]
                    V.scalar_tensor_tensor(y, dbank("y3T", m)[:, :], IS, y, ALU.mult, ALU.add).then_inc(d_free, 1)
                    done(yf)
                    dve.wait_ge(yh, k * C + m + 1)
                    V.tensor_tensor(QL[:, m * NT:(m + 1) * NT], y, QH[:, m * NT:(m + 1) * NT], ALU.subtract).then_inc(yl, 1)
                filled(k, "log3", 0)
                for j in range(B):
                    ins = V.scalar_tensor_tensor(L[:, j * 9:(j + 1) * 9], dbank("log3", 0)[:, j * 9:(j + 1) * 9], IS,
                                                 row("egsg_b", 9), ALU.mult, ALU.add)
                ins.then_inc(d_free, 1)
                done(g_diff)
                dve.wait_ge(g_tanh, k * 5 + 4)
                V.tensor_scalar(SC[:, :], SC[:, :], 0.5, 0.5, ALU.mult, ALU.add)
                V.drain()
                for j in range(B):
                    V.tensor_tensor(SB_[:, j * E:(j + 1) * E], SC[:, j * 9:j * 9 + E], row("exp_bias", E), ALU.add)
                V.drain()
                top2(SB_)
                V.tensor_copy(IN[:, :], INSET[:, bass.ds(k * B, B)])
                V.drain()
                for j in range(B):
                    V.tensor_scalar(GA[:, j * 8:(j + 1) * 8], IOTA[:, 0:E], IXF[:, j * 8:j * 8 + 1], None, ALU.is_equal)
                V.drain()
                V.tensor_tensor(SB_[:, :].rearrange("p (j e) -> p j e", j=B), GA[:, :].rearrange("p (j e) -> p j e", j=B),
                                SC[:, :].rearrange("p (j e) -> p j e", j=B)[:, :, 0:E], ALU.mult)
                V.drain()
                V.reduce_sum(SM[:, 48:52], SB_[:, :].rearrange("p (j e) -> p j e", j=B), AX.X)
                V.drain()
                V.tensor_tensor(SM[:, 32:36], SC[:, :].rearrange("p (j e) -> p j e", j=B)[:, :, E], SM[:, 48:52], ALU.subtract)
                done(g_diff)
                dve.wait_ge(g_tanh, k * 5 + 5)
                V.tensor_scalar(SM[:, 40:44], SM[:, 36:40], 0.5, -0.5, ALU.mult, ALU.add)
                V.tensor_scalar(SM[:, 44:48], SM[:, 36:40], -0.5, 0.5, ALU.mult, ALU.add)
                V.memset(GT[:, :], 1.0)
                V.drain()
                V.tensor_tensor(SM[:, 40:44], SM[:, 40:44], IN[:, :], ALU.mult)
                V.tensor_tensor(SM[:, 44:48], SM[:, 44:48], IN[:, :], ALU.mult)
                V.drain()
                gt9 = GT[:, 0:B * 9].rearrange("p (j e) -> p j e", j=B)
                gt29 = GT2[:, 0:B * 9].rearrange("p (j e) -> p j e", j=B)
                V.tensor_copy(gt9[:, :, 0:E], GA[:, :].rearrange("p (j e) -> p j e", j=B))
                for j in range(B):
                    V.tensor_scalar(GT2[:, j * 9:j * 9 + E], GA[:, j * 8:(j + 1) * 8], SM[:, 44 + j:45 + j], None, ALU.mult)
                V.tensor_scalar(gt29[:, :, E], SM[:, 40:44], 1.0, None, ALU.add)
                V.drain()
                V.tensor_scalar(GE[:, 0:36], GT2[:, 0:36], IS, None, ALU.mult)
                V.tensor_scalar(GA[:, :], GA[:, :], IS, None, ALU.mult)
                done(g_mat)
                for h in range(2):
                    filled(k, "g3T", h)
                    V.tensor_copy(GTT[0:9, h * NT:(h + 1) * NT], dbank("g3T", h)[0:9, :]).then_inc(d_free, 1)
                done(gt_copy)
                for j in range(B):
                    hb = HB[j % 2]
                    filled(k, "hid3", 6 * j)
                    V.tensor_copy(hb[:, :], dbank("hid3", 6 * j)[:, :]).then_inc(d_free, 1)
                    for w in range(4):
                        V.drain()
                        filled(k, "hid3", 6 * j + 1 + w)
                        for h in range(2):
                            if h:
                                V.drain()
                            e = 2 * w + h
                            ins = V.scalar_tensor_tensor(hb[:, 0:256], dbank("hid3", 6 * j + 1 + w)[:, h * 256:(h + 1) * 256],
                                                         GA[:, j * E + e:j * E + e + 1], hb[:, 0:256], ALU.mult, ALU.add)
                        ins.then_inc(d_free, 1)
                    filled(k, "hid3", 6 * j + 5)
                    V.scalar_tensor_tensor(hb[:, 256:512], dbank("hid3", 6 * j + 5)[:, 0:256], IS, hb[:, 256:512],
                                           ALU.mult, ALU.add).then_inc(d_free, 1)
                    done(hs_row)
                    dve.wait_ge(hs_tanh, k * B + j + 1)
                    hv = hb[:, :].rearrange("p (v w h) -> p v w h", v=2, w=2)
                    tv = TT[0][:, (j % 2) * 256:(j % 2) * 256 + 256].rearrange("p (v h) -> p v h", v=2)
                    qv = TT[1][:, (j % 2) * 256:(j % 2) * 256 + 256].rearrange("p (v h) -> p v h", v=2)
                    V.scalar_tensor_tensor(qv, tv, 1.0, hv[:, :, 0, :], ALU.add, ALU.mult)
                    V.drain()
                    V.scalar_tensor_tensor(qv, qv, 0.5, hv[:, :, 1, :], ALU.mult, ALU.mult)
                    V.drain()
                    for v in range(2):
                        V.bn_stats(ST[:, 6 * v:6 * v + 6], qv[:, v, :])
                    V.drain()
                    for v in range(2):
                        V.bn_aggr(ST[:, 16 + 2 * v:18 + 2 * v], ST[:, 6 * v:6 * v + 6])
                    V.drain()
                    for v in range(2):
                        V.tensor_scalar(SM[:, 16 + 2 * j + v:17 + 2 * j + v], ST[:, 17 + 2 * v:18 + 2 * v], LN_EPS, None, ALU.add)
                    done(p_in)
                    dve.wait_ge(p_out, k * 5 + 2 + j)
                    for v in range(2):
                        V.tensor_scalar(NTM[:, (v * B + j) * P:(v * B + j + 1) * P], qv[:, v, :], ST[:, 16 + 2 * v:17 + 2 * v],
                                        SM[:, 24 + 2 * j + v:25 + 2 * j + v], ALU.subtract, ALU.mult)
                    V.drain()
                done(n_row)
                for v in range(2):
                    a_lo(k, AI["nT"] + v, v % 2, ZH[:, v * NT:(v + 1) * NT], ZL[:, v * NT:(v + 1) * NT])
                for j in range(B):
                    r = RES[:, j * D:(j + 1) * D]
                    filled(k, "out3", 6 * j)
                    V.tensor_tensor(r, dbank("out3", 6 * j)[:, 0:D], r, ALU.add).then_inc(d_free, 1)
                    for w in range(4):
                        V.drain()
                        filled(k, "out3", 6 * j + 1 + w)
                        for h in range(2):
                            if h:
                                V.drain()
                            e = 2 * w + h
                            ins = V.scalar_tensor_tensor(r, dbank("out3", 6 * j + 1 + w)[:, h * D:(h + 1) * D],
                                                         GE[:, j * 9 + e:j * 9 + e + 1], r, ALU.mult, ALU.add)
                        ins.then_inc(d_free, 1)
                    V.drain()
                    filled(k, "out3", 6 * j + 5)
                    V.scalar_tensor_tensor(r, dbank("out3", 6 * j + 5)[:, 0:D], GE[:, j * 9 + E:j * 9 + E + 1], r,
                                           ALU.mult, ALU.add).then_inc(d_free, 1)
                    done(r_row)
                done(blk_done)

        @block.tensor
        def _(pe):
            def products(dst, terms, start=True, stop=True):
                n = len(terms) * 3
                i = 0
                for (ah_, al_), (bh_, bl_) in terms:
                    for l_, r_ in ((al_, bh_), (ah_, bl_), (ah_, bh_)):
                        ins = PE.matmul(dst, l_, r_, start=start and i == 0, stop=stop and i == n - 1)
                        i += 1
                return ins

            pe.sem_inc(ew_free, 2)
            pe.sem_inc(a_free, AB)
            pe.wait_ge(s_gen, 6)
            pe.wait_ge(s_ln, 2)
            for c in range(C):
                ins = PE.transpose(DP[0][:, c * B:(c + 1) * B], LNX[:, c * P:(c + 1) * P], IDF[0:B, 0:B])
            ins.then_inc(s_lnT, 1)
            pe.wait_ge(s_tmpw, 16)
            pe.wait_ge(s_ae, 2 * C)
            for w in range(2):
                for m in range(C):
                    for c in range(C):
                        ins = PE.matmul(DP[1][:, (w * C + m) * B:(w * C + m + 1) * B],
                                        tmp("w1_3" if w else "w1_0", P, c * D + m * P),
                                        HC[:, (w * C + c) * B:(w * C + c + 1) * B], start=c == 0, stop=c == C - 1)
            ins.then_inc(s_hc, 1)
            pe.wait_ge(s_eq, 1)
            for k in range(NBLK):
                for i in range(4):
                    ins = PE.matmul(DP[3][:, k * B:(k + 1) * B], EQT[:, i * T + k * TB:i * T + (k + 1) * TB],
                                    EQB[:, i * B:(i + 1) * B], start=i == 0, stop=i == 3)
            ins.then_inc(s_in, 1)
            for m in range(C):
                for c in range(C):
                    ins = PE.matmul(DP[2][:, m * B:(m + 1) * B], tmp("WhhT", P, c * D + m * P), col("condT", B, c * B),
                                    start=c == 0, stop=c == C - 1)
            ins.then_inc(s_hbt, 1)
            pe.wait_ge(s_h, 2 * C)
            for f in range(F_UNITS // 2):
                which, c = f // C, f % C
                hid = 0 if which < 2 else C
                for half in range(2):
                    n = 2 * f + half
                    pe.wait_ge(raw_in[n % 2], 16 * (n // 2 + 1))
                    if n:
                        pe.wait_ge(f_evac, n)
                    rv = RAW[n % 2][:, :].rearrange("p (c r d) -> p c r d", c=C, r=4)
                    for r in range(4):
                        for kc in range(C):
                            ins = PE.matmul(DP[0][:, r * B:(r + 1) * B], rv[:, kc, r, :],
                                            HID[:, (hid + kc) * B:(hid + kc + 1) * B], start=kc == 0, stop=kc == C - 1)
                    ins.then_inc(f_fill, 1)
                pe.wait_ge(f_evac, 2 * f + 2)
                if f:
                    pe.wait_ge(ft_evac, f)
                for b in range(B):
                    ins = PE.transpose(DP[1][0:R, b * P:(b + 1) * P], FV[:, b * R:(b + 1) * R], IDF[:, :])
                ins.then_inc(ft_fill, 1)
                if f % 4 == 3:
                    w3 = f // 4
                    pe.wait_ge(ft_evac, f + 1)
                    ftv = FT[:, :].rearrange("r (w b d) -> r w b d", w=2, b=B)
                    for b in range(B):
                        t = w3 * 4 + b
                        if t >= 2:
                            pe.wait_ge(dw_sum, t - 1)
                        for cc in range(C):
                            ins = PE.matmul(DP[2 + t % 2][:, cc * D:(cc + 1) * D], ftv[:, 0, b, cc * P:(cc + 1) * P],
                                            ftv[:, 1, b, :], start=True, stop=True)
                        ins.then_inc(dw_fill, 1)
            pe.wait_ge(dw_lo, 12)
            pe.wait_ge(res_lo, 1)

            def d_wait(k, stage, i):
                pe.wait_ge(d_free, k * ND + dpos(stage, i) + 1)

            def a_wait(k, idx):
                pe.wait_ge(a_free, k * NA + idx + 1)

            def all_freed(k, stage, i):
                pe.wait_ge(d_free, k * ND + dpos(stage, i) + 1 + DB)

            def transposes(k, stage, c, src):
                d_wait(k, stage, c)
                for j in range(B):
                    ins = PE.transpose(dbank(stage, c)[:, j * P:(j + 1) * P], src[:, j * D + c * P:j * D + (c + 1) * P],
                                       IDF[:, :])
                ins.then_inc(d_fill, 1)

            def gate_transposes(k, stage, i, src, n, js, at=0):
                d_wait(k, stage, i)
                for j in js:
                    ins = PE.transpose(dbank(stage, i)[0:n, (j - js[0]) * P:(j - js[0] + 1) * P], src[:, j * n:(j + 1) * n],
                                       IDF[:, :])
                ins.then_inc(d_fill, 1)

            with pe.Fori(0, NBLK) as k:
                pe.wait_ge(x_in, k * 16 + 16)
                for c in range(C):
                    transposes(k, "xT", c, RES)
                all_freed(k, "xT", C - 1)
                for m in range(C):
                    d_wait(k, "y0T", m)
                    for b in range(B):
                        ins = products(dbank("y0T", m)[:, b * TB:(b + 1) * TB],
                                       [(dwp(0, b, c, m * P, P), pair(QH, QL, c * NT + b * TB, TB)) for c in range(C)])
                    ins.then_inc(d_fill, 1)
                all_freed(k, "y0T", C - 1)
                d_wait(k, "log0", 0)
                for j in range(B):
                    ins = products(dbank("log0", 0)[:, j * E:(j + 1) * E],
                                   [(pair(ZH, ZL, c * NT + j * P, P), res("wgate", c * E, E)) for c in range(C)])
                ins.then_inc(d_fill, 1)
                pe.wait_ge(g_mat, k * 4 + 1)
                gate_transposes(k, "g0T", 0, GT, E, range(B))

                def h0T(j):
                    pe.wait_ge(h_row, k * B + j + 1)
                    d_wait(k, "h0T", j)
                    for m in range(4):
                        ins = PE.transpose(dbank("h0T", j)[:, m * P:(m + 1) * P], HB[j % 2][:, m * P:(m + 1) * P], IDF[:, :])
                    ins.then_inc(d_fill, 1)

                for j in range(B):
                    d_wait(k, "h0", j)
                    products(dbank("h0", j)[:, :],
                             [(pair(ZH, ZL, c * NT + j * P, P), res("Wd", c * 512, 512)) for c in range(C)]).then_inc(d_fill, 1)
                    if j >= 1:
                        h0T(j - 1)
                h0T(B - 1)
                pe.wait_ge(gt_copy, k * 4 + 1)
                for j in range(B):
                    d_wait(k, "out0", j)
                    all_freed(k, "h0T", j)
                    PE.matmul(dbank("out0", j)[:, 0:D], GTT[0:E, j * P:(j + 1) * P], RB[0:E, RBO["bu"]:RBO["bu"] + D],
                              start=True, stop=False)
                    products(dbank("out0", j)[:, 0:D],
                             [(pair(KH, KL, j * 512 + m * P, P), res("Wu", m * D, D)) for m in range(4)],
                             start=False).then_inc(d_fill, 1)
                pe.wait_ge(r_row, k * (4 * B) + B)
                for c in range(C):
                    transposes(k, "x1T", c, RES)
                all_freed(k, "x1T", C - 1)
                for m in range(GC):
                    a_wait(k, AI["xp"] + m)
                    products(abank("xp", m)[:, :],
                             [(res("Wx", c * GATES + m * P, P), pair(QH, QL, c * NT, NT)) for c in range(C)]).then_inc(a_fill, 1)

                pe.wait_ge(al, k * NA + AI["xp"] + GC + 2)
                pe.sem_inc(s_mark, 1)
                with pe.Fori(0, TB // 2) as i:
                    for j in range(2):
                        n = k * TB + i * 2 + j + 1
                        g, h = GP[j], H16[j]
                        PE.matmul(g[:, 0:64], IDH[:, :], XP[:, bass.ds(i * 128 + j * 64, 64)], start=True, stop=False)

                        def wh(hi, c, m):
                            w = WH if hi else WL
                            o = OFF["Wh_ifo"] + c * 768 + m * P if m < 6 else OFF["Wh_g"] + c * 256 + (m - 6) * P
                            return w[:, o:o + P]
                        pe.wait_ge(l_hi, n)
                        for m in range(GC):
                            for c in range(C):
                                PE.matmul(g[:, m * 8:m * 8 + 4], wh(False, c, m), h[:, c * 8:c * 8 + 4], start=False, stop=False)
                        pe.wait_ge(l_lo, n)
                        for m in range(GC):
                            for c in range(C):
                                ins = PE.matmul(g[:, m * 8:m * 8 + 8], wh(True, c, m), h[:, c * 8:c * 8 + 8], start=False,
                                                stop=m == GC - 1 and c == C - 1)
                        ins.then_inc(l_pe, 1)

                pe.wait_ge(l_copy, k * TB + TB + 2)
                for j in range(B):
                    d_wait(k, "log1", j)
                    for c in range(C):
                        ins = PE.matmul(dbank("log1", j)[:, 0:E], HT[:, c * NT + j * P:c * NT + (j + 1) * P],
                                        CENT[:, c * E:(c + 1) * E], start=c == 0, stop=c == C - 1)
                    ins.then_inc(d_fill, 1)
                for j in range(B):
                    d_wait(k, "uT", j)
                    for c in range(C):
                        ins = PE.transpose(dbank("uT", j)[:, c * P:(c + 1) * P], HT[:, c * NT + j * P:c * NT + (j + 1) * P],
                                           IDF[:, :])
                    ins.then_inc(d_fill, 1)
                pe.wait_ge(xn_row, k + 1)
                for c in range(C):
                    transposes(k, "xnT", c, UT)
                for h in range(2):
                    gate_transposes(k, "g1T", h, GT, NE1, range(2 * h, 2 * h + 2))
                pe.wait_ge(gt_copy, k * 4 + 2)
                for j in range(B):
                    d_wait(k, "bias1", j)
                    PE.matmul(dbank("bias1", j)[:, 0:D], GTT[0:NE1, j * P:(j + 1) * P], RB[0:NE1, RBO["b2"]:RBO["b2"] + D],
                              start=True, stop=True).then_inc(d_fill, 1)
                with pe.Fori(0, NE1 // 2) as p:
                    for j2 in range(2):
                        e = 2 * p + j2
                        pe.wait_ge(ew_lo, k * NEW + e + 1)
                        for m in range(M1):
                            a_wait(k, e * M1 + (AI["up"] + m))
                            products(abank("up", m)[:, :],
                                     [(pair(EH[j2], EL[j2], c * H1 + m * P, P), pair(QH, QL, c * NT, NT)) for c in range(C)]
                                     ).then_inc(a_fill, 1)
                        pe.wait_ge(al, k * NA + e * M1 + (AI["up"] + M1 + 2))
                        for j in range(B):
                            pe.wait_ge(d_free, k * ND + e * B + (DI["down"] + j + 1))
                            ins = products(dbank("down", j)[:, 0:D],
                                           [(pair(GH, GL, m * NT + j * P, P), pair(EH[j2], EL[j2], 2 * RU + m * D, D))
                                            for m in range(M1)])
                            ins.then_inc(d_fill, 1)
                        PE.drain().then_inc(ew_free, 1)

                pe.wait_ge(r_row, k * (4 * B) + 2 * B)
                for c in range(C):
                    transposes(k, "x2T", c, RES)
                all_freed(k, "x2T", C - 1)
                for m in range(C):
                    a_wait(k, AI["z2"] + m)
                    products(abank("z2", m)[:, :],
                             [(res("Wih", c * D + m * P, P), pair(QH, QL, c * NT, NT)) for c in range(C)]).then_inc(a_fill, 1)
                pe.wait_ge(al, k * NA + AI["z2"] + 4)
                d_wait(k, "log2", 0)
                for j in range(B):
                    ins = products(dbank("log2", 0)[:, j * E:(j + 1) * E],
                                   [(pair(ZH, ZL, c * NT + j * P, P), res("gatew", c * E, E)) for c in range(C)])
                ins.then_inc(d_fill, 1)
                pe.wait_ge(g_mat, k * 4 + 3)
                for h in range(2):
                    gate_transposes(k, "g2T", h, GT, E, range(2 * h, 2 * h + 2))
                pe.wait_ge(gt_copy, k * 4 + 3)
                for j in range(B):
                    d_wait(k, "bias2", j)
                    PE.matmul(dbank("bias2", j)[:, 0:D], GTT[0:E, j * P:(j + 1) * P], RB[0:E, RBO["eb"]:RBO["eb"] + D],
                              start=True, stop=True).then_inc(d_fill, 1)
                pe.wait_ge(ew_lo, k * NEW + NE1 + 1)
                for j in range(B):
                    for w in range(4):
                        d_wait(k, "exp2", j * 4 + w)
                        products(dbank("exp2", j * 4 + w)[:, :],
                                 [(pair(ZH, ZL, c * NT + j * P, P), pair(EH[0], EL[0], c * 2048 + w * 512, 512))
                                  for c in range(C)]).then_inc(d_fill, 1)
                PE.drain().then_inc(ew_free, 1)

                pe.wait_ge(r_row, k * (4 * B) + 3 * B)
                for c in range(C):
                    transposes(k, "x3T", c, RES)
                all_freed(k, "x3T", C - 1)
                for m in range(C):
                    a_wait(k, AI["mid"] + m)
                    for b in range(B):
                        ins = products(abank("mid", m)[:, b * TB:(b + 1) * TB],
                                       [(dwp(1, b, c, m * P, P), pair(QH, QL, c * NT + b * TB, TB)) for c in range(C)])
                    ins.then_inc(a_fill, 1)
                pe.wait_ge(al, k * NA + AI["mid"] + 4)
                for m in range(C):
                    d_wait(k, "y3T", m)
                    for b in range(B):
                        ins = products(dbank("y3T", m)[:, b * TB:(b + 1) * TB],
                                       [(dwp(2, b, c, m * P, P), pair(ZH, ZL, c * NT + b * TB, TB)) for c in range(C)])
                    ins.then_inc(d_fill, 1)
                pe.wait_ge(yl, k * C + C)
                d_wait(k, "log3", 0)
                for j in range(B):
                    ins = products(dbank("log3", 0)[:, j * 9:(j + 1) * 9],
                                   [(pair(QH, QL, c * NT + j * P, P), res("egsg", c * 9, 9)) for c in range(C)])
                ins.then_inc(d_fill, 1)
                pe.wait_ge(g_mat, k * 4 + 4)
                gate_transposes(k, "g3T", 0, GT, 9, range(B))
                gate_transposes(k, "g3T", 1, GT2, 9, range(B))
                pe.wait_ge(gt_copy, k * 4 + 4)
                pe.wait_ge(ew_lo, k * NEW + NE1 + 2)
                for j in range(B):
                    d_wait(k, "hid3", 6 * j)
                    PE.matmul(dbank("hid3", 6 * j)[:, :], GTT[0:9, j * P:(j + 1) * P], RB[0:9, RBO["eb12"]:RBO["eb12"] + 512],
                              start=True, stop=True).then_inc(d_fill, 1)
                    for w in range(4):
                        d_wait(k, "hid3", 6 * j + 1 + w)
                        products(dbank("hid3", 6 * j + 1 + w)[:, :],
                                 [(pair(QH, QL, c * NT + j * P, P), pair(EH[1], EL[1], c * 2048 + w * 512, 512))
                                  for c in range(C)]).then_inc(d_fill, 1)
                    d_wait(k, "hid3", 6 * j + 5)
                    products(dbank("hid3", 6 * j + 5)[:, 0:256],
                             [(pair(QH, QL, c * NT + j * P, P), res("sw12", c * D, D)) for c in range(C)]).then_inc(d_fill, 1)
                PE.drain().then_inc(ew_free, 1)
                pe.wait_ge(n_row, k + 1)
                for v in range(2):
                    a_wait(k, AI["nT"] + v)
                    for j in range(B):
                        ins = PE.transpose(abank("nT", v)[:, j * P:(j + 1) * P], NTM[:, (v * B + j) * P:(v * B + j + 1) * P],
                                           IDF[:, :])
                    ins.then_inc(a_fill, 1)
                pe.wait_ge(al, k * NA + AI["nT"] + 4)
                for j in range(B):
                    d_wait(k, "out3", 6 * j)
                    PE.matmul(dbank("out3", 6 * j)[:, 0:D], GTT[0:9, NT + j * P:NT + (j + 1) * P],
                              RB[0:9, RBO["b3"]:RBO["b3"] + D], start=True, stop=True).then_inc(d_fill, 1)
                    for w in range(4):
                        d_wait(k, "out3", 6 * j + 1 + w)
                        products(dbank("out3", 6 * j + 1 + w)[:, :],
                                 [(pair(ZH, ZL, j * P, P), res("ew3", w * 512, 512))]).then_inc(d_fill, 1)
                    d_wait(k, "out3", 6 * j + 5)
                    products(dbank("out3", 6 * j + 5)[:, 0:D],
                             [(pair(ZH, ZL, NT + j * P, P), res("sw3", 0, D))]).then_inc(d_fill, 1)


def host_layout(i):
    import numpy as np
    g = {k: np.asarray(v) for k, v in i.items()}

    def chunked(w):
        k, n = w.shape
        return w.reshape(k // P, P, n).transpose(1, 0, 2).reshape(P, -1)

    def column(v):
        return v.reshape(-1, P).T

    def factor(w, b):
        w = w.reshape(C, P, C, P, 2, R // 2).transpose(2, 4, 1, 0, 5, 3)
        return w.reshape(C * 2, P, RU), b.reshape(C, P, R).transpose(1, 0, 2).reshape(P, C * R)

    n = D * R
    w0, b0 = g["L0_cond_w2"], g["L0_cond_b2"]
    w3, b3 = g["L3_cond_W2"], g["L3_cond_bias2"]
    facts = [factor(w0[:, s * n:(s + 1) * n], b0[s * n:(s + 1) * n]) for s in (0, 1)]
    facts += [factor(w3[:, s * n:(s + 1) * n], b3[s * n:(s + 1) * n]) for s in (2, 3, 1, 0)]

    wh = g["L1_cond_Wh"]
    ew3 = g["L3_ffn_ew3"].transpose(2, 0, 1).reshape(P, E * D)
    egsg = np.concatenate([g["L3_ffn_eg_w"], g["L3_ffn_sg_w"]], 0).T
    resident = {
        "Wh_ifo": chunked(wh[:, 0:768]), "Wh_g": chunked(wh[:, 768:1024]), "Wx": chunked(g["L1_cond_Wx"]), "ew3": ew3,
        "Wd": chunked(g["L0_ffn_Wd"].transpose(1, 0, 2).reshape(D, 512)),
        "Wu": chunked(g["L0_ffn_Wu"].reshape(512, D)), "Wih": chunked(g["L2_cond_W_ih"].T),
        "sw12": chunked(np.concatenate([g["L3_ffn_sw1"].T, g["L3_ffn_sw2"].T], 1)), "sw3": g["L3_ffn_sw3"].T,
        "wgate": chunked(g["L0_ffn_w_gate"]), "gatew": chunked(g["L2_ffn_gate_w"].T), "egsg": chunked(egsg),
    }
    w1 = np.concatenate([g["L1_ffn_W1_s"], g["L1_ffn_W1_r"]], 0)
    w2 = np.concatenate([g["L1_ffn_W2_s"], g["L1_ffn_W2_r"]], 0)
    sets = [np.concatenate([chunked(w1[e]), chunked(w2[e])], 1) for e in range(NE1)]
    sets.append(chunked(g["L2_ffn_expert_w"].transpose(1, 0, 2).reshape(D, E * D)))
    ew12 = np.concatenate([g["L3_ffn_ew1"].transpose(0, 2, 1), g["L3_ffn_ew2"].transpose(0, 2, 1)], 2)
    sets.append(chunked(ew12.transpose(1, 0, 2).reshape(D, E * D)))
    sets.append(sets[0])
    gains = [g["L1_ffn_g_shared"]] * 2 + [g["L1_ffn_g_routed"]] * 8
    b1 = np.concatenate([g["L1_ffn_b1_s"], g["L1_ffn_b1_r"]], 0)
    par = [np.concatenate([column(gains[e]), column(b1[e])], 1) for e in range(NE1)]
    par += [np.ones_like(par[0])] * 2 + [par[0]]
    cols = {"lstm_b": column(g["L1_cond_b"]), "g0": column(g["L0_cond_ln_g"]), "be0": column(g["L0_cond_ln_b"]),
            "b1_0": column(g["L0_cond_b1"]), "g3": column(g["L3_cond_ln_gamma"]), "be3": column(g["L3_cond_ln_beta"]),
            "b1_3": column(g["L3_cond_bias1"]), "bih": column(g["L2_cond_b_ih"]), "bhh": column(g["L2_cond_b_hh"]),
            "s_g": column(g["L3_ffn_s_ln_g"]), "s_b": column(g["L3_ffn_s_ln_b"]), "sel_g": column(g["L3_ffn_sel_ln_g"]),
            "sel_b": column(g["L3_ffn_sel_ln_b"]), "fb": np.concatenate([b for _, b in facts], 1),
            "condT": chunked(g["cond_1024"].T)}
    rows = {"bd": g["L0_ffn_bd"].reshape(-1), "gate_b": g["L2_ffn_gate_b"],
            "egsg_b": np.concatenate([g["L3_ffn_eg_b"], g["L3_ffn_sg_b"]]), "exp_bias": g["L3_ffn_exp_bias"]}
    tmpw = {"w1_0": chunked(g["L0_cond_w1"]), "w1_3": chunked(g["L3_cond_W1"]), "base0": chunked(g["L0_cond_base_layer"]),
            "base_down": chunked(g["L3_cond_base_down"]), "base_upT": chunked(g["L3_cond_base_up"].T),
            "WhhT": chunked(g["L2_cond_W_hh"].T), "cent": chunked(g["L1_ffn_centroids"])}
    rb = np.zeros((16, 1536), np.float32)
    rb[0:E, 0:256] = g["L0_ffn_bu"]
    rb[0:2, 256:512] = g["L1_ffn_b2_s"]
    rb[2:NE1, 256:512] = g["L1_ffn_b2_r"]
    rb[0:E, 512:768] = g["L2_ffn_expert_b"]
    rb[0:E, 768:896] = g["L3_ffn_eb1"]
    rb[0:E, 896:1024] = g["L3_ffn_eb2"]
    rb[E, 1024:1152] = g["L3_ffn_sb1"]
    rb[E, 1152:1280] = g["L3_ffn_sb2"]
    rb[0:E, 1280:1536] = g["L3_ffn_eb3"]
    rb[E, 1280:1536] = g["L3_ffn_sb3"]
    idx = np.concatenate([g["L3_ffn_index_b"].reshape(4, P).T, g["L3_ffn_index_t"].reshape(4, P).T], 1)
    made = {
        "x": g["x"], "cond": g["cond_1024"],
        "factors": np.concatenate([w for w, _ in facts], 0),
        "resident": np.concatenate([resident[name] for name, _ in RESIDENT], 1),
        "stream": np.stack(sets), "par": np.concatenate(par, 1),
        "cols": np.concatenate([cols[name] for name, w in COLS if w], 1),
        "rows": np.broadcast_to(np.concatenate([rows[name] for name, _ in ROWS])[None], (P, NROWS)),
        "tmpw": np.concatenate([tmpw[name] for name, _ in TMPW], 1),
        "rb": rb, "idx": idx,
    }
    return {k: np.ascontiguousarray(v) for k, v in made.items()}


def build(nc, arrays):
    a = {k: nc.dram_tensor(f"in_{k}", v.shape, mybir.dt.from_np(v.dtype), kind="ExternalInput").ap()
         for k, v in arrays.items()}
    out = nc.dram_tensor("out_0", (B, T, D), F32, kind="ExternalOutput").ap()
    adaln_lstm_moe(nc, a, out)


def kernel(**inputs):
    import concourse.bacc as bacc
    from concourse.bass_utils import run_bass_kernel_spmd

    nc = bacc.Bacc("TRN2", target_bir_lowering=False, num_devices=1)
    arrays = host_layout(inputs)
    build(nc, arrays)
    r = run_bass_kernel_spmd(nc, [{f"in_{k}": v for k, v in arrays.items()}], core_ids=[0])
    return r.results[0]["out_0"]
```

```python
from contextlib import ExitStack, contextmanager

import concourse.bass as bass
from concourse import mybir

F32 = mybir.dt.float32
F16 = mybir.dt.float16
I32 = mybir.dt.int32
U32 = mybir.dt.uint32
ALU = mybir.AluOpType
ACT = mybir.ActivationFunctionType
AX = mybir.AxisListType

P = 128
B = 4
T = 512
D = 256
C = D // P
TB = 128
NBLK = T // TB
NT = B * TB
E = 8
R = 8
H1 = 1024
M1 = H1 // P
NE1 = 10
NEW = NE1 + 2
HW = 2 * H1
RU = 1024
RS = 4
UPS = 4
GATES = 4 * D
GC = GATES // P
S = 64.0
IS = 1.0 / S
LN_EPS = 1e-5
RMS_EPS = 1.1920928955078125e-07

RESIDENT = [("Wh_ifo", C * 768), ("Wh_g", C * 256), ("Wx", C * GATES), ("ew3", E * D), ("Wd", C * 512),
            ("Wu", 4 * D), ("Wih", C * D), ("sw12", C * D), ("sw3", D), ("wgate", C * E), ("gatew", C * E),
            ("egsg", C * (E + 1))]
OFF = {}
_at = 0
for _n, _w in RESIDENT:
    OFF[_n] = _at
    _at += _w
RES_COLS = _at
RES_UNITS = [(a, min(RU, 1536 - a), S / 2) for a in range(0, 1536, RU)] + \
            [(a, min(RU, RES_COLS - a), S) for a in range(1536, RES_COLS, RU)]
NFACT = 6
F_UNITS = NFACT * C * 2
SETUP_UNITS = F_UNITS + len(RES_UNITS)

COLS = [("lstm_b", GC), ("g0", C), ("be0", C), ("b1_0", C), ("g3", C), ("be3", C), ("b1_3", C), ("bih", C), ("bhh", C),
        ("s_g", 1), ("s_b", 1), ("sel_g", 1), ("sel_b", 1), ("fb", NFACT * C * R), ("condT", C * B), ("idx_b", 0)]
ROWS = [("bd", 512), ("gate_b", E), ("egsg_b", E + 1), ("exp_bias", E)]
TMPW = [("w1_0", C * D), ("w1_3", C * D), ("base0", C * D), ("base_down", C * D), ("base_upT", C * D), ("WhhT", C * D),
        ("cent", C * E)]


def offsets(table):
    at, out = 0, {}
    for name, n in table:
        out[name] = at
        at += n
    return out, at


CO, NCOLS = offsets(COLS)
RO, NROWS = offsets(ROWS)
TO, NTMP = offsets(TMPW)


D_A = [("xT", 2), ("y0T", 2), ("log0", 1), ("g0T", 1), ("h0", 8), ("out0", 4), ("x1T", 2)]
D_C = [("log1", 4), ("uT", 4), ("xnT", 2), ("g1T", 2), ("bias1", 4), ("down", NE1 * 4), ("x2T", 2), ("log2", 1),
       ("g2T", 2), ("bias2", 4), ("exp2", 16), ("x3T", 2), ("y3T", 2), ("log3", 1), ("g3T", 2), ("hid3", 24),
       ("out3", 24)]
A_A, A_X = [("xp0", GC)], [("xp1", GC)]
A_C = [("up", NE1 * M1), ("z2", 2), ("mid", 2), ("nT", 2)]
H_A = [("xT", 2), ("y0T", 2), ("h0T", 4), ("x1T", 2)]
H_C = [("xnT", 2), ("x2T", 2), ("x3T", 2)]

H0_AT, H0T_AT = (0, 1, 3, 5), (2, 4, 6, 7)
PLACE = {}
SIZE = {}
for _name, _x, _c, _a in (("d", [], D_C, D_A), ("a", A_X, A_C, A_A), ("h", [], H_C, H_A)):
    SIZE[_name] = []
    for _part, _table in (("X", _x), ("C", _c), ("A", _a)):
        _off, _n = offsets(_table)
        SIZE[_name].append(_n)
        for _stage, _o in _off.items():
            PLACE[_name, _stage] = (_part, _o)
DB, AB = 4, 2
assert all(n % DB == 0 for n in SIZE["d"]) and all(n % AB == 0 for n in SIZE["a"])
SIZE.update(diff=(0, 4, 1), mat=(0, 3, 1), rrow=(0, 12, 4), hrow=(0, 0, 4), pow=(0, 5, 0), b1=(0, NE1, 0))


def base(name, k, part):
    x, c, a = SIZE[name]
    if isinstance(k, int) and k < 1:
        return 0 if k < 0 else a + (x if part == "A" else 0)
    off = {"X": 0, "C": x, "A": x + c}[part] + (2 * a + x) - (x + c + a)
    if isinstance(k, int) and k == NBLK:
        off -= a + x
    return k * (x + c + a) + off


def plus(k, name, part, n):
    if isinstance(k, int):
        return base(name, k, part) + n
    x, c, a = SIZE[name]
    return k * (x + c + a) + ({"X": 0, "C": x, "A": x + c}[part] + (2 * a + x) - (x + c + a) + n)


def place(stage, i):
    if stage == "h0":
        return "A", PLACE["d", "h0"][1] + H0_AT[i]
    if stage == "h0T":
        return "A", PLACE["d", "h0"][1] + H0T_AT[i]
    part, o = PLACE["d", stage]
    return part, o + i


def d_count(k, stage, i, n=0):
    part, o = place(stage, i)
    return plus(k, "d", part, o + 1 + n)


def a_count(k, stage, i, n=0):
    part, o = PLACE["a", stage]
    return plus(k, "a", part, o + i + 1 + n)


def h_count(k, stage, i):
    part, o = PLACE["h", stage]
    return plus(k, "h", part, o + i + 1)


class Slots:

    def __init__(self, eng, step, block, always=None):
        self.eng, self.step, self.block, self.always = eng, step, block, always
        self.dyn, self.s = 0, 0

    def __call__(self):
        if self.step is not None:
            self.step(self.block, self.dyn, self.s)
        if self.always is not None:
            self.always()
        self.s += 1

    @contextmanager
    def repeat(self, lo, hi, width):
        start = self.s
        with self.eng.Fori(lo, hi) as r:
            self.dyn, self.s = r * width, start - lo * width
            yield r
        self.dyn, self.s = 0, start + (hi - lo) * width

    def bare(self, n):
        if self.step is not None:
            if n > 1:
                with self.repeat(0, n // 2, 2):
                    self()
                    self()
            if n % 2:
                self()


BARE0 = TB - 3 - NEW * 2 * UPS - 11
C_SLOTS = 117
assert C_SLOTS + 11 == TB


def adaln_lstm_moe(nc, a, out, split):
    with ExitStack() as ctx:
        def sb(name, shape, dt=F32):
            return ctx.enter_context(nc.sbuf_tensor(name, shape, dt))

        def sem(name):
            return ctx.enter_context(nc.semaphore(name))

        WH, WL = sb("WH", [P, RES_COLS], F16), sb("WL", [P, RES_COLS], F16)
        EW = [[sb(f"EW{h}{i}", [P, 2 * HW], F16) for i in range(2)] for h in range(2)]
        GH = [sb(f"GH{i}", [P, M1 * NT], F16) for i in range(2)]
        GL = [sb(f"GL{i}", [P, M1 * NT], F16) for i in range(2)]
        RAW = [t[:, :].bitcast(F32)[:, h * RU:(h + 1) * RU] for t in (GH[0], GL[0]) for h in range(2)]
        STAGE = [t[:, h * 2 * RU:(h + 1) * 2 * RU] for t in (GH[1], GL[1]) for h in range(2)]
        KH, KL = GH[1][:, 0:4 * 4 * P], GH[1][:, 4 * 4 * P:8 * 4 * P]
        JUNK = GH[0][:, :].bitcast(F32)
        FT = GH[1][0:R, :].bitcast(F32)
        EQT, EQB = GL[1][:, 0:4 * T], sb("EQB", [P, 4 * B], F16)
        B1 = sb("B1", [P, NE1 * M1])
        B1CUR = [sb(f"B1CUR{i}", [P, M1]) for i in range(2)]
        GAIN = sb("GAIN", [P, NEW * UPS])
        PG = sb("PG", [P, UPS])
        DWH = sb("DWH", [P, 3 * C * B * D], F16)
        DWL = sb("DWL", [P, 3 * C * B * D], F16)
        XP = sb("XP", [P, TB * GC * 2 * B], F16)
        TMP = XP[:, :].bitcast(F32)
        QH, QL = sb("QH", [P, C * NT], F16), sb("QL", [P, C * NT], F16)
        ZH, ZL = sb("ZH", [P, C * NT], F16), sb("ZL", [P, C * NT], F16)
        RX = sb("RX", [P, B * D])
        RW = sb("RW", [P, B * D])
        RES = sb("RES", [P, B * D])
        HT = sb("HT", [P, C * NT])
        UT = sb("UT", [P, B * D])
        YF = sb("YF", [P, C * NT])
        TT = [sb(f"TT{i}", [P, NT]) for i in range(2)]
        HB = [sb(f"HB{i}", [P, 512]) for i in range(2)]
        COL = sb("COL", [P, NCOLS])
        ROW = sb("ROW", [P, NROWS])
        RB = sb("RB", [16, 1536])
        GTT = sb("GTT", [16, 2 * NT])
        CENT = sb("CENT", [P, C * E])
        IDF, IDH = sb("IDF", [P, P]), sb("IDH", [P, P], F16)
        IOTA = sb("IOTA", [P, T])
        INSET = sb("INSET", [P, NBLK * B])
        IN = sb("IN", [P, B])
        IDXI = sb("IDXI", [P, 8], I32)
        IDXF, IDXG = sb("IDXF", [P, 8]), sb("IDXG", [P, 8])
        LB0 = sb("LB0", [P, GC])
        HBT = sb("HBT", [P, C * B])
        L = sb("L", [P, B * 9])
        SC = sb("SC", [P, B * 9])
        SB_ = sb("SB_", [P, B * E])
        MX = sb("MX", [P, B * 8])
        IX = sb("IX", [P, B * 8], U32)
        IXF = sb("IXF", [P, B * 8])
        GA = sb("GA", [P, B * 8])
        GT = sb("GT", [P, B * NE1])
        GT2 = sb("GT2", [P, B * NE1])
        GE = sb("GE", [P, NE1 * B])
        GCUR = [sb(f"GCUR{i}", [P, B]) for i in range(2)]
        SM = sb("SM", [P, 64])
        ST = sb("ST", [P, 64])
        PW = sb("PW", [P, 8])
        NTM = sb("NTM", [P, 2 * B * P])
        LNX = sb("LNX", [B, D])
        HID = sb("HID", [P, 2 * C * B])
        FV = sb("FV", [P, B * R])
        HC = sb("HC", [P, 2 * C * B])
        PRE = sb("PRE", [P, GC * B])
        TG = sb("TG", [P, (GC + C) * B])
        WK = sb("WK", [P, 2 * C * B])
        DC = sb("DC", [P, C * B])
        TC = sb("TC", [P, C * B])
        HF = [sb(f"HF{i}", [P, C * B]) for i in range(2)]
        H16 = [sb(f"H16{i}", [P, C * 2 * B], F16) for i in range(2)]

        DP = [ctx.enter_context(nc.psum_tensor(f"DP{i}", [P, 512], F32)) for i in range(DB)]
        AP_ = [ctx.enter_context(nc.psum_tensor(f"AP{i}", [P, 512], F32)) for i in range(AB)]
        GP = [ctx.enter_context(nc.psum_tensor(f"GP{i}", [P, 512], F32)) for i in range(2)]

        s_const = sem("s_const")
        s_tmpw = sem("s_tmpw")
        s_idx = sem("s_idx")
        s_gen = sem("s_gen")
        raw_in = [sem(f"raw_in{i}") for i in range(RS)]
        raw_free = sem("raw_free")
        w_hi = sem("w_hi")
        e_hi = sem("e_hi")
        pg_ready = sem("pg_ready")
        split_out = [sem(f"split_out{i}") for i in range(RS)]
        w_in = [[sem(f"w_in{h}{i}") for i in range(2)] for h in range(2)]
        b1_ready = sem("b1_ready")
        res_lo = sem("res_lo")
        f_fill, f_evac, ft_fill, ft_evac = sem("f_fill"), sem("f_evac"), sem("ft_fill"), sem("ft_evac")
        dw_fill, dw_sum, dw_hi, dw_lo = sem("dw_fill"), sem("dw_sum"), sem("dw_hi"), sem("dw_lo")
        s_ln, s_lnp, s_lnT, s_ae, s_hc, s_h = (sem(n) for n in ("s_ln", "s_lnp", "s_lnT", "s_ae", "s_hc", "s_h"))
        s_eq, s_in, s_hbt = (sem(n) for n in ("s_eq", "s_in", "s_hbt"))
        d_fill, d_free = sem("d_fill"), sem("d_free")
        a_fill, a_free = sem("a_fill"), sem("a_free")
        dh, ah, al = sem("dh"), sem("ah"), sem("al")
        x_in = sem("x_in")
        s_mark = sem("s_mark")
        st_out = sem("st_out")
        g_diff, g_tanh = sem("g_diff"), sem("g_tanh")
        g_mat, gt_copy = sem("g_mat"), sem("gt_copy")
        r_row = sem("r_row")
        h_row = sem("h_row")
        p_in, p_out = sem("p_in"), sem("p_out")
        sq = sem("sq")
        xn_row = sem("xn_row")
        x3f = sem("x3f")
        yf, yh, yl = sem("yf"), sem("yh"), sem("yl")
        hs_row, hs_tanh, n_row = sem("hs_row"), sem("hs_tanh"), sem("n_row")
        l_pe, l_pre, l_tg, l_w, l_d, l_c, l_tc, l_hi, l_h, l_lo, l_copy = (
            sem(n) for n in ("l_pe", "l_pre", "l_tg", "l_w", "l_d", "l_c", "l_tc", "l_hi", "l_h", "l_lo", "l_copy"))

        V, A_, PE, G = nc.vector, nc.scalar, nc.tensor, nc.gpsimd
        block = ctx.enter_context(nc.Block())

        def col(name, n=1, i=0):
            return COL[:, CO[name] + i:CO[name] + i + n]

        def row(name, n):
            return ROW[:, RO[name]:RO[name] + n]

        def tmp(name, n, i=0):
            return TMP[:, TO[name] + i:TO[name] + i + n]

        def res(name, at, n):
            o = OFF[name] + at
            return WH[:, o:o + n], WL[:, o:o + n]

        def pair(hi, lo, at, n):
            return hi[:, at:at + n], lo[:, at:at + n]

        def ew(half, par, at, n):
            t = EW[half][par]
            return t[:, at:at + n], t[:, HW + at:HW + at + n]

        def dwp(which, b, c, at, n):
            o = ((which * B + b) * C + c) * D + at
            return DWH[:, o:o + n], DWL[:, o:o + n]

        def dbank(stage, i):
            return DP[place(stage, i)[1] % DB]

        def abank(stage, i):
            return AP_[(PLACE["a", stage][1] + i) % AB]

        def at(t, start, n):
            return t[:, start:start + n] if isinstance(start, int) else t[:, bass.ds(start, n)]

        def xp_pair(half):
            v = XP[:, :].rearrange("p (s q b) -> p b s q", q=2 * GC, b=B)
            return v[:, :, half * (TB // 2):(half + 1) * (TB // 2), :]

        def steps(k, dyn, s, n=1):
            return k * TB + (s + n) if isinstance(dyn, int) else k * TB + dyn + (s + n) if not isinstance(k, int) \
                else dyn + (k * TB + s + n)

        RBO = {"bu": 0, "b2": 256, "eb": 512, "eb12": 768, "b3": 1280}

        @block.sync
        def _(sp):
            for dst, src in ((COL[:, :], a["cols"]), (ROW[:, :], a["rows"]), (RB[:, :], a["rb"]), (B1[:, :], a["b1"]),
                             (GAIN[:, :], a["gain"]), (CENT[:, :], a["tmpw"][:, TO["cent"]:TO["cent"] + C * E])):
                sp.dma_start(dst, src).then_inc(s_const, 16)
            sp.dma_start(LNX[:, :], a["cond"]).then_inc(s_const, 16)
            sp.dma_start(TMP[:, 0:NTMP], a["tmpw"]).then_inc(s_tmpw, 16)
            sp.dma_start(IDXI[:, :], a["idx"]).then_inc(s_idx, 16)

            def load(n, slot, src, width):
                sp.wait_ge(raw_free, n + 1)
                sp.dma_start(RAW[slot][:, 0:width], src).then_inc(raw_in[slot], 16)

            n = 0
            for f in range(F_UNITS):
                load(n, n % RS, a["factors"][f], RU)
                n += 1
            for o, w, _ in RES_UNITS:
                load(n, n % RS, a["resident"][:, o:o + w], w)
                n += 1

            def store(u, dst):
                sp.dma_start(dst.rearrange("p (v c) -> p v c", v=2)[:, :, (u % 2) * RU:(u % 2 + 1) * RU],
                             STAGE[u].rearrange("p (v c) -> p v c", v=2)).then_inc(split_out[u], 16)

            for u in range(UPS):
                load(n + u, (n + u) % RS, a["stream"][0, :, u * RU:(u + 1) * RU], RU)
            with sp.Fori(1, NEW) as q:
                for u in range(UPS):
                    load(q * UPS + (n + u), (n + u) % RS,
                         a["stream"][bass.ds(q, 1), :, u * RU:(u + 1) * RU].squeeze(0), RU)
                    store(u, split[bass.ds(q - 1, 1), u // 2].squeeze(0))
            for u in range(UPS):
                sp.wait_ge(raw_free, n + NEW * UPS + u + 1)
                store(u, split[NEW - 1, u // 2])
            for u in range(UPS):
                sp.wait_ge(split_out[u], 16 * NEW)

            def half_set(e, half, par):
                src = split[e, half] if isinstance(e, int) else split[bass.ds(e, 1), half].squeeze(0)
                sp.dma_start(EW[half][par][:, :], src).then_inc(w_in[half][par], 16)

            for e in range(2):
                for half in range(2):
                    half_set(e, half, e)

            def sets(k, last):
                with sp.Fori(0, NE1 // 2) as p:
                    for j in range(2):
                        e = 2 * p + j
                        sp.wait_ge(a_fill, base("a", k, "C") + e * M1 + M1)
                        half_set(e + 2, 0, j)
                        sp.wait_ge(d_fill, base("d", k, "C") + e * B + (PLACE["d", "down"][1] + B))
                        half_set(e + 2, 1, j)
                if not last:
                    for par, stage, i in ((0, "exp2", 15), (1, "hid3", 23)):
                        sp.wait_ge(d_fill, d_count(k, stage, i))
                        half_set(par, 0, par)
                        half_set(par, 1, par)

            with sp.Fori(1, NBLK - 1) as k:
                sets(k, False)
            sets(NBLK - 1, False)
            sets(NBLK, True)
            for half in range(2):
                for par in range(2):
                    sp.wait_ge(w_in[half][par], 16 * NBLK * (NEW // 2))
            sp.wait_ge(st_out, 16 * NBLK * B)

        @block.gpsimd
        def _(g):
            g.sem_inc(l_copy, 2)
            g.dma_start(RX[:, :].rearrange("p (b c) -> p b c", b=B),
                        a["x"][:, 0:TB, :].rearrange("b p c -> p b c")).then_inc(x_in, 16)
            G.memset(IDF[:, :], 0.0).then_inc(s_gen, 1)
            G.memset(IDH[:, :], 0.0).then_inc(s_gen, 1)
            G.memset(PW[:, :], -0.5).then_inc(s_gen, 1)
            G.iota(IOTA[:, :], [[1, T]], base=0, channel_multiplier=0,
                   allow_small_or_imprecise_dtypes=True).then_inc(s_gen, 1)
            g.wait_ge(s_gen, 4)
            G.affine_select(out=IDF[:, :], in_=IDF[:, :], compare_op=ALU.not_equal, fill=1.0, base=0,
                            pattern=[[-1, P]], channel_multiplier=1).then_inc(s_gen, 1)
            G.affine_select(out=IDH[:, :], in_=IDH[:, :], compare_op=ALU.not_equal, fill=1.0, base=0,
                            pattern=[[-1, P]], channel_multiplier=1).then_inc(s_gen, 1)
            g.wait_ge(s_ln, 1)
            G.tensor_tensor(SM[0:B, 2:3], SM[0:B, 1:2], PW[0:B, 0:1], ALU.pow).then_inc(s_lnp, 1)

            def step(k, dyn, s):
                g.wait_ge(l_h, steps(k, dyn, s))
                if isinstance(dyn, int) and not isinstance(k, int):
                    g.sem_inc(s_mark, 1)
                h = HT[:, :].rearrange("p (q s) -> p q s", s=TB)
                h = h[:, :, s:s + 1] if isinstance(dyn, int) else h[:, :, bass.ds(dyn + s, 1)]
                G.tensor_copy(h, HF[s % 2][:, :].rearrange("p (q o) -> p q o", o=1)).then_inc(l_copy, 1)

            def load_x(k):
                g.wait_ge(r_row, base("rrow", k, "X"))
                g.sem_inc(s_mark, 1)
                src = a["x"][:, TB:2 * TB, :] if isinstance(k, int) else a["x"][:, bass.ds(k * TB + TB, TB), :]
                g.dma_start(RX[:, :].rearrange("p (b c) -> p b c", b=B), src.rearrange("b p c -> p b c")).then_inc(x_in, 16)

            def c_part(k, slot):
                g.wait_ge(p_in, plus(k, "pow", "C", 1))
                G.tensor_tensor(SM[:, 8:12], SM[:, 4:8], PW[:, 0:4], ALU.pow).then_inc(p_out, 1)
                g.wait_ge(d_fill, d_count(k, "uT", B - 1))
                g.sem_inc(s_mark, 1)
                slot.bare(C_SLOTS - 12)
                for j in range(B):
                    slot.bare(2 if j else 1)
                    g.wait_ge(p_in, plus(k, "pow", "C", 2 + j))
                    G.tensor_tensor(SM[:, 24 + 2 * j:26 + 2 * j], SM[:, 16 + 2 * j:18 + 2 * j], PW[:, 0:2],
                                    ALU.pow).then_inc(p_out, 1)
                slot.bare(1)
                for j in range(B):
                    slot.bare(1)
                    g.wait_ge(r_row, plus(k, "rrow", "C", 2 * B + j + 1))
                    g.sem_inc(s_mark, 1)
                    dst = out[j, (k - 1) * TB:k * TB, :] if isinstance(k, int) else out[j, bass.ds((k - 1) * TB, TB), :]
                    g.dma_start(dst, RES[:, j * D:(j + 1) * D]).then_inc(st_out, 16)

            load_x(0)
            Slots(g, step, 0).bare(TB)
            with g.Fori(1, NBLK - 1) as k:
                load_x(k)
                slot = Slots(g, step, k)
                c_part(k, slot)
                slot.bare(TB - C_SLOTS)
            slot = Slots(g, step, NBLK - 1)
            c_part(NBLK - 1, slot)
            slot.bare(TB - C_SLOTS)
            c_part(NBLK, Slots(g, None, NBLK))

        @block.scalar
        def _(act):
            act.wait_ge(s_const, 16 * 7)
            act.wait_ge(s_lnT, 1)
            for c in range(C):
                A_.activation(HC[:, c * B:(c + 1) * B], DP[0][:, c * B:(c + 1) * B], ACT.Identity,
                              scale=col("g0", 1, c), bias=col("be0", 1, c)).then_inc(s_ae, 1)
                A_.activation(HC[:, (C + c) * B:(C + c + 1) * B], DP[0][:, c * B:(c + 1) * B], ACT.Identity,
                              scale=col("g3", 1, c), bias=col("be3", 1, c)).then_inc(s_ae, 1)
            act.wait_ge(s_hc, 1)
            for w in range(2):
                for m in range(C):
                    A_.activation(HID[:, (w * C + m) * B:(w * C + m + 1) * B],
                                  DP[1][:, (w * C + m) * B:(w * C + m + 1) * B], ACT.Gelu,
                                  bias=col("b1_3" if w else "b1_0", 1, m)).then_inc(s_h, 1)
            for t in range(12):
                act.wait_ge(dw_sum, t + 1)
                A_.activation(DWH[:, t * 2 * D:(t + 1) * 2 * D], TT[t % 2][:, :], ACT.Copy, scale=S).then_inc(dw_hi, 1)
            for i, (o, w, sc) in enumerate(RES_UNITS):
                n = F_UNITS + i
                act.wait_ge(raw_in[n % RS], 16 * (n // RS + 1))
                A_.activation(WH[:, o:o + w], RAW[n % RS][:, 0:w], ACT.Copy, scale=sc).then_inc(w_hi, 1)

            def step(k, dyn, s):
                n = steps(k, dyn, s)
                act.wait_ge(l_pre, n)
                A_.activation(TG[:, 0:GC * B], PRE[:, :], ACT.Tanh, scale=1.0 / 128).then_inc(l_tg, 1)
                act.wait_ge(l_d, n)
                A_.activation(TC[:, :], DC[:, :], ACT.Tanh, scale=0.5).then_inc(l_tc, 1)

            def d_hi(k, stage, i, dst, scale=1.0):
                act.wait_ge(d_fill, d_count(k, stage, i))
                A_.activation(dst, dbank(stage, i)[:, :], ACT.Copy, scale=scale).then_inc(dh, 1)

            def a_split(fills, lows, frees, par, evac, hi_dst, view=None):
                act.wait_ge(a_fill, fills)
                act.wait_ge(al, lows)
                evac(TT[par])
                act.wait_ge(a_free, frees)
                A_.activation(hi_dst, TT[par][:, :] if view is None else view(TT[par]), ACT.Copy).then_inc(ah, 1)

            def split_a(k, stage, i, evac, hi_dst, view=None):
                a_split(a_count(k, stage, i), a_count(k, stage, i), a_count(k, stage, i, AB), i % 2, evac, hi_dst, view)

            def xp_half(k, half, ms):
                for m in ms:
                    def evac(t, m=m):
                        A_.activation(t[:, 0:NT // 2], abank(f"xp{half}", m)[:, 0:NT // 2], ACT.Identity,
                                      scale=2.0 if m >= 6 else 1.0, bias=LB0[:, m:m + 1]).then_inc(a_free, 1)
                    split_a(k, f"xp{half}", m, evac, xp_pair(half)[:, :, :, 2 * m],
                            lambda t: t[:, 0:NT // 2].rearrange("p (b s) -> p b s", b=B))

            def up(k, e, par, m):
                def evac(t):
                    A_.activation(t[:, :], abank("up", m)[:, :], ACT.Gelu, scale=IS,
                                  bias=B1CUR[par][:, m:m + 1]).then_inc(a_free, 1)
                if m == 0:
                    act.wait_ge(b1_ready, base("b1", k, "C") + e + 1)
                n = base("a", k, "C") + e * M1 + m
                a_split(n + 1, n + 1, n + 1 + AB, m % 2, evac, GH[par][:, m * NT:(m + 1) * NT])

            def a_part(k, slot):
                slot()
                for c in range(C):
                    d_hi(k, "xT", c, QH[:, c * NT:(c + 1) * NT])
                for m in range(C):
                    slot()
                    d_hi(k, "y0T", m, ZH[:, m * NT:(m + 1) * NT], IS)
                act.wait_ge(g_diff, plus(k, "diff", "A", 1))
                A_.activation(SM[:, 36:40], SM[:, 32:36], ACT.Tanh, scale=0.5).then_inc(g_tanh, 1)
                slot()
                slot()
                for j in range(B):
                    if j % 2 == 0:
                        slot()
                    d_hi(k, "h0T", j, KH[:, j * 512:(j + 1) * 512])
                slot()
                slot()
                for c in range(C):
                    d_hi(k, "x1T", c, QH[:, c * NT:(c + 1) * NT])
                for m in range(0, GC, 4):
                    slot()
                    xp_half(k, 0, range(m, m + 4))

            def c_part(k, slot, x):
                act.wait_ge(g_diff, plus(k, "diff", "C", 1))
                A_.activation(SC[:, 0:B * E], L[:, 0:B * E], ACT.Tanh, scale=0.5).then_inc(g_tanh, 1)
                for j in range(B):
                    act.wait_ge(d_fill, d_count(k, "uT", j))
                    A_.activation(JUNK[:, j * D:(j + 1) * D], dbank("uT", j)[:, 0:D], ACT.Square, scale=0.5,
                                  accum_out=SM[:, j:j + 1]).then_inc(sq, 1)
                if x:
                    for m in range(0, GC, 4):
                        slot()
                        xp_half(k, 1, range(m, m + 4))
                slot()
                slot()
                for c in range(C):
                    d_hi(k, "xnT", c, QH[:, c * NT:(c + 1) * NT])
                slot()
                slot()
                for m in range(M1):
                    if m % 2 == 0:
                        slot()
                    up(k, 0, 0, m)
                with slot.repeat(0, 4, 2 * M1) as p:
                    for j in range(2):
                        for m in range(M1):
                            slot()
                            up(k, 2 * p + (j + 1), (j + 1) % 2, m)
                for m in range(M1):
                    slot()
                    up(k, NE1 - 1, 1, m)
                slot.bare(B)

                for m in range(C):
                    slot()
                    if m == 0:
                        for c in range(C):
                            d_hi(k, "x2T", c, QH[:, c * NT:(c + 1) * NT])

                    def evac(t, m=m):
                        for b in range(B):
                            ins = A_.activation(t[:, b * TB:(b + 1) * TB], abank("z2", m)[:, b * TB:(b + 1) * TB],
                                                ACT.Tanh, scale=IS, bias=HBT[:, m * B + b:m * B + b + 1])
                        ins.then_inc(a_free, 1)
                    split_a(k, "z2", m, evac, ZH[:, m * NT:(m + 1) * NT])
                act.wait_ge(g_diff, plus(k, "diff", "C", 2))
                A_.activation(SM[:, 36:40], SM[:, 32:36], ACT.Tanh, scale=0.5).then_inc(g_tanh, 1)
                slot.bare(10)

                for m in range(C):
                    slot()
                    if m == 0:
                        for c in range(C):
                            act.wait_ge(d_fill, d_count(k, "x3T", c))
                            A_.activation(YF[:, c * NT:(c + 1) * NT], dbank("x3T", c)[:, :], ACT.Copy).then_inc(x3f, 1)
                            d_hi(k, "x3T", c, QH[:, c * NT:(c + 1) * NT])

                    def evac(t, m=m):
                        A_.activation(t[:, :], abank("mid", m)[:, :], ACT.Gelu, scale=IS).then_inc(a_free, 1)
                    split_a(k, "mid", m, evac, ZH[:, m * NT:(m + 1) * NT])
                slot()
                for m in range(C):
                    act.wait_ge(yf, (k - 1) * C + m + 1)
                    A_.activation(QH[:, m * NT:(m + 1) * NT], YF[:, m * NT:(m + 1) * NT], ACT.Copy).then_inc(yh, 1)
                slot()
                act.wait_ge(g_diff, plus(k, "diff", "C", 3))
                A_.activation(SC[:, :], L[:, :], ACT.Tanh, scale=0.5).then_inc(g_tanh, 1)
                act.wait_ge(g_diff, plus(k, "diff", "C", 4))
                A_.activation(SM[:, 36:40], SM[:, 32:36], ACT.Tanh, scale=0.5).then_inc(g_tanh, 1)
                slot.bare(3)
                for j in range(B):
                    if j:
                        slot()
                    slot()
                    act.wait_ge(hs_row, (k - 1) * B + j + 1)
                    hv = HB[j % 2][:, :].rearrange("p (v w h) -> p v w h", v=2, w=2)
                    A_.activation(TT[0][:, (j % 2) * 256:(j % 2) * 256 + 256].rearrange("p (v h) -> p v h", v=2),
                                  hv[:, :, 0, :], ACT.Tanh, scale=0.5).then_inc(hs_tanh, 1)
                slot()
                for v in range(2):
                    def evac(t, v=v):
                        A_.activation(t[:, :], abank("nT", v)[:, :], ACT.Identity,
                                      scale=col("s_g" if v else "sel_g"), bias=col("s_b" if v else "sel_b")).then_inc(a_free, 1)
                    split_a(k, "nT", v, evac, ZH[:, v * NT:(v + 1) * NT])
                slot.bare(B)

            none = Slots(act, None, 0)
            a_part(-1, none)

            slot = Slots(act, step, 0)
            for m in range(0, GC, 4):
                slot()
                xp_half(0, 1, range(m, m + 4))
            slot.bare(1)

            def split_set(q):
                act.wait_ge(pg_ready, q + 1)
                for u in range(UPS):
                    r = (SETUP_UNITS + u) % RS
                    for half in range(2):
                        slot()
                        if half == 0:
                            act.wait_ge(raw_in[r], q * 16 + 16 * ((SETUP_UNITS + u) // RS + 1))
                            if not isinstance(q, int):
                                act.wait_ge(split_out[u], q * 16)
                        o = half * (RU // 2)
                        A_.activation(STAGE[u][:, o:o + RU // 2], RAW[r][:, o:o + RU // 2], ACT.Identity,
                                      scale=PG[:, u:u + 1]).then_inc(e_hi, 1)

            split_set(0)
            with slot.repeat(1, NEW, 2 * UPS) as q:
                split_set(q)
            slot.bare(BARE0)
            for u in range(UPS):
                act.wait_ge(split_out[u], 16 * NEW)
            a_part(0, slot)
            with act.Fori(1, NBLK - 1) as k:
                slot = Slots(act, step, k)
                c_part(k, slot, True)
                a_part(k, slot)
            slot = Slots(act, step, NBLK - 1)
            c_part(NBLK - 1, slot, True)
            slot.bare(TB - C_SLOTS)
            c_part(NBLK, none, False)

        @block.vector
        def _(dve):
            def done(sem_, n=1):
                V.drain().then_inc(sem_, n)

            done(raw_free, RS)
            done(l_c)
            done(d_free, DB)
            done(al, 2)
            dve.wait_ge(s_const, 16 * 7)
            V.bn_stats(ST[0:B, 0:6], LNX[:, :])
            V.drain()
            V.bn_aggr(SM[0:B, 0:2], ST[0:B, 0:6])
            V.drain()
            V.tensor_scalar(SM[0:B, 1:2], SM[0:B, 1:2], LN_EPS, None, ALU.add).then_inc(s_ln, 1)
            V.tensor_scalar(LB0[:, 0:6], col("lstm_b", 6), S, None, ALU.mult)
            V.tensor_scalar(LB0[:, 6:8], col("lstm_b", 2, 6), 2 * S, None, ALU.mult)
            V.tensor_scalar(GAIN[:, :], GAIN[:, :], S, None, ALU.mult)
            V.memset(TG[:, GC * B:(GC + C) * B], 0.0)
            V.tensor_scalar(HF[1][:, :], col("condT", C * B), 2.0, None, ALU.mult)
            V.drain()
            h0v = H16[0][:, :].rearrange("p (c v b) -> p c v b", c=C, v=2)
            hfv = [HF[i][:, :].rearrange("p (c b) -> p c b", c=C) for i in range(2)]
            V.tensor_copy(h0v[:, :, 0, :], hfv[1])
            V.drain()
            V.tensor_tensor(h0v[:, :, 1, :], hfv[1], h0v[:, :, 0, :], ALU.subtract)
            done(l_hi)
            done(l_lo)
            dve.wait_ge(s_lnp, 1)
            V.tensor_scalar(LNX[:, :], LNX[:, :], SM[0:B, 0:1], SM[0:B, 2:3], ALU.subtract, ALU.mult)
            done(s_ln)
            dve.wait_ge(s_gen, 6)
            dve.wait_ge(s_idx, 16)
            V.tensor_copy(IDXF[:, :], IDXI[:, :])
            V.drain()
            V.tensor_scalar(IDXG[:, 0:4], IDXF[:, 0:4], 0.0, float(B), ALU.is_lt, ALU.mult)
            V.tensor_scalar(IDXG[:, 4:8], IDXF[:, 4:8], 0.0, float(T), ALU.is_lt, ALU.mult)
            V.drain()
            V.tensor_tensor(IDXF[:, :], IDXF[:, :], IDXG[:, :], ALU.add)
            V.drain()
            for i in range(4):
                V.tensor_scalar(EQB[:, i * B:(i + 1) * B], IOTA[:, 0:B], IDXF[:, i:i + 1], None, ALU.is_equal)
                V.tensor_scalar(EQT[:, i * T:(i + 1) * T], IOTA[:, :], IDXF[:, 4 + i:5 + i], None, ALU.is_equal)
            done(s_eq)
            dve.wait_ge(s_in, 1)
            V.tensor_scalar(INSET[:, :], DP[3][:, 0:NBLK * B], 1.0, None, ALU.min)
            dve.wait_ge(s_hbt, 1)
            for m in range(C):
                V.tensor_scalar(HBT[:, m * B:(m + 1) * B], DP[2][:, m * B:(m + 1) * B], col("bhh", 1, m),
                                col("bih", 1, m), ALU.add, ALU.add)
            dve.wait_ge(s_tmpw, 16)
            for c in range(C):
                o = TO["base0"] + c * D + c * P
                V.tensor_tensor(TMP[:, o:o + P], TMP[:, o:o + P], IDF[:, :], ALU.add)
            V.drain()
            for f in range(F_UNITS // 2):
                which, c = f // C, f % C
                for half in range(2):
                    n = 2 * f + half
                    dve.wait_ge(f_fill, n + 1)
                    for b in range(B):
                        o = (which * C + c) * R + half * 4
                        V.tensor_tensor(FV[:, b * R + half * 4:b * R + half * 4 + 4],
                                        DP[0][:, 0:16].rearrange("p (r b) -> p b r", b=B)[:, b, :],
                                        col("fb", 4, o), ALU.add)
                    V.drain().then_inc(raw_free, 1)
                    done(f_evac)
                dve.wait_ge(ft_fill, f + 1)
                ftv = FT[:, :].rearrange("r (w b d) -> r w b d", w=2, b=B)
                V.tensor_copy(ftv[:, which % 2, :, c * P:(c + 1) * P],
                              DP[1][0:R, :].rearrange("r (b d) -> r b d", b=B))
                done(ft_evac)
                if f % 4 == 3:
                    w3 = f // 4
                    base_ = ("base0", "base_down", "base_upT")[w3]
                    for b in range(B):
                        t = w3 * 4 + b
                        dve.wait_ge(dw_fill, t + 1)
                        if t >= 2:
                            dve.wait_ge(dw_hi, t - 1)
                        V.tensor_tensor(TT[t % 2][:, :], DP[2 + t % 2][:, :], tmp(base_, C * D), ALU.add).then_inc(dw_sum, 1)
                        dve.wait_ge(dw_hi, t + 1)
                        V.scalar_tensor_tensor(DWL[:, t * 2 * D:(t + 1) * 2 * D], TT[t % 2][:, :], S,
                                               DWH[:, t * 2 * D:(t + 1) * 2 * D], ALU.mult, ALU.subtract).then_inc(dw_lo, 1)
                    V.drain()
            for i, (o, w, sc) in enumerate(RES_UNITS):
                n = F_UNITS + i
                dve.wait_ge(w_hi, i + 1)
                V.scalar_tensor_tensor(WL[:, o:o + w], RAW[n % RS][:, 0:w], sc, WH[:, o:o + w],
                                       ALU.mult, ALU.subtract).then_inc(raw_free, 1)
            done(res_lo)

            def step(k, dyn, s):
                j, n = s % 2, steps(k, dyn, s)
                h16 = H16[(j + 1) % 2][:, :].rearrange("p (c v b) -> p c v b", c=C, v=2)
                dve.wait_ge(l_pe, n)
                V.tensor_reduce(PRE[:, :].rearrange("p (c b) -> p c b", c=GC),
                                GP[j][:, 0:GC * 2 * B].rearrange("p (c v b) -> p c b v", v=2, b=B),
                                AX.X, ALU.add).then_inc(l_pre, 1)
                dve.wait_ge(l_tg, n)
                V.scalar_tensor_tensor(WK[:, :], TG[:, 0:16], 1.0, TG[:, 24:40], ALU.add, ALU.mult).then_inc(l_w, 1)
                dve.wait_ge(l_w, n)
                V.tensor_tensor(DC[:, :], WK[:, 0:8], WK[:, 8:16], ALU.add).then_inc(l_d, 1)
                dve.wait_ge(l_d, n)
                V.tensor_scalar(TG[:, 32:40], DC[:, :], 0.5, None, ALU.mult).then_inc(l_c, 1)
                dve.wait_ge(l_tc, n)
                tov = TG[:, 16:24].rearrange("p (c b) -> p c b", c=C)
                tcv = TC[:, :].rearrange("p (c b) -> p c b", c=C)
                V.scalar_tensor_tensor(h16[:, :, 0, :], tov, 1.0, tcv, ALU.add, ALU.mult).then_inc(l_hi, 1)
                dve.wait_ge(l_copy, n)
                V.scalar_tensor_tensor(hfv[j], tov, 1.0, tcv, ALU.add, ALU.mult).then_inc(l_h, 1)
                dve.wait_ge(l_hi, steps(k, dyn, s, 2))
                dve.wait_ge(l_h, n)
                V.tensor_tensor(h16[:, :, 1, :], hfv[j], h16[:, :, 0, :], ALU.subtract).then_inc(l_lo, 1)

            def d_lo(k, stage, i, hi, dst, scale=1.0):
                dve.wait_ge(dh, h_count(k, stage, i))
                V.scalar_tensor_tensor(dst, dbank(stage, i)[:, :], scale, hi, ALU.mult, ALU.subtract).then_inc(d_free, 1)

            def q_lo(k, stage):
                for c in range(C):
                    d_lo(k, stage, c, QH[:, c * NT:(c + 1) * NT], QL[:, c * NT:(c + 1) * NT])

            def z_lo(k, stage, i):
                dve.wait_ge(ah, a_count(k, stage, i))
                V.tensor_tensor(ZL[:, i * NT:(i + 1) * NT], TT[i % 2][:, :], ZH[:, i * NT:(i + 1) * NT],
                                ALU.subtract).then_inc(al, 1)

            def up_lo(k, e, par, m):
                dve.wait_ge(ah, base("a", k, "C") + e * M1 + (m + 1))
                V.tensor_tensor(GL[par][:, m * NT:(m + 1) * NT], TT[m % 2][:, :], GH[par][:, m * NT:(m + 1) * NT],
                                ALU.subtract).then_inc(al, 1)

            def down_add(k, e, par, j):
                dve.wait_ge(d_fill, base("d", k, "C") + e * B + (PLACE["d", "down"][1] + j + 1))
                r = RES[:, j * D:(j + 1) * D]
                V.scalar_tensor_tensor(r, dbank("down", j)[:, 0:D], GCUR[par][:, j:j + 1], r,
                                       ALU.mult, ALU.add).then_inc(d_free, 1)

            def xp_half(k, half, ms):
                for m in ms:
                    xv = xp_pair(half)
                    dve.wait_ge(ah, a_count(k, f"xp{half}", m))
                    V.tensor_tensor(xv[:, :, :, 2 * m + 1], TT[m % 2][:, 0:NT // 2].rearrange("p (b s) -> p b s", b=B),
                                    xv[:, :, :, 2 * m], ALU.subtract).then_inc(al, 1)

            def filled(k, stage, i):
                dve.wait_ge(d_fill, d_count(k, stage, i))

            def top2(src, n=E):
                for j in range(B):
                    V.max(MX[:, j * 8:(j + 1) * 8], src[:, j * n:j * n + E])
                V.drain()
                for j in range(B):
                    V.max_index(IX[:, j * 8:(j + 1) * 8], MX[:, j * 8:(j + 1) * 8], src[:, j * n:j * n + E])
                V.drain()
                V.tensor_copy(IXF[:, :], IX[:, :])
                mxv = MX[:, :].rearrange("p (j e) -> p j e", j=B)
                V.tensor_tensor(SM[:, 32:36], mxv[:, :, 0], mxv[:, :, 1], ALU.subtract)

            def softmax2(tanhs, scale):
                dve.wait_ge(g_tanh, tanhs)
                V.tensor_scalar(SM[:, 40:44], SM[:, 36:40], 0.5 * scale, 0.5 * scale, ALU.mult, ALU.add)
                V.tensor_scalar(SM[:, 44:48], SM[:, 36:40], -0.5 * scale, 0.5 * scale, ALU.mult, ALU.add)
                V.drain()
                for j in range(B):
                    V.tensor_scalar(GA[:, j * 8:(j + 1) * 8], IOTA[:, 0:E], IXF[:, j * 8:j * 8 + 1],
                                    SM[:, 40 + j:41 + j], ALU.is_equal, ALU.mult)
                    V.tensor_scalar(GT[:, j * 8:(j + 1) * 8], IOTA[:, 0:E], IXF[:, j * 8 + 1:j * 8 + 2],
                                    SM[:, 44 + j:45 + j], ALU.is_equal, ALU.mult)
                V.drain()
                V.tensor_tensor(GT[:, 0:B * E], GT[:, 0:B * E], GA[:, :], ALU.add)
                V.drain()

            def a_part(k, slot):
                slot()
                q_lo(k, "xT")
                for m in range(C):
                    slot()
                    d_lo(k, "y0T", m, ZH[:, m * NT:(m + 1) * NT], ZL[:, m * NT:(m + 1) * NT], IS)
                filled(k, "log0", 0)
                V.tensor_scalar(L[:, 0:B * E], dbank("log0", 0)[:, 0:B * E], IS, None, ALU.mult).then_inc(d_free, 1)
                V.drain()
                top2(L)
                done(g_diff)
                softmax2(plus(k, "diff", "A", 1), 0.5)
                done(g_mat)
                slot()
                filled(k, "g0T", 0)
                V.tensor_scalar(GTT[0:E, 0:NT], dbank("g0T", 0)[0:E, :], S, None, ALU.mult).then_inc(d_free, 1)
                done(gt_copy)
                if not (isinstance(k, int) and k < 0):
                    rows_in(k)

                for j in range(B):
                    if j % 2 == 0:
                        slot()
                    if j >= 2:
                        d_lo(k, "h0T", j - 2, KH[:, (j - 2) * 512:(j - 1) * 512], KL[:, (j - 2) * 512:(j - 1) * 512])
                    filled(k, "h0", j)
                    hb = HB[j % 2]
                    V.scalar_tensor_tensor(hb[:, :], dbank("h0", j)[:, :], IS, row("bd", 512), ALU.mult, ALU.add).then_inc(d_free, 1)
                    V.drain()
                    V.scalar_tensor_tensor(hb[:, :].rearrange("p (e h) -> p e h", e=E),
                                           hb[:, :].rearrange("p (e h) -> p e h", e=E), 0.0,
                                           GT[:, j * E:(j + 1) * E].unsqueeze(2).to_broadcast([P, E, 64]),
                                           ALU.max, ALU.mult)
                    done(h_row)
                slot()
                for j in range(2, B):
                    d_lo(k, "h0T", j, KH[:, j * 512:(j + 1) * 512], KL[:, j * 512:(j + 1) * 512])
                for j in range(B):
                    if j == 2:
                        slot()
                    filled(k, "out0", j)
                    V.scalar_tensor_tensor(RW[:, j * D:(j + 1) * D], dbank("out0", j)[:, 0:D], IS,
                                           RX[:, j * D:(j + 1) * D], ALU.mult, ALU.add).then_inc(d_free, 1)
                    done(r_row)
                slot()
                q_lo(k, "x1T")
                for m in range(0, GC, 4):
                    slot()
                    xp_half(k, 0, range(m, m + 4))

            def rows_in(k):
                if not (isinstance(k, int) and k == 0):
                    dve.wait_ge(st_out, k * (16 * B))
                V.tensor_copy(RES[:, :], RW[:, :])

            def c_part(k, slot, x):
                for j in range(B):
                    filled(k, "log1", j)
                    V.tensor_scalar(L[:, j * E:(j + 1) * E], dbank("log1", j)[:, 0:E], 0.5, None, ALU.mult).then_inc(d_free, 1)
                done(g_diff)
                for j in range(B):
                    filled(k, "uT", j)
                    dve.wait_ge(sq, (k - 1) * B + j + 1)
                    V.tensor_scalar(UT[:, j * D:(j + 1) * D], dbank("uT", j)[:, 0:D], 0.5, None, ALU.mult).then_inc(d_free, 1)
                V.tensor_scalar(SM[:, 4:8], SM[:, 0:4], 1.0 / D, RMS_EPS, ALU.mult, ALU.add)
                done(p_in)
                for e in range(2):
                    V.tensor_copy(B1CUR[e][:, :], B1[:, e * M1:(e + 1) * M1])
                    done(b1_ready)
                if x:
                    for m in range(0, GC, 4):
                        slot()
                        xp_half(k, 1, range(m, m + 4))
                slot()
                V.tensor_tensor(RES[:, :], RES[:, :], UT[:, :], ALU.add)
                V.drain()
                dve.wait_ge(p_out, plus(k, "pow", "C", 1))
                for j in range(B):
                    V.tensor_scalar(UT[:, j * D:(j + 1) * D], UT[:, j * D:(j + 1) * D], SM[:, 8 + j:9 + j], None, ALU.mult)
                done(xn_row)
                dve.wait_ge(g_tanh, plus(k, "diff", "C", 1))
                V.tensor_scalar(SC[:, 0:B * E], SC[:, 0:B * E], 0.5, 0.5, ALU.mult, ALU.add)
                V.drain()
                top2(SC)
                slot()
                q_lo(k, "xnT")
                V.reduce_sum(SM[:, 48:52], SC[:, 0:B * E].rearrange("p (j e) -> p j e", j=B), AX.X)
                V.drain()
                V.reciprocal(SM[:, 52:56], SM[:, 48:52])
                V.memset(GT[:, :], 1.0)
                for j in range(B):
                    V.tensor_scalar(GA[:, j * 8:(j + 1) * 8], IOTA[:, 0:E], IXF[:, j * 8:j * 8 + 1], None, ALU.is_equal)
                V.drain()
                for j in range(B):
                    V.scalar_tensor_tensor(GA[:, j * 8:(j + 1) * 8], IOTA[:, 0:E], IXF[:, j * 8 + 1:j * 8 + 2],
                                           GA[:, j * 8:(j + 1) * 8], ALU.is_equal, ALU.add)
                V.drain()
                for j in range(B):
                    V.scalar_tensor_tensor(GT[:, j * NE1 + 2:(j + 1) * NE1], SC[:, j * E:(j + 1) * E], SM[:, 52 + j:53 + j],
                                           GA[:, j * 8:(j + 1) * 8], ALU.mult, ALU.mult)
                V.drain()
                V.tensor_scalar(GE[:, :].rearrange("p (e j) -> p j e", j=B), GT[:, :].rearrange("p (j e) -> p j e", j=B),
                                IS, None, ALU.mult)
                done(g_mat)
                slot()
                for h in range(2):
                    filled(k, "g1T", h)
                    V.tensor_copy(GTT[0:NE1, h * 256:(h + 1) * 256], dbank("g1T", h)[0:NE1, 0:256]).then_inc(d_free, 1)
                done(gt_copy)
                slot()
                for j in range(B):
                    filled(k, "bias1", j)
                    r = RES[:, j * D:(j + 1) * D]
                    V.tensor_tensor(r, dbank("bias1", j)[:, 0:D], r, ALU.add).then_inc(d_free, 1)
                for t in range(M1 // 2):
                    slot()
                    if t:
                        up_lo(k, 0, 0, 2 * t - 2)
                        up_lo(k, 0, 0, 2 * t - 1)
                    if t == M1 // 2 - 1:
                        up_lo(k, 0, 0, 2 * t)

                def group(e, par, last):
                    for i in range(M1):
                        slot()
                        if i == 0:
                            up_lo(k, e, par, M1 - 1)
                            V.tensor_copy(GCUR[par][:, :], at(GE, e * B, B))
                            if not last:
                                V.tensor_copy(B1CUR[par][:, :], at(B1, (e + 2) * M1, M1))
                                done(b1_ready)
                        else:
                            up_lo(k, e + 1, 1 - par, i - 1)
                        if i % 2 == 0 and i:
                            down_add(k, e, par, i // 2 - 1)
                        if i == M1 - 1:
                            down_add(k, e, par, B - 1)

                with slot.repeat(0, 4, 2 * M1) as p:
                    for j2 in range(2):
                        group(2 * p + j2, j2, False)
                group(NE1 - 2, 0, True)
                for j in range(B):
                    slot()
                    if j == 0:
                        up_lo(k, NE1 - 1, 1, M1 - 1)
                        V.tensor_copy(GCUR[1][:, :], at(GE, (NE1 - 1) * B, B))
                        V.drain()
                    down_add(k, NE1 - 1, 1, j)
                done(r_row, B)

                slot()
                q_lo(k, "x2T")
                slot()
                for m in range(C):
                    z_lo(k, "z2", m)
                filled(k, "log2", 0)
                for j in range(B):
                    ins = V.scalar_tensor_tensor(L[:, j * E:(j + 1) * E], dbank("log2", 0)[:, j * E:(j + 1) * E], IS,
                                                 row("gate_b", E), ALU.mult, ALU.add)
                ins.then_inc(d_free, 1)
                V.drain()
                top2(L)
                done(g_diff)
                softmax2(plus(k, "diff", "C", 2), 1.0)
                V.tensor_scalar(GT2[:, 0:B * E], GT[:, 0:B * E], IS, None, ALU.mult)
                done(g_mat)
                slot()
                for h in range(2):
                    filled(k, "g2T", h)
                    V.tensor_copy(GTT[0:E, h * 256:(h + 1) * 256], dbank("g2T", h)[0:E, 0:256]).then_inc(d_free, 1)
                done(gt_copy)
                slot()
                for j in range(B):
                    filled(k, "bias2", j)
                    r = RES[:, j * D:(j + 1) * D]
                    V.tensor_tensor(r, dbank("bias2", j)[:, 0:D], r, ALU.add).then_inc(d_free, 1)
                for j in range(B):
                    for w in range(4):
                        if w % 2 == 0:
                            slot()
                        else:
                            V.drain()
                        filled(k, "exp2", j * 4 + w)
                        r = RES[:, j * D:(j + 1) * D]
                        for h in range(2):
                            if h:
                                V.drain()
                            e = 2 * w + h
                            ins = V.scalar_tensor_tensor(r, dbank("exp2", j * 4 + w)[:, h * D:(h + 1) * D],
                                                         GT2[:, j * E + e:j * E + e + 1], r, ALU.mult, ALU.add)
                        ins.then_inc(d_free, 1)
                done(r_row, B)

                slot()
                q_lo(k, "x3T")
                z_lo(k, "mid", 0)
                slot()
                z_lo(k, "mid", 1)
                slot()
                dve.wait_ge(x3f, (k - 1) * C + C)
                for m in range(C):
                    filled(k, "y3T", m)
                    y = YF[:, m * NT:(m + 1) * NT]
                    V.scalar_tensor_tensor(y, dbank("y3T", m)[:, :], IS, y, ALU.mult, ALU.add).then_inc(d_free, 1)
                    done(yf)
                    dve.wait_ge(yh, (k - 1) * C + m + 1)
                    V.tensor_tensor(QL[:, m * NT:(m + 1) * NT], y, QH[:, m * NT:(m + 1) * NT], ALU.subtract).then_inc(yl, 1)
                slot()
                filled(k, "log3", 0)
                for j in range(B):
                    ins = V.scalar_tensor_tensor(L[:, j * 9:(j + 1) * 9], dbank("log3", 0)[:, j * 9:(j + 1) * 9], IS,
                                                 row("egsg_b", 9), ALU.mult, ALU.add)
                ins.then_inc(d_free, 1)
                done(g_diff)
                dve.wait_ge(g_tanh, plus(k, "diff", "C", 3))
                V.tensor_scalar(SC[:, :], SC[:, :], 0.5, 0.5, ALU.mult, ALU.add)
                V.drain()
                for j in range(B):
                    V.tensor_tensor(SB_[:, j * E:(j + 1) * E], SC[:, j * 9:j * 9 + E], row("exp_bias", E), ALU.add)
                V.drain()
                top2(SB_)
                V.tensor_copy(IN[:, :], at(INSET, (k - 1) * B, B))
                V.drain()
                for j in range(B):
                    V.tensor_scalar(GA[:, j * 8:(j + 1) * 8], IOTA[:, 0:E], IXF[:, j * 8:j * 8 + 1], None, ALU.is_equal)
                V.drain()
                V.tensor_tensor(SB_[:, :].rearrange("p (j e) -> p j e", j=B), GA[:, :].rearrange("p (j e) -> p j e", j=B),
                                SC[:, :].rearrange("p (j e) -> p j e", j=B)[:, :, 0:E], ALU.mult)
                V.drain()
                V.reduce_sum(SM[:, 48:52], SB_[:, :].rearrange("p (j e) -> p j e", j=B), AX.X)
                V.drain()
                V.tensor_tensor(SM[:, 32:36], SC[:, :].rearrange("p (j e) -> p j e", j=B)[:, :, E], SM[:, 48:52], ALU.subtract)
                done(g_diff)
                dve.wait_ge(g_tanh, plus(k, "diff", "C", 4))
                V.tensor_scalar(SM[:, 40:44], SM[:, 36:40], 0.5, -0.5, ALU.mult, ALU.add)
                V.tensor_scalar(SM[:, 44:48], SM[:, 36:40], -0.5, 0.5, ALU.mult, ALU.add)
                V.memset(GT[:, :], 1.0)
                V.drain()
                V.tensor_tensor(SM[:, 40:44], SM[:, 40:44], IN[:, :], ALU.mult)
                V.tensor_tensor(SM[:, 44:48], SM[:, 44:48], IN[:, :], ALU.mult)
                V.drain()
                gt9 = GT[:, 0:B * 9].rearrange("p (j e) -> p j e", j=B)
                gt29 = GT2[:, 0:B * 9].rearrange("p (j e) -> p j e", j=B)
                V.tensor_copy(gt9[:, :, 0:E], GA[:, :].rearrange("p (j e) -> p j e", j=B))
                for j in range(B):
                    V.tensor_scalar(GT2[:, j * 9:j * 9 + E], GA[:, j * 8:(j + 1) * 8], SM[:, 44 + j:45 + j], None, ALU.mult)
                V.tensor_scalar(gt29[:, :, E], SM[:, 40:44], 1.0, None, ALU.add)
                V.drain()
                V.tensor_scalar(GE[:, 0:36], GT2[:, 0:36], IS, None, ALU.mult)
                V.tensor_scalar(GA[:, :], GA[:, :], IS, None, ALU.mult)
                done(g_mat)
                slot()
                for h in range(2):
                    filled(k, "g3T", h)
                    V.tensor_copy(GTT[0:9, h * NT:(h + 1) * NT], dbank("g3T", h)[0:9, :]).then_inc(d_free, 1)
                done(gt_copy)

                def views(j):
                    o = (j % 2) * 256
                    return (HB[j % 2][:, :].rearrange("p (v w h) -> p v w h", v=2, w=2),
                            TT[0][:, o:o + 256].rearrange("p (v h) -> p v h", v=2),
                            TT[1][:, o:o + 256].rearrange("p (v h) -> p v h", v=2))

                def gated(j):
                    hv, tv, qv = views(j)
                    dve.wait_ge(hs_tanh, (k - 1) * B + j + 1)
                    V.scalar_tensor_tensor(qv, tv, 1.0, hv[:, :, 0, :], ALU.add, ALU.mult)
                    V.drain()
                    V.scalar_tensor_tensor(qv, qv, 0.5, hv[:, :, 1, :], ALU.mult, ALU.mult)
                    V.drain()
                    for v in range(2):
                        V.bn_stats(ST[:, 6 * v:6 * v + 6], qv[:, v, :])
                    V.drain()
                    for v in range(2):
                        V.bn_aggr(ST[:, 16 + 2 * v:18 + 2 * v], ST[:, 6 * v:6 * v + 6])
                    V.drain()
                    for v in range(2):
                        V.tensor_scalar(SM[:, 16 + 2 * j + v:17 + 2 * j + v], ST[:, 17 + 2 * v:18 + 2 * v], LN_EPS, None, ALU.add)
                    done(p_in)

                def normed(j):
                    _, _, qv = views(j)
                    dve.wait_ge(p_out, plus(k, "pow", "C", 2 + j))
                    for v in range(2):
                        V.tensor_scalar(NTM[:, (v * B + j) * P:(v * B + j + 1) * P], qv[:, v, :], ST[:, 16 + 2 * v:17 + 2 * v],
                                        SM[:, 24 + 2 * j + v:25 + 2 * j + v], ALU.subtract, ALU.mult)

                for j in range(B):
                    hb = HB[j % 2]
                    slot()
                    if j:
                        gated(j - 1)
                    filled(k, "hid3", 6 * j)
                    V.tensor_copy(hb[:, :], dbank("hid3", 6 * j)[:, :]).then_inc(d_free, 1)
                    for w in range(4):
                        if w == 2:
                            slot()
                            if j:
                                normed(j - 1)
                        else:
                            V.drain()
                        filled(k, "hid3", 6 * j + 1 + w)
                        for h in range(2):
                            if h:
                                V.drain()
                            e = 2 * w + h
                            ins = V.scalar_tensor_tensor(hb[:, 0:256], dbank("hid3", 6 * j + 1 + w)[:, h * 256:(h + 1) * 256],
                                                         GA[:, j * E + e:j * E + e + 1], hb[:, 0:256], ALU.mult, ALU.add)
                        ins.then_inc(d_free, 1)
                    filled(k, "hid3", 6 * j + 5)
                    V.scalar_tensor_tensor(hb[:, 256:512], dbank("hid3", 6 * j + 5)[:, 0:256], IS, hb[:, 256:512],
                                           ALU.mult, ALU.add).then_inc(d_free, 1)
                    done(hs_row)
                slot()
                gated(B - 1)
                slot()
                normed(B - 1)
                done(n_row)
                for j in range(B):
                    slot()
                    if j == 0:
                        for v in range(2):
                            z_lo(k, "nT", v)
                    r = RES[:, j * D:(j + 1) * D]
                    filled(k, "out3", 6 * j)
                    V.tensor_tensor(r, dbank("out3", 6 * j)[:, 0:D], r, ALU.add).then_inc(d_free, 1)
                    for w in range(4):
                        V.drain()
                        filled(k, "out3", 6 * j + 1 + w)
                        for h in range(2):
                            if h:
                                V.drain()
                            e = 2 * w + h
                            ins = V.scalar_tensor_tensor(r, dbank("out3", 6 * j + 1 + w)[:, h * D:(h + 1) * D],
                                                         GE[:, j * 9 + e:j * 9 + e + 1], r, ALU.mult, ALU.add)
                        ins.then_inc(d_free, 1)
                    V.drain()
                    filled(k, "out3", 6 * j + 5)
                    V.scalar_tensor_tensor(r, dbank("out3", 6 * j + 5)[:, 0:D], GE[:, j * 9 + E:j * 9 + E + 1], r,
                                           ALU.mult, ALU.add).then_inc(d_free, 1)
                    done(r_row)

            none = Slots(dve, None, 0, V.drain)
            a_part(-1, none)

            slot = Slots(dve, step, 0, V.drain)
            for m in range(0, GC, 4):
                slot()
                xp_half(0, 1, range(m, m + 4))
            slot.bare(1)

            def split_set(q):
                V.drain()
                V.tensor_copy(PG[:, :], at(GAIN, q * UPS, UPS))
                done(pg_ready)
                for u in range(UPS):
                    r = (SETUP_UNITS + u) % RS
                    for half in range(2):
                        slot()
                        dve.wait_ge(e_hi, q * (2 * UPS) + (2 * u + half + 1))
                        o = half * (RU // 2)
                        ins = V.scalar_tensor_tensor(STAGE[u][:, RU + o:RU + o + RU // 2], RAW[r][:, o:o + RU // 2],
                                                     PG[:, u:u + 1], STAGE[u][:, o:o + RU // 2], ALU.mult, ALU.subtract)
                        if half:
                            ins.then_inc(raw_free, 1)

            split_set(0)
            with slot.repeat(1, NEW, 2 * UPS) as q:
                split_set(q)
            slot.bare(BARE0)
            a_part(0, slot)
            with dve.Fori(1, NBLK - 1) as k:
                slot = Slots(dve, step, k, V.drain)
                c_part(k, slot, True)
                a_part(k, slot)
            slot = Slots(dve, step, NBLK - 1, V.drain)
            c_part(NBLK - 1, slot, True)
            slot.bare(TB - C_SLOTS)
            rows_in(NBLK - 1)
            V.drain()
            c_part(NBLK, none, False)

        @block.tensor
        def _(pe):
            def products(dst, terms, start=True, stop=True):
                n = len(terms) * 3
                i = 0
                for (ah_, al_), (bh_, bl_) in terms:
                    for l_, r_ in ((al_, bh_), (ah_, bl_), (ah_, bh_)):
                        ins = PE.matmul(dst, l_, r_, start=start and i == 0, stop=stop and i == n - 1)
                        i += 1
                return ins

            pe.sem_inc(a_free, AB)
            pe.wait_ge(s_gen, 6)
            pe.wait_ge(s_ln, 2)
            for c in range(C):
                ins = PE.transpose(DP[0][:, c * B:(c + 1) * B], LNX[:, c * P:(c + 1) * P], IDF[0:B, 0:B])
            ins.then_inc(s_lnT, 1)
            pe.wait_ge(s_tmpw, 16)
            pe.wait_ge(s_ae, 2 * C)
            for w in range(2):
                for m in range(C):
                    for c in range(C):
                        ins = PE.matmul(DP[1][:, (w * C + m) * B:(w * C + m + 1) * B],
                                        tmp("w1_3" if w else "w1_0", P, c * D + m * P),
                                        HC[:, (w * C + c) * B:(w * C + c + 1) * B], start=c == 0, stop=c == C - 1)
            ins.then_inc(s_hc, 1)
            pe.wait_ge(s_eq, 1)
            for k in range(NBLK):
                for i in range(4):
                    ins = PE.matmul(DP[3][:, k * B:(k + 1) * B], EQT[:, i * T + k * TB:i * T + (k + 1) * TB],
                                    EQB[:, i * B:(i + 1) * B], start=i == 0, stop=i == 3)
            ins.then_inc(s_in, 1)
            for m in range(C):
                for c in range(C):
                    ins = PE.matmul(DP[2][:, m * B:(m + 1) * B], tmp("WhhT", P, c * D + m * P), col("condT", B, c * B),
                                    start=c == 0, stop=c == C - 1)
            ins.then_inc(s_hbt, 1)
            pe.wait_ge(s_h, 2 * C)
            for f in range(F_UNITS // 2):
                which, c = f // C, f % C
                hid = 0 if which < 2 else C
                for half in range(2):
                    n = 2 * f + half
                    pe.wait_ge(raw_in[n % RS], 16 * (n // RS + 1))
                    if n:
                        pe.wait_ge(f_evac, n)
                    rv = RAW[n % RS].rearrange("p (c r d) -> p c r d", c=C, r=4)
                    for r in range(4):
                        for kc in range(C):
                            ins = PE.matmul(DP[0][:, r * B:(r + 1) * B], rv[:, kc, r, :],
                                            HID[:, (hid + kc) * B:(hid + kc + 1) * B], start=kc == 0, stop=kc == C - 1)
                    ins.then_inc(f_fill, 1)
                pe.wait_ge(f_evac, 2 * f + 2)
                if f:
                    pe.wait_ge(ft_evac, f)
                for b in range(B):
                    ins = PE.transpose(DP[1][0:R, b * P:(b + 1) * P], FV[:, b * R:(b + 1) * R], IDF[:, :])
                ins.then_inc(ft_fill, 1)
                if f % 4 == 3:
                    w3 = f // 4
                    pe.wait_ge(ft_evac, f + 1)
                    ftv = FT[:, :].rearrange("r (w b d) -> r w b d", w=2, b=B)
                    for b in range(B):
                        t = w3 * 4 + b
                        if t >= 2:
                            pe.wait_ge(dw_sum, t - 1)
                        for cc in range(C):
                            ins = PE.matmul(DP[2 + t % 2][:, cc * D:(cc + 1) * D], ftv[:, 0, b, cc * P:(cc + 1) * P],
                                            ftv[:, 1, b, :], start=True, stop=True)
                        ins.then_inc(dw_fill, 1)
            pe.wait_ge(dw_lo, 12)
            pe.wait_ge(res_lo, 1)

            def step(k, dyn, s):
                n, g, h = steps(k, dyn, s), GP[s % 2], H16[s % 2]
                PE.matmul(g[:, 0:64], IDH[:, :], at(XP, s * 64 if isinstance(dyn, int) else dyn * 64 + s * 64, 64),
                          start=True, stop=False)

                def wh(hi, c, m):
                    w = WH if hi else WL
                    o = OFF["Wh_ifo"] + c * 768 + m * P if m < 6 else OFF["Wh_g"] + c * 256 + (m - 6) * P
                    return w[:, o:o + P]
                pe.wait_ge(l_hi, n)
                for m in range(GC):
                    for c in range(C):
                        PE.matmul(g[:, m * 8:m * 8 + 4], wh(False, c, m), h[:, c * 8:c * 8 + 4], start=False, stop=False)
                pe.wait_ge(l_lo, n)
                for m in range(GC):
                    for c in range(C):
                        ins = PE.matmul(g[:, m * 8:m * 8 + 8], wh(True, c, m), h[:, c * 8:c * 8 + 8], start=False,
                                        stop=m == GC - 1 and c == C - 1)
                ins.then_inc(l_pe, 1)

            def d_wait(k, stage, i):
                pe.wait_ge(d_free, d_count(k, stage, i))

            def a_wait(k, stage, i):
                pe.wait_ge(a_free, a_count(k, stage, i))

            def all_freed(k, stage, i):
                pe.wait_ge(d_free, d_count(k, stage, i, DB))

            def a_lows(k, stage, i):
                pe.wait_ge(al, a_count(k, stage, i, 2))

            def transposes(k, stage, src):
                for c in range(C):
                    d_wait(k, stage, c)
                    for j in range(B):
                        ins = PE.transpose(dbank(stage, c)[:, j * P:(j + 1) * P],
                                           src[:, j * D + c * P:j * D + (c + 1) * P], IDF[:, :])
                    ins.then_inc(d_fill, 1)

            def gate_transposes(k, stage, i, src, n, js):
                d_wait(k, stage, i)
                for j in js:
                    ins = PE.transpose(dbank(stage, i)[0:n, (j - js[0]) * P:(j - js[0] + 1) * P], src[:, j * n:(j + 1) * n],
                                       IDF[:, :])
                ins.then_inc(d_fill, 1)

            def xp_half(k, half, ms):
                qv = [t[:, :].rearrange("p (c b s) -> p c b s", c=C, b=B) for t in (QH, QL)]
                hs = slice(half * (TB // 2), (half + 1) * (TB // 2))
                for m in ms:
                    a_wait(k, f"xp{half}", m)
                    products(abank(f"xp{half}", m)[:, 0:NT // 2],
                             [(res("Wx", c * GATES + m * P, P), (qv[0][:, c, :, hs], qv[1][:, c, :, hs]))
                              for c in range(C)]).then_inc(a_fill, 1)

            def a_part(k, slot):
                slot()
                pe.wait_ge(x_in, k * 16 + 32)
                transposes(k, "xT", RX)
                all_freed(k, "xT", C - 1)
                for m in range(C):
                    slot()
                    d_wait(k, "y0T", m)
                    for b in range(B):
                        ins = products(dbank("y0T", m)[:, b * TB:(b + 1) * TB],
                                       [(dwp(0, b, c, m * P, P), pair(QH, QL, c * NT + b * TB, TB)) for c in range(C)])
                    ins.then_inc(d_fill, 1)
                all_freed(k, "y0T", C - 1)
                d_wait(k, "log0", 0)
                for j in range(B):
                    ins = products(dbank("log0", 0)[:, j * E:(j + 1) * E],
                                   [(pair(ZH, ZL, c * NT + j * P, P), res("wgate", c * E, E)) for c in range(C)])
                ins.then_inc(d_fill, 1)
                slot()
                pe.wait_ge(g_mat, plus(k, "mat", "A", 1))
                gate_transposes(k, "g0T", 0, GT, E, range(B))

                def h0(j):
                    d_wait(k, "h0", j)
                    products(dbank("h0", j)[:, :],
                             [(pair(ZH, ZL, c * NT + j * P, P), res("Wd", c * 512, 512)) for c in range(C)]).then_inc(d_fill, 1)

                def h0T(j):
                    pe.wait_ge(h_row, plus(k, "hrow", "A", j + 1))
                    d_wait(k, "h0T", j)
                    for m in range(4):
                        ins = PE.transpose(dbank("h0T", j)[:, m * P:(m + 1) * P], HB[j % 2][:, m * P:(m + 1) * P], IDF[:, :])
                    ins.then_inc(d_fill, 1)

                slot()
                h0(0)
                h0(1)
                slot()
                h0T(0)
                h0(2)
                h0T(1)
                h0(3)
                slot()
                h0T(2)
                h0T(3)
                pe.wait_ge(gt_copy, plus(k, "mat", "A", 1))
                for j in range(B):
                    if j == 2:
                        slot()
                    d_wait(k, "out0", j)
                    all_freed(k, "h0T", j)
                    PE.matmul(dbank("out0", j)[:, 0:D], GTT[0:E, j * P:(j + 1) * P], RB[0:E, RBO["bu"]:RBO["bu"] + D],
                              start=True, stop=False)
                    products(dbank("out0", j)[:, 0:D],
                             [(pair(KH, KL, j * 512 + m * P, P), res("Wu", m * D, D)) for m in range(4)],
                             start=False).then_inc(d_fill, 1)
                slot()
                pe.wait_ge(r_row, plus(k, "rrow", "A", B))
                transposes(k, "x1T", RW)
                all_freed(k, "x1T", C - 1)
                for m in range(0, GC, 4):
                    slot()
                    xp_half(k, 0, range(m, m + 4))

            def up_chunk(k, p, par, m):
                if m == 0:
                    pe.wait_ge(w_in[0][par], p * 16 + ((k - 1) * (16 * (NEW // 2)) + 16))
                pe.wait_ge(a_free, base("a", k, "C") + p * (2 * M1) + (par * M1 + m + 1))
                products(abank("up", m)[:, :],
                         [(ew(0, par, c * H1 + m * P, P), pair(QH, QL, c * NT, NT)) for c in range(C)]).then_inc(a_fill, 1)

            def down(k, p, par, j, h):
                if j == 0 and h == 0:
                    pe.wait_ge(w_in[1][par], p * 16 + ((k - 1) * (16 * (NEW // 2)) + 16))
                if j == 0:
                    pe.wait_ge(al, base("a", k, "C") + p * (2 * M1) + (par * M1 + (h + 1) * (M1 // 2) + 2))
                if h == 0:
                    pe.wait_ge(d_free, base("d", k, "C") + p * (2 * B) + (PLACE["d", "down"][1] + par * B + j + 1))
                ins = products(dbank("down", j)[:, 0:D],
                               [(pair(GH[par], GL[par], m * NT + j * P, P), ew(1, par, m * D, D))
                                for m in range(h * (M1 // 2), (h + 1) * (M1 // 2))], start=h == 0, stop=h == 1)
                if h:
                    ins.then_inc(d_fill, 1)

            def set_in(k, par):
                for half in range(2):
                    pe.wait_ge(w_in[half][par], k * (16 * (NEW // 2)))

            def c_part(k, slot, x):
                pe.wait_ge(l_copy, k * TB + 2)
                for j in range(B):
                    d_wait(k, "log1", j)
                    for c in range(C):
                        ins = PE.matmul(dbank("log1", j)[:, 0:E], HT[:, c * NT + j * P:c * NT + (j + 1) * P],
                                        CENT[:, c * E:(c + 1) * E], start=c == 0, stop=c == C - 1)
                    ins.then_inc(d_fill, 1)
                for j in range(B):
                    d_wait(k, "uT", j)
                    for c in range(C):
                        ins = PE.transpose(dbank("uT", j)[:, c * P:(c + 1) * P], HT[:, c * NT + j * P:c * NT + (j + 1) * P],
                                           IDF[:, :])
                    ins.then_inc(d_fill, 1)
                if x:
                    pe.wait_ge(al, base("a", k, "X") + 2)
                    for m in range(0, GC, 4):
                        slot()
                        xp_half(k, 1, range(m, m + 4))
                slot()
                slot()
                pe.wait_ge(xn_row, k)
                transposes(k, "xnT", UT)
                slot()
                pe.wait_ge(g_mat, plus(k, "mat", "C", 1))
                for h in range(2):
                    gate_transposes(k, "g1T", h, GT, NE1, range(2 * h, 2 * h + 2))
                slot()
                pe.wait_ge(gt_copy, plus(k, "mat", "C", 1))
                for j in range(B):
                    d_wait(k, "bias1", j)
                    PE.matmul(dbank("bias1", j)[:, 0:D], GTT[0:NE1, j * P:(j + 1) * P], RB[0:NE1, RBO["b2"]:RBO["b2"] + D],
                              start=True, stop=True).then_inc(d_fill, 1)
                all_freed(k, "xnT", C - 1)
                for m in range(M1):
                    if m % 2 == 0:
                        slot()
                    up_chunk(k, 0, 0, m)
                with slot.repeat(0, 4, 2 * M1) as p:
                    for par in range(2):
                        for i in range(M1):
                            slot()
                            up_chunk(k, p + par, 1 - par, i)
                            down(k, p, par, i // 2, i % 2)
                for i in range(M1):
                    slot()
                    up_chunk(k, 4, 1, i)
                    down(k, 4, 0, i // 2, i % 2)
                for j in range(B):
                    slot()
                    down(k, 4, 1, j, 0)
                    down(k, 4, 1, j, 1)

                for m in range(C):
                    slot()
                    if m == 0:
                        pe.wait_ge(r_row, plus(k, "rrow", "C", B))
                        transposes(k, "x2T", RES)
                        all_freed(k, "x2T", C - 1)
                    a_wait(k, "z2", m)
                    products(abank("z2", m)[:, :],
                             [(res("Wih", c * D + m * P, P), pair(QH, QL, c * NT, NT)) for c in range(C)]).then_inc(a_fill, 1)
                a_lows(k, "z2", C - 1)
                d_wait(k, "log2", 0)
                for j in range(B):
                    ins = products(dbank("log2", 0)[:, j * E:(j + 1) * E],
                                   [(pair(ZH, ZL, c * NT + j * P, P), res("gatew", c * E, E)) for c in range(C)])
                ins.then_inc(d_fill, 1)
                slot()
                pe.wait_ge(g_mat, plus(k, "mat", "C", 2))
                for h in range(2):
                    gate_transposes(k, "g2T", h, GT, E, range(2 * h, 2 * h + 2))
                slot()
                pe.wait_ge(gt_copy, plus(k, "mat", "C", 2))
                for j in range(B):
                    d_wait(k, "bias2", j)
                    PE.matmul(dbank("bias2", j)[:, 0:D], GTT[0:E, j * P:(j + 1) * P], RB[0:E, RBO["eb"]:RBO["eb"] + D],
                              start=True, stop=True).then_inc(d_fill, 1)
                set_in(k, 0)
                for j in range(B):
                    for w in range(4):
                        if w % 2 == 0:
                            slot()
                        d_wait(k, "exp2", j * 4 + w)
                        products(dbank("exp2", j * 4 + w)[:, :],
                                 [(pair(ZH, ZL, c * NT + j * P, P), ew(c, 0, w * 512, 512))
                                  for c in range(C)]).then_inc(d_fill, 1)

                for m in range(C):
                    slot()
                    if m == 0:
                        pe.wait_ge(r_row, plus(k, "rrow", "C", 2 * B))
                        transposes(k, "x3T", RES)
                        all_freed(k, "x3T", C - 1)
                    a_wait(k, "mid", m)
                    for b in range(B):
                        ins = products(abank("mid", m)[:, b * TB:(b + 1) * TB],
                                       [(dwp(1, b, c, m * P, P), pair(QH, QL, c * NT + b * TB, TB)) for c in range(C)])
                    ins.then_inc(a_fill, 1)
                slot()
                a_lows(k, "mid", C - 1)
                for m in range(C):
                    d_wait(k, "y3T", m)
                    for b in range(B):
                        ins = products(dbank("y3T", m)[:, b * TB:(b + 1) * TB],
                                       [(dwp(2, b, c, m * P, P), pair(ZH, ZL, c * NT + b * TB, TB)) for c in range(C)])
                    ins.then_inc(d_fill, 1)
                slot()
                pe.wait_ge(yl, k * C)
                d_wait(k, "log3", 0)
                for j in range(B):
                    ins = products(dbank("log3", 0)[:, j * 9:(j + 1) * 9],
                                   [(pair(QH, QL, c * NT + j * P, P), res("egsg", c * 9, 9)) for c in range(C)])
                ins.then_inc(d_fill, 1)
                slot()
                pe.wait_ge(g_mat, plus(k, "mat", "C", 3))
                gate_transposes(k, "g3T", 0, GT, 9, range(B))
                gate_transposes(k, "g3T", 1, GT2, 9, range(B))
                for j in range(B):
                    slot()
                    if j == 0:
                        pe.wait_ge(gt_copy, plus(k, "mat", "C", 3))
                        set_in(k, 1)
                    d_wait(k, "hid3", 6 * j)
                    PE.matmul(dbank("hid3", 6 * j)[:, :], GTT[0:9, j * P:(j + 1) * P], RB[0:9, RBO["eb12"]:RBO["eb12"] + 512],
                              start=True, stop=True).then_inc(d_fill, 1)
                    for w in range(4):
                        if w == 2:
                            slot()
                        d_wait(k, "hid3", 6 * j + 1 + w)
                        products(dbank("hid3", 6 * j + 1 + w)[:, :],
                                 [(pair(QH, QL, c * NT + j * P, P), ew(c, 1, w * 512, 512))
                                  for c in range(C)]).then_inc(d_fill, 1)
                    d_wait(k, "hid3", 6 * j + 5)
                    products(dbank("hid3", 6 * j + 5)[:, 0:256],
                             [(pair(QH, QL, c * NT + j * P, P), res("sw12", c * D, D)) for c in range(C)]).then_inc(d_fill, 1)
                slot()
                slot()
                pe.wait_ge(n_row, k)
                for v in range(2):
                    a_wait(k, "nT", v)
                    for j in range(B):
                        ins = PE.transpose(abank("nT", v)[:, j * P:(j + 1) * P], NTM[:, (v * B + j) * P:(v * B + j + 1) * P],
                                           IDF[:, :])
                    ins.then_inc(a_fill, 1)
                for j in range(B):
                    slot()
                    d_wait(k, "out3", 6 * j)
                    PE.matmul(dbank("out3", 6 * j)[:, 0:D], GTT[0:9, NT + j * P:NT + (j + 1) * P],
                              RB[0:9, RBO["b3"]:RBO["b3"] + D], start=True, stop=True).then_inc(d_fill, 1)
                    if j == 0:
                        a_lows(k, "nT", 1)
                    for w in range(4):
                        d_wait(k, "out3", 6 * j + 1 + w)
                        products(dbank("out3", 6 * j + 1 + w)[:, :],
                                 [(pair(ZH, ZL, j * P, P), res("ew3", w * 512, 512))]).then_inc(d_fill, 1)
                    d_wait(k, "out3", 6 * j + 5)
                    products(dbank("out3", 6 * j + 5)[:, 0:D],
                             [(pair(ZH, ZL, NT + j * P, P), res("sw3", 0, D))]).then_inc(d_fill, 1)

            none = Slots(pe, None, 0)
            a_part(-1, none)
            pe.wait_ge(al, base("a", 0, "X") + 2)
            slot = Slots(pe, step, 0)
            for m in range(0, GC, 4):
                slot()
                xp_half(0, 1, range(m, m + 4))
            slot.bare(1)
            pe.wait_ge(al, base("a", 0, "A") + 2)
            pe.sem_inc(s_mark, 1)
            slot.bare(NEW * 2 * UPS)
            slot.bare(BARE0)
            a_part(0, slot)
            with pe.Fori(1, NBLK - 1) as k:
                slot = Slots(pe, step, k)
                c_part(k, slot, True)
                a_part(k, slot)
            slot = Slots(pe, step, NBLK - 1)
            c_part(NBLK - 1, slot, True)
            slot.bare(TB - C_SLOTS)
            c_part(NBLK, none, False)


def host_layout(i):
    import numpy as np
    g = {k: np.asarray(v) for k, v in i.items()}

    def chunked(w):
        k, n = w.shape
        return w.reshape(k // P, P, n).transpose(1, 0, 2).reshape(P, -1)

    def column(v):
        return v.reshape(-1, P).T

    def factor(w, b):
        w = w.reshape(C, P, C, P, 2, R // 2).transpose(2, 4, 1, 0, 5, 3)
        return w.reshape(C * 2, P, RU), b.reshape(C, P, R).transpose(1, 0, 2).reshape(P, C * R)

    n = D * R
    w0, b0 = g["L0_cond_w2"], g["L0_cond_b2"]
    w3, b3 = g["L3_cond_W2"], g["L3_cond_bias2"]
    facts = [factor(w0[:, s * n:(s + 1) * n], b0[s * n:(s + 1) * n]) for s in (0, 1)]
    facts += [factor(w3[:, s * n:(s + 1) * n], b3[s * n:(s + 1) * n]) for s in (2, 3, 1, 0)]

    wh = g["L1_cond_Wh"]
    ew3 = g["L3_ffn_ew3"].transpose(2, 0, 1).reshape(P, E * D)
    egsg = np.concatenate([g["L3_ffn_eg_w"], g["L3_ffn_sg_w"]], 0).T
    resident = {
        "Wh_ifo": chunked(wh[:, 0:768]), "Wh_g": chunked(wh[:, 768:1024]), "Wx": chunked(g["L1_cond_Wx"]), "ew3": ew3,
        "Wd": chunked(g["L0_ffn_Wd"].transpose(1, 0, 2).reshape(D, 512)),
        "Wu": chunked(g["L0_ffn_Wu"].reshape(512, D)), "Wih": chunked(g["L2_cond_W_ih"].T),
        "sw12": chunked(np.concatenate([g["L3_ffn_sw1"].T, g["L3_ffn_sw2"].T], 1)), "sw3": g["L3_ffn_sw3"].T,
        "wgate": chunked(g["L0_ffn_w_gate"]), "gatew": chunked(g["L2_ffn_gate_w"].T), "egsg": chunked(egsg),
    }
    w1 = np.concatenate([g["L1_ffn_W1_s"], g["L1_ffn_W1_r"]], 0)
    w2 = np.concatenate([g["L1_ffn_W2_s"], g["L1_ffn_W2_r"]], 0)
    sets = [np.concatenate([chunked(w1[e]), chunked(w2[e])], 1) for e in range(NE1)]
    sets.append(chunked(g["L2_ffn_expert_w"].transpose(1, 0, 2).reshape(D, E * D)))
    ew12 = np.concatenate([g["L3_ffn_ew1"].transpose(0, 2, 1), g["L3_ffn_ew2"].transpose(0, 2, 1)], 2)
    sets.append(chunked(ew12.transpose(1, 0, 2).reshape(D, E * D)))
    gains = [g["L1_ffn_g_shared"]] * 2 + [g["L1_ffn_g_routed"]] * 8
    b1 = np.concatenate([g["L1_ffn_b1_s"], g["L1_ffn_b1_r"]], 0)
    ones = np.ones((P, UPS), np.float32)
    gain = [np.concatenate([column(gains[e]), ones[:, C:]], 1) for e in range(NE1)] + [ones] * (NEW - NE1)
    cols = {"lstm_b": column(g["L1_cond_b"]), "g0": column(g["L0_cond_ln_g"]), "be0": column(g["L0_cond_ln_b"]),
            "b1_0": column(g["L0_cond_b1"]), "g3": column(g["L3_cond_ln_gamma"]), "be3": column(g["L3_cond_ln_beta"]),
            "b1_3": column(g["L3_cond_bias1"]), "bih": column(g["L2_cond_b_ih"]), "bhh": column(g["L2_cond_b_hh"]),
            "s_g": column(g["L3_ffn_s_ln_g"]), "s_b": column(g["L3_ffn_s_ln_b"]), "sel_g": column(g["L3_ffn_sel_ln_g"]),
            "sel_b": column(g["L3_ffn_sel_ln_b"]), "fb": np.concatenate([b for _, b in facts], 1),
            "condT": chunked(g["cond_1024"].T)}
    rows = {"bd": g["L0_ffn_bd"].reshape(-1), "gate_b": g["L2_ffn_gate_b"],
            "egsg_b": np.concatenate([g["L3_ffn_eg_b"], g["L3_ffn_sg_b"]]), "exp_bias": g["L3_ffn_exp_bias"]}
    tmpw = {"w1_0": chunked(g["L0_cond_w1"]), "w1_3": chunked(g["L3_cond_W1"]), "base0": chunked(g["L0_cond_base_layer"]),
            "base_down": chunked(g["L3_cond_base_down"]), "base_upT": chunked(g["L3_cond_base_up"].T),
            "WhhT": chunked(g["L2_cond_W_hh"].T), "cent": chunked(g["L1_ffn_centroids"])}
    rb = np.zeros((16, 1536), np.float32)
    rb[0:E, 0:256] = g["L0_ffn_bu"]
    rb[0:2, 256:512] = g["L1_ffn_b2_s"]
    rb[2:NE1, 256:512] = g["L1_ffn_b2_r"]
    rb[0:E, 512:768] = g["L2_ffn_expert_b"]
    rb[0:E, 768:896] = g["L3_ffn_eb1"]
    rb[0:E, 896:1024] = g["L3_ffn_eb2"]
    rb[E, 1024:1152] = g["L3_ffn_sb1"]
    rb[E, 1152:1280] = g["L3_ffn_sb2"]
    rb[0:E, 1280:1536] = g["L3_ffn_eb3"]
    rb[E, 1280:1536] = g["L3_ffn_sb3"]
    idx = np.concatenate([g["L3_ffn_index_b"].reshape(4, P).T, g["L3_ffn_index_t"].reshape(4, P).T], 1)
    made = {
        "x": g["x"], "cond": g["cond_1024"],
        "factors": np.concatenate([w for w, _ in facts], 0),
        "resident": np.concatenate([resident[name] for name, _ in RESIDENT], 1),
        "stream": np.stack(sets), "b1": np.concatenate([column(v) for v in b1], 1),
        "gain": np.concatenate(gain, 1),
        "cols": np.concatenate([cols[name] for name, w in COLS if w], 1),
        "rows": np.broadcast_to(np.concatenate([rows[name] for name, _ in ROWS])[None], (P, NROWS)),
        "tmpw": np.concatenate([tmpw[name] for name, _ in TMPW], 1),
        "rb": rb, "idx": idx,
    }
    return {k: np.ascontiguousarray(v) for k, v in made.items()}


def build(nc, arrays):
    a = {k: nc.dram_tensor(f"in_{k}", v.shape, mybir.dt.from_np(v.dtype), kind="ExternalInput").ap()
         for k, v in arrays.items()}
    out = nc.dram_tensor("out_0", (B, T, D), F32, kind="ExternalOutput").ap()
    split = nc.dram_tensor("split_weights", (NEW, 2, P, 2 * HW), F16, kind="Internal").ap()
    adaln_lstm_moe(nc, a, out, split)


def kernel(**inputs):
    import concourse.bacc as bacc
    from concourse.bass_utils import run_bass_kernel_spmd

    nc = bacc.Bacc("TRN2", target_bir_lowering=False, num_devices=1)
    arrays = host_layout(inputs)
    build(nc, arrays)
    r = run_bass_kernel_spmd(nc, [{f"in_{k}": v for k, v in arrays.items()}], core_ids=[0])
    return r.results[0]["out_0"]
```

```python
from contextlib import ExitStack, contextmanager

import concourse.bass as bass
from concourse import mybir

F32 = mybir.dt.float32
F16 = mybir.dt.float16
I32 = mybir.dt.int32
U32 = mybir.dt.uint32
ALU = mybir.AluOpType
ACT = mybir.ActivationFunctionType
AX = mybir.AxisListType

P = 128
B = 4
T = 512
D = 256
C = D // P
TB = 128
NBLK = T // TB
NT = B * TB
E = 8
R = 8
H1 = 1024
M1 = H1 // P
NE1 = 10
NEW = NE1 + 2
HW = 2 * H1
RU = 1024
RS = 4
UPS = 4
GATES = 4 * D
GC = GATES // P
S = 64.0
IS = 1.0 / S
LN_EPS = 1e-5
RMS_EPS = 1.1920928955078125e-07

RESIDENT = [("Wh_ifo", C * 768), ("Wh_g", C * 256), ("Wx", C * GATES), ("ew3", E * D), ("Wd", C * 512),
            ("Wu", 4 * D), ("Wih", C * D), ("sw12", C * D), ("sw3", D), ("wgate", C * E), ("gatew", C * E),
            ("egsg", C * (E + 1))]
OFF = {}
_at = 0
for _n, _w in RESIDENT:
    OFF[_n] = _at
    _at += _w
RES_COLS = _at
RES_UNITS = [(a, min(RU, 1536 - a), S / 2) for a in range(0, 1536, RU)] + \
            [(a, min(RU, RES_COLS - a), S) for a in range(1536, RES_COLS, RU)]
NFACT = 6
F_UNITS = NFACT * C * 2
SETUP_UNITS = F_UNITS + len(RES_UNITS)

COLS = [("lstm_b", GC), ("g0", C), ("be0", C), ("b1_0", C), ("g3", C), ("be3", C), ("b1_3", C), ("bih", C), ("bhh", C),
        ("s_g", 1), ("s_b", 1), ("sel_g", 1), ("sel_b", 1), ("condT", C * B), ("idx_b", 0)]
ROWS = [("bd", 512), ("gate_b", E), ("egsg_b", E + 1), ("exp_bias", E)]
TMPW = [("w1_0", C * D), ("w1_3", C * D), ("base0", C * D), ("base_down", C * D), ("base_upT", C * D), ("WhhT", C * D),
        ("cent", C * E)]


def offsets(table):
    at, out = 0, {}
    for name, n in table:
        out[name] = at
        at += n
    return out, at


CO, NCOLS = offsets(COLS)
RO, NROWS = offsets(ROWS)
TO, NTMP = offsets(TMPW)


D_A = [("xT", 2), ("y0T", 2), ("log0", 1), ("g0T", 1), ("h0", 8), ("out0", 4), ("x1T", 2)]
D_C = [("log1", 4), ("uT", 4), ("xnT", 2), ("g1T", 2), ("bias1", 4), ("down", NE1 * 4), ("x2T", 2), ("log2", 1),
       ("g2T", 2), ("bias2", 4), ("exp2", 16), ("x3T", 2), ("y3T", 2), ("log3", 1), ("g3T", 2), ("hid3", 24),
       ("out3", 24)]
A_A, A_X = [("xp0", GC)], [("xp1", GC)]
A_C = [("up", NE1 * M1), ("z2", 2), ("mid", 2), ("nT", 2)]
H_A = [("xT", 2), ("y0T", 2), ("h0T", 4), ("x1T", 2)]
H_C = [("xnT", 2), ("x2T", 2), ("x3T", 2)]

H0_AT, H0T_AT = (0, 1, 3, 5), (2, 4, 6, 7)
PLACE = {}
SIZE = {}
for _name, _x, _c, _a in (("d", [], D_C, D_A), ("a", A_X, A_C, A_A), ("h", [], H_C, H_A)):
    SIZE[_name] = []
    for _part, _table in (("X", _x), ("C", _c), ("A", _a)):
        _off, _n = offsets(_table)
        SIZE[_name].append(_n)
        for _stage, _o in _off.items():
            PLACE[_name, _stage] = (_part, _o)
DB, AB = 4, 2
assert all(n % DB == 0 for n in SIZE["d"]) and all(n % AB == 0 for n in SIZE["a"])
SIZE.update(diff=(0, 4, 1), mat=(0, 3, 1), rrow=(0, 4, 4), gated=(0, 48, 0), hrow=(0, 0, 4), pow=(0, 5, 0), b1=(0, NE1, 0))


def base(name, k, part):
    x, c, a = SIZE[name]
    if isinstance(k, int) and k < 1:
        return 0 if k < 0 else a + (x if part == "A" else 0)
    off = {"X": 0, "C": x, "A": x + c}[part] + (2 * a + x) - (x + c + a)
    if isinstance(k, int) and k == NBLK:
        off -= a + x
    return k * (x + c + a) + off


def plus(k, name, part, n):
    if isinstance(k, int):
        return base(name, k, part) + n
    x, c, a = SIZE[name]
    return k * (x + c + a) + ({"X": 0, "C": x, "A": x + c}[part] + (2 * a + x) - (x + c + a) + n)


def place(stage, i):
    if stage == "h0":
        return "A", PLACE["d", "h0"][1] + H0_AT[i]
    if stage == "h0T":
        return "A", PLACE["d", "h0"][1] + H0T_AT[i]
    part, o = PLACE["d", stage]
    return part, o + i


def d_count(k, stage, i, n=0):
    part, o = place(stage, i)
    return plus(k, "d", part, o + 1 + n)


def a_count(k, stage, i, n=0):
    part, o = PLACE["a", stage]
    return plus(k, "a", part, o + i + 1 + n)


def h_count(k, stage, i):
    part, o = PLACE["h", stage]
    return plus(k, "h", part, o + i + 1)


def gated_fill(x):
    stage, i = (("exp2", x), ("hid3", x - 16), ("out3", x - 32))[x // 16]
    return stage, i if stage == "exp2" else 6 * (i // 4) + 2 + i % 4


def gated_count(k, x, n=0):
    return plus(k, "gated", "C", x + 1 + n)


class Slots:

    def __init__(self, eng, step, block, always=None):
        self.eng, self.step, self.block, self.always = eng, step, block, always
        self.dyn, self.s = 0, 0

    def __call__(self):
        if self.step is not None:
            self.step(self.block, self.dyn, self.s)
        if self.always is not None:
            self.always()
        self.s += 1

    @contextmanager
    def repeat(self, lo, hi, width):
        start = self.s
        with self.eng.Fori(lo, hi) as r:
            self.dyn, self.s = r * width, start - lo * width
            yield r
        self.dyn, self.s = 0, start + (hi - lo) * width

    def bare(self, n):
        if self.step is not None:
            if n > 1:
                with self.repeat(0, n // 2, 2):
                    self()
                    self()
            if n % 2:
                self()


F_GROUP = 4 * C
F_SLOTS = (2, 2, 2, 2, 2, 1, 1, 1, 1, 1, 1)
assert F_GROUP + sum(F_SLOTS) == F_UNITS
DW0_AT = 4
BARE0 = TB - 3 - 2 * B - NEW * 2 * UPS - 11
C_SLOTS = 117
assert C_SLOTS + 11 == TB


def adaln_lstm_moe(nc, a, out, split, turn):
    with ExitStack() as ctx:
        def sb(name, shape, dt=F32):
            return ctx.enter_context(nc.sbuf_tensor(name, shape, dt))

        def sem(name):
            return ctx.enter_context(nc.semaphore(name))

        WH, WL = sb("WH", [P, RES_COLS], F16), sb("WL", [P, RES_COLS], F16)
        EW = [[sb(f"EW{h}{i}", [P, 2 * HW], F16) for i in range(2)] for h in range(2)]
        GH = [sb(f"GH{i}", [P, M1 * NT], F16) for i in range(2)]
        GL = [sb(f"GL{i}", [P, M1 * NT], F16) for i in range(2)]
        RAW = [t[:, :].bitcast(F32)[:, h * RU:(h + 1) * RU] for t in (GH[0], GL[0]) for h in range(2)]
        STAGE = [t[:, h * 2 * RU:(h + 1) * 2 * RU] for t in (GH[1], GL[1]) for h in range(2)]
        KH, KL = GH[1][:, 0:4 * 4 * P], GH[1][:, 4 * 4 * P:8 * 4 * P]
        JUNK = GH[0][:, :].bitcast(F32)
        EQT, EQB = GL[1][:, 0:4 * T], sb("EQB", [P, 4 * B], F16)
        B1 = sb("B1", [P, NE1 * M1])
        B1CUR = [sb(f"B1CUR{i}", [P, M1]) for i in range(2)]
        GAIN = sb("GAIN", [P, NEW * UPS])
        PG = sb("PG", [P, UPS])
        DWH = sb("DWH", [P, 3 * C * B * D], F16)
        DWL = sb("DWL", [P, 3 * C * B * D], F16)
        XP = sb("XP", [P, TB * GC * 2 * B], F16)
        TMP = XP[:, :].bitcast(F32)
        QH, QL = sb("QH", [P, C * NT], F16), sb("QL", [P, C * NT], F16)
        ZH, ZL = sb("ZH", [P, C * NT], F16), sb("ZL", [P, C * NT], F16)
        RX = sb("RX", [P, B * D])
        RW = sb("RW", [P, B * D])
        RES = sb("RES", [P, B * D])
        HT = sb("HT", [P, C * NT])
        UT = sb("UT", [P, B * D])
        YF = sb("YF", [P, C * NT])
        TT = [sb(f"TT{i}", [P, NT]) for i in range(2)]
        HB = [sb(f"HB{i}", [P, 512]) for i in range(2)]
        GS = [sb(f"GS{i}", [P, D]) for i in range(2)]
        GP2 = [sb(f"GP2{i}", [P, D]) for i in range(4)]
        COL = sb("COL", [P, NCOLS])
        ROW = sb("ROW", [P, NROWS])
        RB = sb("RB", [16, 1536])
        GTT = sb("GTT", [16, 2 * NT])
        CENT = sb("CENT", [P, C * E])
        IDF, IDH = sb("IDF", [P, P]), sb("IDH", [P, P], F16)
        IOTA = sb("IOTA", [P, T])
        INSET = sb("INSET", [P, NBLK * B])
        IN = sb("IN", [P, B])
        IDXI = sb("IDXI", [P, 8], I32)
        IDXF, IDXG = sb("IDXF", [P, 8]), sb("IDXG", [P, 8])
        LB0 = sb("LB0", [P, GC])
        HBT = sb("HBT", [P, C * B])
        L = sb("L", [P, B * 9])
        SC = sb("SC", [P, B * 9])
        SB_ = sb("SB_", [P, B * E])
        MX = sb("MX", [P, B * 8])
        IX = sb("IX", [P, B * 8], U32)
        IXF = sb("IXF", [P, B * 8])
        GA = sb("GA", [P, B * 8])
        GT = sb("GT", [P, B * NE1])
        GT2 = sb("GT2", [P, B * NE1])
        GE = sb("GE", [P, NE1 * B])
        GCUR = [sb(f"GCUR{i}", [P, B]) for i in range(2)]
        SM = sb("SM", [P, 64])
        ST = sb("ST", [P, 64])
        PW = sb("PW", [P, 8])
        NTM = UT
        LNX = sb("LNX", [B, D])
        HID = sb("HID", [P, 2 * C * B])
        FO = [EW[h][i][0:B, :].bitcast(F32) for h, i in ((0, 0), (0, 1), (1, 0))]
        FT = [t[0:R, :].bitcast(F32) for t in (GL[1], GL[1], EW[1][1])]
        FB = [t[0:R, 0:NFACT * D // 2] for t in (UT, YF)]
        HC = sb("HC", [P, 2 * C * B])
        PRE = sb("PRE", [P, GC * B])
        TG = sb("TG", [P, (GC + C) * B])
        WK = sb("WK", [P, 2 * C * B])
        DC = sb("DC", [P, C * B])
        TC = sb("TC", [P, C * B])
        HF = [sb(f"HF{i}", [P, C * B]) for i in range(2)]
        H16 = [sb(f"H16{i}", [P, C * 2 * B], F16) for i in range(2)]

        DP = [ctx.enter_context(nc.psum_tensor(f"DP{i}", [P, 512], F32)) for i in range(DB)]
        AP_ = [ctx.enter_context(nc.psum_tensor(f"AP{i}", [P, 512], F32)) for i in range(AB)]
        GP = [ctx.enter_context(nc.psum_tensor(f"GP{i}", [P, 512], F32)) for i in range(2)]

        s_const = sem("s_const")
        s_tmpw = sem("s_tmpw")
        s_idx = sem("s_idx")
        s_gen = sem("s_gen")
        raw_in = [sem(f"raw_in{i}") for i in range(RS)]
        raw_free = sem("raw_free")
        w_hi = sem("w_hi")
        e_hi = sem("e_hi")
        pg_ready = sem("pg_ready")
        split_out = [sem(f"split_out{i}") for i in range(RS)]
        w_in = [[sem(f"w_in{h}{i}") for i in range(2)] for h in range(2)]
        b1_ready = sem("b1_ready")
        res_lo = sem("res_lo")
        f_fill, f_evac, f_out, f_in, f_bias = (sem(n) for n in ("f_fill", "f_evac", "f_out", "f_in", "f_bias"))
        dw_fill, dw_sum, dw_hi, dw_lo = sem("dw_fill"), sem("dw_sum"), sem("dw_hi"), sem("dw_lo")
        s_ln, s_lnp, s_lnT, s_ae, s_hc, s_h = (sem(n) for n in ("s_ln", "s_lnp", "s_lnT", "s_ae", "s_hc", "s_h"))
        s_eq, s_in, s_hbt = (sem(n) for n in ("s_eq", "s_in", "s_hbt"))
        d_fill, d_free = sem("d_fill"), sem("d_free")
        a_fill, a_free = sem("a_fill"), sem("a_free")
        dh, ah, al = sem("dh"), sem("ah"), sem("al")
        x_in = sem("x_in")
        s_mark = sem("s_mark")
        st_out = sem("st_out")
        g_diff, g_tanh = sem("g_diff"), sem("g_tanh")
        g_mat, gt_copy = sem("g_mat"), sem("gt_copy")
        r_row = sem("r_row")
        h_row = sem("h_row")
        p_in, p_out = sem("p_in"), sem("p_out")
        half_in = sem("half_in")
        pair_add = sem("pair_add")
        sq = sem("sq")
        xn_row = sem("xn_row")
        x3f = sem("x3f")
        yf, yh, yl = sem("yf"), sem("yh"), sem("yl")
        hs_tanh, n_row = sem("hs_tanh"), sem("n_row")
        l_pe, l_pre, l_tg, l_w, l_d, l_c, l_tc, l_hi, l_h, l_lo, l_copy = (
            sem(n) for n in ("l_pe", "l_pre", "l_tg", "l_w", "l_d", "l_c", "l_tc", "l_hi", "l_h", "l_lo", "l_copy"))

        V, A_, PE, G = nc.vector, nc.scalar, nc.tensor, nc.gpsimd
        block = ctx.enter_context(nc.Block())

        def col(name, n=1, i=0):
            return COL[:, CO[name] + i:CO[name] + i + n]

        def row(name, n):
            return ROW[:, RO[name]:RO[name] + n]

        def tmp(name, n, i=0):
            return TMP[:, TO[name] + i:TO[name] + i + n]

        def res(name, at, n):
            o = OFF[name] + at
            return WH[:, o:o + n], WL[:, o:o + n]

        def pair(hi, lo, at, n):
            return hi[:, at:at + n], lo[:, at:at + n]

        def ew(half, par, at, n):
            t = EW[half][par]
            return t[:, at:at + n], t[:, HW + at:HW + at + n]

        def dwp(which, b, c, at, n):
            o = ((which * B + b) * C + c) * D + at
            return DWH[:, o:o + n], DWL[:, o:o + n]

        def dbank(stage, i):
            return DP[place(stage, i)[1] % DB]

        def abank(stage, i):
            return AP_[(PLACE["a", stage][1] + i) % AB]

        def at(t, start, n):
            return t[:, start:start + n] if isinstance(start, int) else t[:, bass.ds(start, n)]

        def xp_pair(half):
            v = XP[:, :].rearrange("p (s q b) -> p b s q", q=2 * GC, b=B)
            return v[:, :, half * (TB // 2):(half + 1) * (TB // 2), :]

        def steps(k, dyn, s, n=1):
            return k * TB + (s + n) if isinstance(dyn, int) else k * TB + dyn + (s + n) if not isinstance(k, int) \
                else dyn + (k * TB + s + n)

        def res_unit(i):
            return F_GROUP + i

        def f_unit(f):
            return f if f < F_GROUP else f + len(RES_UNITS)

        RBO = {"bu": 0, "b2": 256, "eb": 512, "eb12": 768, "b3": 1280}

        @block.sync
        def _(sp):
            for dst, src in ((COL[:, :], a["cols"]), (ROW[:, :], a["rows"]), (RB[:, :], a["rb"]), (B1[:, :], a["b1"]),
                             (GAIN[:, :], a["gain"]), (CENT[:, :], a["tmpw"][:, TO["cent"]:TO["cent"] + C * E])):
                sp.dma_start(dst, src).then_inc(s_const, 16)
            sp.dma_start(LNX[:, :], a["cond"]).then_inc(s_const, 16)
            for i in range(2):
                sp.dma_start(FB[i], a["factor_bias"][:, i * NFACT * D // 2:(i + 1) * NFACT * D // 2]).then_inc(s_const, 16)
            sp.dma_start(TMP[:, 0:NTMP], a["tmpw"]).then_inc(s_tmpw, 16)
            sp.dma_start(RES[:, 0:2 * C * D], a["tmpw"][:, TO["base_down"]:TO["base_down"] + 2 * C * D]).then_inc(s_tmpw, 16)
            sp.dma_start(IDXI[:, :], a["idx"]).then_inc(s_idx, 16)

            def load(n, slot, src, width):
                sp.wait_ge(raw_free, n + 1)
                sp.dma_start(RAW[slot][:, 0:width], src).then_inc(raw_in[slot], 16)

            for f in range(F_GROUP):
                load(f, f % RS, a["factors"][f], RU)
            for i, (o, w, _) in enumerate(RES_UNITS):
                load(res_unit(i), res_unit(i) % RS, a["resident"][:, o:o + w], w)
            for f in range(F_GROUP, F_UNITS):
                load(f_unit(f), f_unit(f) % RS, a["factors"][f], RU)
            n = SETUP_UNITS

            def store(u, dst):
                sp.dma_start(dst.rearrange("p (v c) -> p v c", v=2)[:, :, (u % 2) * RU:(u % 2 + 1) * RU],
                             STAGE[u].rearrange("p (v c) -> p v c", v=2)).then_inc(split_out[u], 16)

            for u in range(UPS):
                load(n + u, (n + u) % RS, a["stream"][0, :, u * RU:(u + 1) * RU], RU)
            with sp.Fori(1, NEW) as q:
                for u in range(UPS):
                    load(q * UPS + (n + u), (n + u) % RS,
                         a["stream"][bass.ds(q, 1), :, u * RU:(u + 1) * RU].squeeze(0), RU)
                    store(u, split[bass.ds(q - 1, 1), u // 2].squeeze(0))
            for u in range(UPS):
                sp.wait_ge(raw_free, n + NEW * UPS + u + 1)
                store(u, split[NEW - 1, u // 2])
            for u in range(UPS):
                sp.wait_ge(split_out[u], 16 * NEW)

            def half_set(e, half, par):
                src = split[e, half] if isinstance(e, int) else split[bass.ds(e, 1), half].squeeze(0)
                sp.dma_start(EW[half][par][:, :], src).then_inc(w_in[half][par], 16)

            for e in range(2):
                for half in range(2):
                    half_set(e, half, e)

            def sets(k, last):
                with sp.Fori(0, NE1 // 2) as p:
                    for j in range(2):
                        e = 2 * p + j
                        sp.wait_ge(a_fill, base("a", k, "C") + e * M1 + M1)
                        half_set(e + 2, 0, j)
                        sp.wait_ge(d_fill, base("d", k, "C") + e * B + (PLACE["d", "down"][1] + B))
                        half_set(e + 2, 1, j)
                if not last:
                    for par, stage, i in ((0, "exp2", 15), (1, "hid3", 23)):
                        sp.wait_ge(d_fill, d_count(k, stage, i))
                        half_set(par, 0, par)
                        half_set(par, 1, par)

            with sp.Fori(1, NBLK - 1) as k:
                sets(k, False)
            sets(NBLK - 1, False)
            sets(NBLK, True)
            for half in range(2):
                for par in range(2):
                    sp.wait_ge(w_in[half][par], 16 * NBLK * (NEW // 2))
            sp.wait_ge(st_out, 16 * NBLK * B)

        @block.gpsimd
        def _(g):
            g.sem_inc(l_copy, 2)
            g.sem_inc(pair_add, 4)
            g.dma_start(RX[:, :].rearrange("p (b c) -> p b c", b=B),
                        a["x"][:, 0:TB, :].rearrange("b p c -> p b c")).then_inc(x_in, 16)
            G.memset(IDF[:, :], 0.0).then_inc(s_gen, 1)
            G.memset(IDH[:, :], 0.0).then_inc(s_gen, 1)
            G.memset(PW[:, :], -0.5).then_inc(s_gen, 1)
            G.iota(IOTA[:, :], [[1, T]], base=0, channel_multiplier=0,
                   allow_small_or_imprecise_dtypes=True).then_inc(s_gen, 1)
            g.wait_ge(s_gen, 4)
            G.affine_select(out=IDF[:, :], in_=IDF[:, :], compare_op=ALU.not_equal, fill=1.0, base=0,
                            pattern=[[-1, P]], channel_multiplier=1).then_inc(s_gen, 1)
            G.affine_select(out=IDH[:, :], in_=IDH[:, :], compare_op=ALU.not_equal, fill=1.0, base=0,
                            pattern=[[-1, P]], channel_multiplier=1).then_inc(s_gen, 1)
            g.wait_ge(s_ln, 1)
            G.tensor_tensor(SM[0:B, 2:3], SM[0:B, 1:2], PW[0:B, 0:1], ALU.pow).then_inc(s_lnp, 1)

            for w3 in range(F_UNITS // F_GROUP):
                for f in (2 * w3, 2 * w3 + 1):
                    g.wait_ge(f_evac, 2 * C * (f + 1))
                    if f:
                        g.wait_ge(f_out, 16 * f)
                    g.dma_start(turn[f], FO[f % 3]).then_inc(f_out, 16)
                g.wait_ge(f_out, 16 * (2 * w3 + 2))
                if w3:
                    g.wait_ge(f_in, 16 * 4 * w3)
                if w3 == 1:
                    g.wait_ge(dw_fill, B)
                src = turn[2 * w3:2 * w3 + 2].rearrange("w b (c h r d) -> w h r b c d", c=C, h=2, r=R // 2)
                for w in range(2):
                    for h in range(2):
                        dst = FT[w3][h * (R // 2):(h + 1) * (R // 2), w * B * D:(w + 1) * B * D]
                        g.dma_start(dst.rearrange("r (b c d) -> r b c d", b=B, c=C), src[w, h]).then_inc(f_in, 16)

            def step(k, dyn, s):
                g.wait_ge(l_h, steps(k, dyn, s))
                if isinstance(dyn, int) and not isinstance(k, int):
                    g.sem_inc(s_mark, 1)
                h = HT[:, :].rearrange("p (q s) -> p q s", s=TB)
                h = h[:, :, s:s + 1] if isinstance(dyn, int) else h[:, :, bass.ds(dyn + s, 1)]
                G.tensor_copy(h, HF[s % 2][:, :].rearrange("p (q o) -> p q o", o=1)).then_inc(l_copy, 1)

            def load_x(k):
                g.wait_ge(r_row, base("rrow", k, "X"))
                g.sem_inc(s_mark, 1)
                src = a["x"][:, TB:2 * TB, :] if isinstance(k, int) else a["x"][:, bass.ds(k * TB + TB, TB), :]
                g.dma_start(RX[:, :].rearrange("p (b c) -> p b c", b=B), src.rearrange("b p c -> p b c")).then_inc(x_in, 16)

            def c_part(k, slot):
                g.wait_ge(p_in, plus(k, "pow", "C", 1))
                G.tensor_tensor(SM[:, 8:12], SM[:, 4:8], PW[:, 0:4], ALU.pow).then_inc(p_out, 1)
                g.wait_ge(d_fill, d_count(k, "uT", B - 1))
                g.sem_inc(s_mark, 1)
                slot.bare(C_SLOTS - 27)

                def add_pairs(xs, dst):
                    for x in xs:
                        g.wait_ge(d_free, d_count(k, *gated_fill(x), DB))
                        g.wait_ge(pair_add, gated_count(k, x, 3))
                        G.tensor_tensor(dst, dst, GP2[x % 4][:, :], ALU.add).then_inc(pair_add, 1)

                for x in range(0, 16, 2):
                    slot()
                    add_pairs((x, x + 1), RES[:, (x // 4) * D:(x // 4 + 1) * D])
                slot.bare(5)

                def rstd(j):
                    g.wait_ge(p_in, plus(k, "pow", "C", 2 + j))
                    G.tensor_tensor(SM[:, 24 + 2 * j:26 + 2 * j], SM[:, 16 + 2 * j:18 + 2 * j], PW[:, 0:2],
                                    ALU.pow).then_inc(p_out, 1)

                for j in range(B):
                    slot()
                    if j:
                        rstd(j - 1)
                    add_pairs((16 + 4 * j,), HB[j % 2][:, 0:D])
                    slot()
                    add_pairs(range(17 + 4 * j, 20 + 4 * j), HB[j % 2][:, 0:D])
                slot()
                rstd(B - 1)
                slot()
                for j in range(B):
                    slot()
                    add_pairs(range(32 + 4 * j, 36 + 4 * j), RES[:, j * D:(j + 1) * D])
                    g.wait_ge(pair_add, gated_count(k, 35 + 4 * j, 4))
                    g.sem_inc(s_mark, 1)
                    dst = out[j, (k - 1) * TB:k * TB, :] if isinstance(k, int) else out[j, bass.ds((k - 1) * TB, TB), :]
                    g.dma_start(dst, RES[:, j * D:(j + 1) * D]).then_inc(st_out, 16)

            load_x(0)
            Slots(g, step, 0).bare(TB)
            with g.Fori(1, NBLK - 1) as k:
                load_x(k)
                slot = Slots(g, step, k)
                c_part(k, slot)
                slot.bare(TB - C_SLOTS)
            slot = Slots(g, step, NBLK - 1)
            c_part(NBLK - 1, slot)
            slot.bare(TB - C_SLOTS)
            c_part(NBLK, Slots(g, None, NBLK))

        @block.scalar
        def _(act):
            act.wait_ge(s_const, 16 * 9)
            act.wait_ge(s_lnT, 1)
            for c in range(C):
                A_.activation(HC[:, c * B:(c + 1) * B], DP[0][:, c * B:(c + 1) * B], ACT.Identity,
                              scale=col("g0", 1, c), bias=col("be0", 1, c)).then_inc(s_ae, 1)
                A_.activation(HC[:, (C + c) * B:(C + c + 1) * B], DP[0][:, c * B:(c + 1) * B], ACT.Identity,
                              scale=col("g3", 1, c), bias=col("be3", 1, c)).then_inc(s_ae, 1)
            act.wait_ge(s_hc, 1)
            for w in range(2):
                for m in range(C):
                    A_.activation(HID[:, (w * C + m) * B:(w * C + m + 1) * B],
                                  DP[1][:, (w * C + m) * B:(w * C + m + 1) * B], ACT.Gelu,
                                  bias=col("b1_3" if w else "b1_0", 1, m)).then_inc(s_h, 1)
            def factor(n):
                act.wait_ge(f_fill, n + 1)
                f, u = divmod(n, 2 * C)
                if f >= 3 and u == 0:
                    act.wait_ge(f_out, 16 * (f - 2))
                A_.activation(FO[f % 3][:, u * 512:(u + 1) * 512], GP[n % 2][0:B, :], ACT.Copy).then_inc(f_evac, 1)

            def matrix_hi(t):
                act.wait_ge(dw_sum, t + 1)
                A_.activation(DWH[:, t * 2 * D:(t + 1) * 2 * D], TT[t % 2][:, :], ACT.Copy, scale=S).then_inc(dw_hi, 1)

            for n in range(F_GROUP):
                factor(n)
            for i, (o, w, sc) in enumerate(RES_UNITS):
                if i == DW0_AT:
                    for t in range(B):
                        matrix_hi(t)
                n = res_unit(i)
                act.wait_ge(raw_in[n % RS], 16 * (n // RS + 1))
                A_.activation(WH[:, o:o + w], RAW[n % RS][:, 0:w], ACT.Copy, scale=sc).then_inc(w_hi, 1)

            def step(k, dyn, s):
                n = steps(k, dyn, s)
                act.wait_ge(l_pre, n)
                A_.activation(TG[:, 0:GC * B], PRE[:, :], ACT.Tanh, scale=1.0 / 128).then_inc(l_tg, 1)
                act.wait_ge(l_d, n)
                A_.activation(TC[:, :], DC[:, :], ACT.Tanh, scale=0.5).then_inc(l_tc, 1)

            def d_hi(k, stage, i, dst, scale=1.0):
                act.wait_ge(d_fill, d_count(k, stage, i))
                A_.activation(dst, dbank(stage, i)[:, :], ACT.Copy, scale=scale).then_inc(dh, 1)

            def a_split(fills, lows, frees, par, evac, hi_dst, view=None):
                act.wait_ge(a_fill, fills)
                act.wait_ge(al, lows)
                evac(TT[par])
                act.wait_ge(a_free, frees)
                A_.activation(hi_dst, TT[par][:, :] if view is None else view(TT[par]), ACT.Copy).then_inc(ah, 1)

            def split_a(k, stage, i, evac, hi_dst, view=None):
                a_split(a_count(k, stage, i), a_count(k, stage, i), a_count(k, stage, i, AB), i % 2, evac, hi_dst, view)

            def xp_half(k, half, ms):
                for m in ms:
                    def evac(t, m=m):
                        A_.activation(t[:, 0:NT // 2], abank(f"xp{half}", m)[:, 0:NT // 2], ACT.Identity,
                                      scale=2.0 if m >= 6 else 1.0, bias=LB0[:, m:m + 1]).then_inc(a_free, 1)
                    split_a(k, f"xp{half}", m, evac, xp_pair(half)[:, :, :, 2 * m],
                            lambda t: t[:, 0:NT // 2].rearrange("p (b s) -> p b s", b=B))

            def up(k, e, par, m):
                def evac(t):
                    A_.activation(t[:, :], abank("up", m)[:, :], ACT.Gelu, scale=IS,
                                  bias=B1CUR[par][:, m:m + 1]).then_inc(a_free, 1)
                if m == 0:
                    act.wait_ge(b1_ready, base("b1", k, "C") + e + 1)
                n = base("a", k, "C") + e * M1 + m
                a_split(n + 1, n + 1, n + 1 + AB, m % 2, evac, GH[par][:, m * NT:(m + 1) * NT])

            def a_part(k, slot):
                slot()
                for c in range(C):
                    d_hi(k, "xT", c, QH[:, c * NT:(c + 1) * NT])
                for m in range(C):
                    slot()
                    d_hi(k, "y0T", m, ZH[:, m * NT:(m + 1) * NT], IS)
                act.wait_ge(g_diff, plus(k, "diff", "A", 1))
                A_.activation(SM[:, 36:40], SM[:, 32:36], ACT.Tanh, scale=0.5).then_inc(g_tanh, 1)
                slot()
                slot()
                for j in range(B):
                    if j % 2 == 0:
                        slot()
                    d_hi(k, "h0T", j, KH[:, j * 512:(j + 1) * 512])
                slot()
                slot()
                for c in range(C):
                    d_hi(k, "x1T", c, QH[:, c * NT:(c + 1) * NT])
                for m in range(0, GC, 4):
                    slot()
                    xp_half(k, 0, range(m, m + 4))

            def c_part(k, slot, x):
                act.wait_ge(g_diff, plus(k, "diff", "C", 1))
                A_.activation(SC[:, 0:B * E], L[:, 0:B * E], ACT.Tanh, scale=0.5).then_inc(g_tanh, 1)
                for j in range(B):
                    act.wait_ge(d_fill, d_count(k, "uT", j))
                    A_.activation(JUNK[:, j * D:(j + 1) * D], dbank("uT", j)[:, 0:D], ACT.Square, scale=0.5,
                                  accum_out=SM[:, j:j + 1]).then_inc(sq, 1)
                if x:
                    for m in range(0, GC, 4):
                        slot()
                        xp_half(k, 1, range(m, m + 4))
                slot()
                slot()
                for c in range(C):
                    d_hi(k, "xnT", c, QH[:, c * NT:(c + 1) * NT])
                slot()
                slot()
                for m in range(M1):
                    if m % 2 == 0:
                        slot()
                    up(k, 0, 0, m)
                with slot.repeat(0, 4, 2 * M1) as p:
                    for j in range(2):
                        for m in range(M1):
                            slot()
                            up(k, 2 * p + (j + 1), (j + 1) % 2, m)
                for m in range(M1):
                    slot()
                    up(k, NE1 - 1, 1, m)
                slot.bare(B)

                for m in range(C):
                    slot()
                    if m == 0:
                        for c in range(C):
                            d_hi(k, "x2T", c, QH[:, c * NT:(c + 1) * NT])

                    def evac(t, m=m):
                        for b in range(B):
                            ins = A_.activation(t[:, b * TB:(b + 1) * TB], abank("z2", m)[:, b * TB:(b + 1) * TB],
                                                ACT.Tanh, scale=IS, bias=HBT[:, m * B + b:m * B + b + 1])
                        ins.then_inc(a_free, 1)
                    split_a(k, "z2", m, evac, ZH[:, m * NT:(m + 1) * NT])
                act.wait_ge(g_diff, plus(k, "diff", "C", 2))
                A_.activation(SM[:, 36:40], SM[:, 32:36], ACT.Tanh, scale=0.5).then_inc(g_tanh, 1)
                slot.bare(2)

                def halves(xs, gates):
                    for x in xs:
                        stage, i = gated_fill(x)
                        if x >= 2:
                            act.wait_ge(d_free, d_count(k, *gated_fill(x - 2), DB))
                        act.wait_ge(d_fill, d_count(k, stage, i))
                        A_.activation(GS[x % 2][:, :], dbank(stage, i)[:, D:2 * D], ACT.Copy,
                                      scale=gates[x]).then_inc(half_in, 1)

                def second(t, n):
                    return [t[:, j * n + 2 * w + 1:j * n + 2 * w + 2] for j in range(B) for w in range(4)]

                gates = second(GT2, E) + second(GA, E) + second(GE, 9)
                for x in range(0, 16, 2):
                    slot()
                    halves((x, x + 1), gates)

                for m in range(C):
                    slot()
                    if m == 0:
                        for c in range(C):
                            act.wait_ge(d_fill, d_count(k, "x3T", c))
                            A_.activation(YF[:, c * NT:(c + 1) * NT], dbank("x3T", c)[:, :], ACT.Copy).then_inc(x3f, 1)
                            d_hi(k, "x3T", c, QH[:, c * NT:(c + 1) * NT])

                    def evac(t, m=m):
                        A_.activation(t[:, :], abank("mid", m)[:, :], ACT.Gelu, scale=IS).then_inc(a_free, 1)
                    split_a(k, "mid", m, evac, ZH[:, m * NT:(m + 1) * NT])
                slot()
                for m in range(C):
                    act.wait_ge(yf, (k - 1) * C + m + 1)
                    A_.activation(QH[:, m * NT:(m + 1) * NT], YF[:, m * NT:(m + 1) * NT], ACT.Copy).then_inc(yh, 1)
                slot()
                act.wait_ge(g_diff, plus(k, "diff", "C", 3))
                A_.activation(SC[:, :], L[:, :], ACT.Tanh, scale=0.5).then_inc(g_tanh, 1)
                act.wait_ge(g_diff, plus(k, "diff", "C", 4))
                A_.activation(SM[:, 36:40], SM[:, 32:36], ACT.Tanh, scale=0.5).then_inc(g_tanh, 1)
                slot.bare(1)

                def hidden_tanh(j):
                    act.wait_ge(pair_add, gated_count(k, 19 + 4 * j, 4))
                    hv = HB[j % 2][:, :].rearrange("p (v w h) -> p v w h", v=2, w=2)
                    A_.activation(TT[0][:, (j % 2) * 256:(j % 2) * 256 + 256].rearrange("p (v h) -> p v h", v=2),
                                  hv[:, :, 0, :], ACT.Tanh, scale=0.5).then_inc(hs_tanh, 1)

                for j in range(B):
                    slot()
                    if j:
                        hidden_tanh(j - 1)
                    halves((16 + 4 * j,), gates)
                    slot()
                    halves(range(17 + 4 * j, 20 + 4 * j), gates)
                slot()
                hidden_tanh(B - 1)
                slot()
                for v in range(2):
                    def evac(t, v=v):
                        A_.activation(t[:, :], abank("nT", v)[:, :], ACT.Identity,
                                      scale=col("s_g" if v else "sel_g"), bias=col("s_b" if v else "sel_b")).then_inc(a_free, 1)
                    split_a(k, "nT", v, evac, ZH[:, v * NT:(v + 1) * NT])
                for j in range(B):
                    slot()
                    halves(range(32 + 4 * j, 36 + 4 * j), gates)

            def factors(k, dyn, s):
                first = F_GROUP + sum(F_SLOTS[:s])
                for n in range(first, first + F_SLOTS[s]):
                    factor(n)

            act.wait_ge(dw_lo, B)
            a_part(-1, Slots(act, factors, -1))
            none = Slots(act, None, 0)

            slot = Slots(act, step, 0)
            for m in range(0, GC, 4):
                slot()
                xp_half(0, 1, range(m, m + 4))
            slot.bare(1)
            for t in range(B, 3 * B):
                slot()
                matrix_hi(t)

            def split_set(q):
                act.wait_ge(pg_ready, q + 1)
                for u in range(UPS):
                    r = (SETUP_UNITS + u) % RS
                    for half in range(2):
                        slot()
                        if half == 0:
                            act.wait_ge(raw_in[r], q * 16 + 16 * ((SETUP_UNITS + u) // RS + 1))
                            if not isinstance(q, int):
                                act.wait_ge(split_out[u], q * 16)
                        o = half * (RU // 2)
                        A_.activation(STAGE[u][:, o:o + RU // 2], RAW[r][:, o:o + RU // 2], ACT.Identity,
                                      scale=PG[:, u:u + 1]).then_inc(e_hi, 1)

            split_set(0)
            with slot.repeat(1, NEW, 2 * UPS) as q:
                split_set(q)
            slot.bare(BARE0)
            act.wait_ge(dw_lo, 3 * B)
            for u in range(UPS):
                act.wait_ge(split_out[u], 16 * NEW)
            a_part(0, slot)
            with act.Fori(1, NBLK - 1) as k:
                slot = Slots(act, step, k)
                c_part(k, slot, True)
                a_part(k, slot)
            slot = Slots(act, step, NBLK - 1)
            c_part(NBLK - 1, slot, True)
            slot.bare(TB - C_SLOTS)
            c_part(NBLK, none, False)

        @block.vector
        def _(dve):
            def done(sem_, n=1):
                V.drain().then_inc(sem_, n)

            done(raw_free, RS)
            done(l_c)
            done(d_free, DB)
            done(al, 2)
            dve.wait_ge(s_const, 16 * 9)
            V.bn_stats(ST[0:B, 0:6], LNX[:, :])
            V.drain()
            V.bn_aggr(SM[0:B, 0:2], ST[0:B, 0:6])
            V.drain()
            V.tensor_scalar(SM[0:B, 1:2], SM[0:B, 1:2], LN_EPS, None, ALU.add).then_inc(s_ln, 1)
            V.tensor_scalar(LB0[:, 0:6], col("lstm_b", 6), S, None, ALU.mult)
            V.tensor_scalar(LB0[:, 6:8], col("lstm_b", 2, 6), 2 * S, None, ALU.mult)
            V.tensor_scalar(GAIN[:, :], GAIN[:, :], S, None, ALU.mult)
            V.memset(TG[:, GC * B:(GC + C) * B], 0.0)
            V.tensor_scalar(HF[1][:, :], col("condT", C * B), 2.0, None, ALU.mult)
            V.drain()
            h0v = H16[0][:, :].rearrange("p (c v b) -> p c v b", c=C, v=2)
            hfv = [HF[i][:, :].rearrange("p (c b) -> p c b", c=C) for i in range(2)]
            V.tensor_copy(h0v[:, :, 0, :], hfv[1])
            V.drain()
            V.tensor_tensor(h0v[:, :, 1, :], hfv[1], h0v[:, :, 0, :], ALU.subtract)
            done(l_hi)
            done(l_lo)
            dve.wait_ge(s_lnp, 1)
            V.tensor_scalar(LNX[:, :], LNX[:, :], SM[0:B, 0:1], SM[0:B, 2:3], ALU.subtract, ALU.mult)
            done(s_ln)
            dve.wait_ge(s_gen, 6)
            dve.wait_ge(s_idx, 16)
            V.tensor_copy(IDXF[:, :], IDXI[:, :])
            V.drain()
            V.tensor_scalar(IDXG[:, 0:4], IDXF[:, 0:4], 0.0, float(B), ALU.is_lt, ALU.mult)
            V.tensor_scalar(IDXG[:, 4:8], IDXF[:, 4:8], 0.0, float(T), ALU.is_lt, ALU.mult)
            V.drain()
            V.tensor_tensor(IDXF[:, :], IDXF[:, :], IDXG[:, :], ALU.add)
            V.drain()
            for i in range(4):
                V.tensor_scalar(EQB[:, i * B:(i + 1) * B], IOTA[:, 0:B], IDXF[:, i:i + 1], None, ALU.is_equal)
                V.tensor_scalar(EQT[:, i * T:(i + 1) * T], IOTA[:, :], IDXF[:, 4 + i:5 + i], None, ALU.is_equal)
            done(s_eq)
            dve.wait_ge(s_in, 1)
            V.tensor_scalar(INSET[:, :], DP[3][:, 0:NBLK * B], 1.0, None, ALU.min)
            dve.wait_ge(s_hbt, 1)
            for m in range(C):
                V.tensor_scalar(HBT[:, m * B:(m + 1) * B], DP[2][:, m * B:(m + 1) * B], col("bhh", 1, m),
                                col("bih", 1, m), ALU.add, ALU.add)
            dve.wait_ge(s_tmpw, 32)
            for c in range(C):
                o = TO["base0"] + c * D + c * P
                V.tensor_tensor(TMP[:, o:o + P], TMP[:, o:o + P], IDF[:, :], ALU.add)
            V.drain()
            def factor_bias(w3):
                dve.wait_ge(f_in, 16 * 4 * (w3 + 1))
                ftv = FT[w3].rearrange("r (w b d) -> r w b d", w=2, b=B)
                for w in range(2):
                    f, o = divmod(2 * w3 + w, NFACT // 2)
                    V.tensor_tensor(ftv[:, w, :, :], ftv[:, w, :, :],
                                    FB[f][:, o * D:(o + 1) * D].unsqueeze(1).to_broadcast([R, B, D]), ALU.add)
                done(f_bias)

            def matrix_sum(t):
                w3 = t // B
                dve.wait_ge(dw_fill, t + 1)
                V.drain()
                V.tensor_tensor(TT[t % 2][:, :], DP[2 + t % 2][:, :],
                                RES[:, (w3 - 1) * C * D:w3 * C * D] if w3 else tmp("base0", C * D), ALU.add).then_inc(dw_sum, 1)

            def matrix_lo(t):
                dve.wait_ge(dw_hi, t + 1)
                V.scalar_tensor_tensor(DWL[:, t * 2 * D:(t + 1) * 2 * D], TT[t % 2][:, :], S,
                                       DWH[:, t * 2 * D:(t + 1) * 2 * D], ALU.mult, ALU.subtract).then_inc(dw_lo, 1)

            dve.wait_ge(raw_free, RS + F_GROUP)
            for i, (o, w, sc) in enumerate(RES_UNITS):
                if i == DW0_AT:
                    factor_bias(0)
                    for t in range(B):
                        matrix_sum(t)
                        if t:
                            matrix_lo(t - 1)
                    matrix_lo(B - 1)
                n = res_unit(i)
                dve.wait_ge(w_hi, i + 1)
                V.scalar_tensor_tensor(WL[:, o:o + w], RAW[n % RS][:, 0:w], sc, WH[:, o:o + w],
                                       ALU.mult, ALU.subtract).then_inc(raw_free, 1)
            done(res_lo)

            def step(k, dyn, s):
                j, n = s % 2, steps(k, dyn, s)
                h16 = H16[(j + 1) % 2][:, :].rearrange("p (c v b) -> p c v b", c=C, v=2)
                dve.wait_ge(l_pe, n)
                V.tensor_reduce(PRE[:, :].rearrange("p (c b) -> p c b", c=GC),
                                GP[j][:, 0:GC * 2 * B].rearrange("p (c v b) -> p c b v", v=2, b=B),
                                AX.X, ALU.add).then_inc(l_pre, 1)
                dve.wait_ge(l_tg, n)
                V.scalar_tensor_tensor(WK[:, :], TG[:, 0:16], 1.0, TG[:, 24:40], ALU.add, ALU.mult).then_inc(l_w, 1)
                dve.wait_ge(l_w, n)
                V.tensor_tensor(DC[:, :], WK[:, 0:8], WK[:, 8:16], ALU.add).then_inc(l_d, 1)
                dve.wait_ge(l_d, n)
                V.tensor_scalar(TG[:, 32:40], DC[:, :], 0.5, None, ALU.mult).then_inc(l_c, 1)
                dve.wait_ge(l_tc, n)
                tov = TG[:, 16:24].rearrange("p (c b) -> p c b", c=C)
                tcv = TC[:, :].rearrange("p (c b) -> p c b", c=C)
                V.scalar_tensor_tensor(h16[:, :, 0, :], tov, 1.0, tcv, ALU.add, ALU.mult).then_inc(l_hi, 1)
                dve.wait_ge(l_copy, n)
                V.scalar_tensor_tensor(hfv[j], tov, 1.0, tcv, ALU.add, ALU.mult).then_inc(l_h, 1)
                dve.wait_ge(l_hi, steps(k, dyn, s, 2))
                dve.wait_ge(l_h, n)
                V.tensor_tensor(h16[:, :, 1, :], hfv[j], h16[:, :, 0, :], ALU.subtract).then_inc(l_lo, 1)

            def d_lo(k, stage, i, hi, dst, scale=1.0):
                dve.wait_ge(dh, h_count(k, stage, i))
                V.scalar_tensor_tensor(dst, dbank(stage, i)[:, :], scale, hi, ALU.mult, ALU.subtract).then_inc(d_free, 1)

            def q_lo(k, stage):
                for c in range(C):
                    d_lo(k, stage, c, QH[:, c * NT:(c + 1) * NT], QL[:, c * NT:(c + 1) * NT])

            def z_lo(k, stage, i):
                dve.wait_ge(ah, a_count(k, stage, i))
                V.tensor_tensor(ZL[:, i * NT:(i + 1) * NT], TT[i % 2][:, :], ZH[:, i * NT:(i + 1) * NT],
                                ALU.subtract).then_inc(al, 1)

            def up_lo(k, e, par, m):
                dve.wait_ge(ah, base("a", k, "C") + e * M1 + (m + 1))
                V.tensor_tensor(GL[par][:, m * NT:(m + 1) * NT], TT[m % 2][:, :], GH[par][:, m * NT:(m + 1) * NT],
                                ALU.subtract).then_inc(al, 1)

            def down_add(k, e, par, j):
                dve.wait_ge(d_fill, base("d", k, "C") + e * B + (PLACE["d", "down"][1] + j + 1))
                r = RES[:, j * D:(j + 1) * D]
                V.scalar_tensor_tensor(r, dbank("down", j)[:, 0:D], GCUR[par][:, j:j + 1], r,
                                       ALU.mult, ALU.add).then_inc(d_free, 1)

            def xp_half(k, half, ms):
                for m in ms:
                    xv = xp_pair(half)
                    dve.wait_ge(ah, a_count(k, f"xp{half}", m))
                    V.tensor_tensor(xv[:, :, :, 2 * m + 1], TT[m % 2][:, 0:NT // 2].rearrange("p (b s) -> p b s", b=B),
                                    xv[:, :, :, 2 * m], ALU.subtract).then_inc(al, 1)

            def filled(k, stage, i):
                dve.wait_ge(d_fill, d_count(k, stage, i))

            def top2(src, n=E):
                for j in range(B):
                    V.max(MX[:, j * 8:(j + 1) * 8], src[:, j * n:j * n + E])
                V.drain()
                for j in range(B):
                    V.max_index(IX[:, j * 8:(j + 1) * 8], MX[:, j * 8:(j + 1) * 8], src[:, j * n:j * n + E])
                V.drain()
                V.tensor_copy(IXF[:, :], IX[:, :])
                mxv = MX[:, :].rearrange("p (j e) -> p j e", j=B)
                V.tensor_tensor(SM[:, 32:36], mxv[:, :, 0], mxv[:, :, 1], ALU.subtract)

            def softmax2(tanhs, scale):
                dve.wait_ge(g_tanh, tanhs)
                V.tensor_scalar(SM[:, 40:44], SM[:, 36:40], 0.5 * scale, 0.5 * scale, ALU.mult, ALU.add)
                V.tensor_scalar(SM[:, 44:48], SM[:, 36:40], -0.5 * scale, 0.5 * scale, ALU.mult, ALU.add)
                V.drain()
                for j in range(B):
                    V.tensor_scalar(GA[:, j * 8:(j + 1) * 8], IOTA[:, 0:E], IXF[:, j * 8:j * 8 + 1],
                                    SM[:, 40 + j:41 + j], ALU.is_equal, ALU.mult)
                    V.tensor_scalar(GT[:, j * 8:(j + 1) * 8], IOTA[:, 0:E], IXF[:, j * 8 + 1:j * 8 + 2],
                                    SM[:, 44 + j:45 + j], ALU.is_equal, ALU.mult)
                V.drain()
                V.tensor_tensor(GT[:, 0:B * E], GT[:, 0:B * E], GA[:, :], ALU.add)
                V.drain()

            def a_part(k, slot):
                slot()
                q_lo(k, "xT")
                for m in range(C):
                    slot()
                    d_lo(k, "y0T", m, ZH[:, m * NT:(m + 1) * NT], ZL[:, m * NT:(m + 1) * NT], IS)
                filled(k, "log0", 0)
                V.tensor_scalar(L[:, 0:B * E], dbank("log0", 0)[:, 0:B * E], IS, None, ALU.mult).then_inc(d_free, 1)
                V.drain()
                top2(L)
                done(g_diff)
                softmax2(plus(k, "diff", "A", 1), 0.5)
                done(g_mat)
                slot()
                filled(k, "g0T", 0)
                V.tensor_scalar(GTT[0:E, 0:NT], dbank("g0T", 0)[0:E, :], S, None, ALU.mult).then_inc(d_free, 1)
                done(gt_copy)
                if not (isinstance(k, int) and k < 0):
                    rows_in(k)

                for j in range(B):
                    if j % 2 == 0:
                        slot()
                    if j >= 2:
                        d_lo(k, "h0T", j - 2, KH[:, (j - 2) * 512:(j - 1) * 512], KL[:, (j - 2) * 512:(j - 1) * 512])
                    filled(k, "h0", j)
                    hb = HB[j % 2]
                    V.scalar_tensor_tensor(hb[:, :], dbank("h0", j)[:, :], IS, row("bd", 512), ALU.mult, ALU.add).then_inc(d_free, 1)
                    V.drain()
                    V.scalar_tensor_tensor(hb[:, :].rearrange("p (e h) -> p e h", e=E),
                                           hb[:, :].rearrange("p (e h) -> p e h", e=E), 0.0,
                                           GT[:, j * E:(j + 1) * E].unsqueeze(2).to_broadcast([P, E, 64]),
                                           ALU.max, ALU.mult)
                    done(h_row)
                slot()
                for j in range(2, B):
                    d_lo(k, "h0T", j, KH[:, j * 512:(j + 1) * 512], KL[:, j * 512:(j + 1) * 512])
                for j in range(B):
                    if j == 2:
                        slot()
                    filled(k, "out0", j)
                    V.scalar_tensor_tensor(RW[:, j * D:(j + 1) * D], dbank("out0", j)[:, 0:D], IS,
                                           RX[:, j * D:(j + 1) * D], ALU.mult, ALU.add).then_inc(d_free, 1)
                    done(r_row)
                slot()
                q_lo(k, "x1T")
                for m in range(0, GC, 4):
                    slot()
                    xp_half(k, 0, range(m, m + 4))

            def rows_in(k):
                if not (isinstance(k, int) and k == 0):
                    dve.wait_ge(st_out, k * (16 * B))
                V.tensor_copy(RES[:, :], RW[:, :])

            def c_part(k, slot, x):
                for j in range(B):
                    filled(k, "log1", j)
                    V.tensor_scalar(L[:, j * E:(j + 1) * E], dbank("log1", j)[:, 0:E], 0.5, None, ALU.mult).then_inc(d_free, 1)
                done(g_diff)
                for j in range(B):
                    filled(k, "uT", j)
                    dve.wait_ge(sq, (k - 1) * B + j + 1)
                    V.tensor_scalar(UT[:, j * D:(j + 1) * D], dbank("uT", j)[:, 0:D], 0.5, None, ALU.mult).then_inc(d_free, 1)
                V.tensor_scalar(SM[:, 4:8], SM[:, 0:4], 1.0 / D, RMS_EPS, ALU.mult, ALU.add)
                done(p_in)
                for e in range(2):
                    V.tensor_copy(B1CUR[e][:, :], B1[:, e * M1:(e + 1) * M1])
                    done(b1_ready)
                if x:
                    for m in range(0, GC, 4):
                        slot()
                        xp_half(k, 1, range(m, m + 4))
                slot()
                V.tensor_tensor(RES[:, :], RES[:, :], UT[:, :], ALU.add)
                V.drain()
                dve.wait_ge(p_out, plus(k, "pow", "C", 1))
                for j in range(B):
                    V.tensor_scalar(UT[:, j * D:(j + 1) * D], UT[:, j * D:(j + 1) * D], SM[:, 8 + j:9 + j], None, ALU.mult)
                done(xn_row)
                dve.wait_ge(g_tanh, plus(k, "diff", "C", 1))
                V.tensor_scalar(SC[:, 0:B * E], SC[:, 0:B * E], 0.5, 0.5, ALU.mult, ALU.add)
                V.drain()
                top2(SC)
                slot()
                q_lo(k, "xnT")
                V.reduce_sum(SM[:, 48:52], SC[:, 0:B * E].rearrange("p (j e) -> p j e", j=B), AX.X)
                V.drain()
                V.reciprocal(SM[:, 52:56], SM[:, 48:52])
                V.memset(GT[:, :], 1.0)
                for j in range(B):
                    V.tensor_scalar(GA[:, j * 8:(j + 1) * 8], IOTA[:, 0:E], IXF[:, j * 8:j * 8 + 1], None, ALU.is_equal)
                V.drain()
                for j in range(B):
                    V.scalar_tensor_tensor(GA[:, j * 8:(j + 1) * 8], IOTA[:, 0:E], IXF[:, j * 8 + 1:j * 8 + 2],
                                           GA[:, j * 8:(j + 1) * 8], ALU.is_equal, ALU.add)
                V.drain()
                for j in range(B):
                    V.scalar_tensor_tensor(GT[:, j * NE1 + 2:(j + 1) * NE1], SC[:, j * E:(j + 1) * E], SM[:, 52 + j:53 + j],
                                           GA[:, j * 8:(j + 1) * 8], ALU.mult, ALU.mult)
                V.drain()
                V.tensor_scalar(GE[:, :].rearrange("p (e j) -> p j e", j=B), GT[:, :].rearrange("p (j e) -> p j e", j=B),
                                IS, None, ALU.mult)
                done(g_mat)
                slot()
                for h in range(2):
                    filled(k, "g1T", h)
                    V.tensor_copy(GTT[0:NE1, h * 256:(h + 1) * 256], dbank("g1T", h)[0:NE1, 0:256]).then_inc(d_free, 1)
                done(gt_copy)
                slot()
                for j in range(B):
                    filled(k, "bias1", j)
                    r = RES[:, j * D:(j + 1) * D]
                    V.tensor_tensor(r, dbank("bias1", j)[:, 0:D], r, ALU.add).then_inc(d_free, 1)
                for t in range(M1 // 2):
                    slot()
                    if t:
                        up_lo(k, 0, 0, 2 * t - 2)
                        up_lo(k, 0, 0, 2 * t - 1)
                    if t == M1 // 2 - 1:
                        up_lo(k, 0, 0, 2 * t)

                def group(e, par, last):
                    for i in range(M1):
                        slot()
                        if i == 0:
                            up_lo(k, e, par, M1 - 1)
                            V.tensor_copy(GCUR[par][:, :], at(GE, e * B, B))
                            if not last:
                                V.tensor_copy(B1CUR[par][:, :], at(B1, (e + 2) * M1, M1))
                                done(b1_ready)
                        else:
                            up_lo(k, e + 1, 1 - par, i - 1)
                        if i % 2 == 0 and i:
                            down_add(k, e, par, i // 2 - 1)
                        if i == M1 - 1:
                            down_add(k, e, par, B - 1)

                with slot.repeat(0, 4, 2 * M1) as p:
                    for j2 in range(2):
                        group(2 * p + j2, j2, False)
                group(NE1 - 2, 0, True)
                for j in range(B):
                    slot()
                    if j == 0:
                        up_lo(k, NE1 - 1, 1, M1 - 1)
                        V.tensor_copy(GCUR[1][:, :], at(GE, (NE1 - 1) * B, B))
                        V.drain()
                    down_add(k, NE1 - 1, 1, j)
                done(r_row, B)

                slot()
                q_lo(k, "x2T")
                slot()
                for m in range(C):
                    z_lo(k, "z2", m)
                filled(k, "log2", 0)
                for j in range(B):
                    ins = V.scalar_tensor_tensor(L[:, j * E:(j + 1) * E], dbank("log2", 0)[:, j * E:(j + 1) * E], IS,
                                                 row("gate_b", E), ALU.mult, ALU.add)
                ins.then_inc(d_free, 1)
                V.drain()
                top2(L)
                done(g_diff)
                softmax2(plus(k, "diff", "C", 2), 1.0)
                V.tensor_scalar(GT2[:, 0:B * E], GT[:, 0:B * E], IS, None, ALU.mult)
                done(g_mat)
                slot()
                for h in range(2):
                    filled(k, "g2T", h)
                    V.tensor_copy(GTT[0:E, h * 256:(h + 1) * 256], dbank("g2T", h)[0:E, 0:256]).then_inc(d_free, 1)
                done(gt_copy)
                slot()
                for j in range(B):
                    filled(k, "bias2", j)
                    r = RES[:, j * D:(j + 1) * D]
                    V.tensor_tensor(r, dbank("bias2", j)[:, 0:D], r, ALU.add).then_inc(d_free, 1)

                def pairs(xs, gates):
                    for x in xs:
                        stage, i = gated_fill(x)
                        dve.wait_ge(pair_add, gated_count(k, x))
                        dve.wait_ge(half_in, gated_count(k, x))
                        V.scalar_tensor_tensor(GP2[x % 4][:, :], dbank(stage, i)[:, 0:D], gates[x], GS[x % 2][:, :],
                                               ALU.mult, ALU.add).then_inc(d_free, 1)

                def first(t, n):
                    return [t[:, j * n + 2 * w:j * n + 2 * w + 1] for j in range(B) for w in range(4)]

                gates = first(GT2, E) + first(GA, E) + first(GE, 9)
                for x in range(0, 16, 2):
                    slot()
                    pairs((x, x + 1), gates)

                slot()
                q_lo(k, "x3T")
                z_lo(k, "mid", 0)
                slot()
                z_lo(k, "mid", 1)
                slot()
                dve.wait_ge(x3f, (k - 1) * C + C)
                for m in range(C):
                    filled(k, "y3T", m)
                    y = YF[:, m * NT:(m + 1) * NT]
                    V.scalar_tensor_tensor(y, dbank("y3T", m)[:, :], IS, y, ALU.mult, ALU.add).then_inc(d_free, 1)
                    done(yf)
                    dve.wait_ge(yh, (k - 1) * C + m + 1)
                    V.tensor_tensor(QL[:, m * NT:(m + 1) * NT], y, QH[:, m * NT:(m + 1) * NT], ALU.subtract).then_inc(yl, 1)
                slot()
                filled(k, "log3", 0)
                for j in range(B):
                    ins = V.scalar_tensor_tensor(L[:, j * 9:(j + 1) * 9], dbank("log3", 0)[:, j * 9:(j + 1) * 9], IS,
                                                 row("egsg_b", 9), ALU.mult, ALU.add)
                ins.then_inc(d_free, 1)
                done(g_diff)
                dve.wait_ge(g_tanh, plus(k, "diff", "C", 3))
                V.tensor_scalar(SC[:, :], SC[:, :], 0.5, 0.5, ALU.mult, ALU.add)
                V.drain()
                for j in range(B):
                    V.tensor_tensor(SB_[:, j * E:(j + 1) * E], SC[:, j * 9:j * 9 + E], row("exp_bias", E), ALU.add)
                V.drain()
                top2(SB_)
                V.tensor_copy(IN[:, :], at(INSET, (k - 1) * B, B))
                V.drain()
                for j in range(B):
                    V.tensor_scalar(GA[:, j * 8:(j + 1) * 8], IOTA[:, 0:E], IXF[:, j * 8:j * 8 + 1], None, ALU.is_equal)
                V.drain()
                V.tensor_tensor(SB_[:, :].rearrange("p (j e) -> p j e", j=B), GA[:, :].rearrange("p (j e) -> p j e", j=B),
                                SC[:, :].rearrange("p (j e) -> p j e", j=B)[:, :, 0:E], ALU.mult)
                V.drain()
                V.reduce_sum(SM[:, 48:52], SB_[:, :].rearrange("p (j e) -> p j e", j=B), AX.X)
                V.drain()
                V.tensor_tensor(SM[:, 32:36], SC[:, :].rearrange("p (j e) -> p j e", j=B)[:, :, E], SM[:, 48:52], ALU.subtract)
                done(g_diff)
                dve.wait_ge(g_tanh, plus(k, "diff", "C", 4))
                V.tensor_scalar(SM[:, 40:44], SM[:, 36:40], 0.5, -0.5, ALU.mult, ALU.add)
                V.tensor_scalar(SM[:, 44:48], SM[:, 36:40], -0.5, 0.5, ALU.mult, ALU.add)
                V.memset(GT[:, :], 1.0)
                V.drain()
                V.tensor_tensor(SM[:, 40:44], SM[:, 40:44], IN[:, :], ALU.mult)
                V.tensor_tensor(SM[:, 44:48], SM[:, 44:48], IN[:, :], ALU.mult)
                V.drain()
                gt9 = GT[:, 0:B * 9].rearrange("p (j e) -> p j e", j=B)
                gt29 = GT2[:, 0:B * 9].rearrange("p (j e) -> p j e", j=B)
                V.tensor_copy(gt9[:, :, 0:E], GA[:, :].rearrange("p (j e) -> p j e", j=B))
                for j in range(B):
                    V.tensor_scalar(GT2[:, j * 9:j * 9 + E], GA[:, j * 8:(j + 1) * 8], SM[:, 44 + j:45 + j], None, ALU.mult)
                V.tensor_scalar(gt29[:, :, E], SM[:, 40:44], 1.0, None, ALU.add)
                V.drain()
                V.tensor_scalar(GE[:, 0:36], GT2[:, 0:36], IS, None, ALU.mult)
                V.tensor_scalar(GA[:, :], GA[:, :], IS, None, ALU.mult)
                done(g_mat)
                slot()
                for h in range(2):
                    filled(k, "g3T", h)
                    V.tensor_copy(GTT[0:9, h * NT:(h + 1) * NT], dbank("g3T", h)[0:9, :]).then_inc(d_free, 1)
                done(gt_copy)

                def views(j):
                    o = (j % 2) * 256
                    return (HB[j % 2][:, :].rearrange("p (v w h) -> p v w h", v=2, w=2),
                            TT[0][:, o:o + 256].rearrange("p (v h) -> p v h", v=2),
                            TT[1][:, o:o + 256].rearrange("p (v h) -> p v h", v=2))

                def gated(j):
                    hv, tv, qv = views(j)
                    dve.wait_ge(hs_tanh, (k - 1) * B + j + 1)
                    V.scalar_tensor_tensor(qv, tv, 1.0, hv[:, :, 0, :], ALU.add, ALU.mult)
                    V.drain()
                    V.scalar_tensor_tensor(qv, qv, 0.5, hv[:, :, 1, :], ALU.mult, ALU.mult)
                    V.drain()
                    for v in range(2):
                        V.bn_stats(ST[:, 6 * v:6 * v + 6], qv[:, v, :])
                    V.drain()
                    for v in range(2):
                        V.bn_aggr(ST[:, 16 + 2 * v:18 + 2 * v], ST[:, 6 * v:6 * v + 6])
                    V.drain()
                    for v in range(2):
                        V.tensor_scalar(SM[:, 16 + 2 * j + v:17 + 2 * j + v], ST[:, 17 + 2 * v:18 + 2 * v], LN_EPS, None, ALU.add)
                    done(p_in)

                def normed(j):
                    _, _, qv = views(j)
                    dve.wait_ge(p_out, plus(k, "pow", "C", 2 + j))
                    for v in range(2):
                        V.tensor_scalar(NTM[:, (v * B + j) * P:(v * B + j + 1) * P], qv[:, v, :], ST[:, 16 + 2 * v:17 + 2 * v],
                                        SM[:, 24 + 2 * j + v:25 + 2 * j + v], ALU.subtract, ALU.mult)

                for j in range(B):
                    hb = HB[j % 2]
                    slot()
                    if j:
                        gated(j - 1)
                    filled(k, "hid3", 6 * j)
                    V.tensor_copy(hb[:, :], dbank("hid3", 6 * j)[:, :]).then_inc(d_free, 1)
                    V.drain()
                    filled(k, "hid3", 6 * j + 1)
                    V.scalar_tensor_tensor(hb[:, 256:512], dbank("hid3", 6 * j + 1)[:, 0:256], IS, hb[:, 256:512],
                                           ALU.mult, ALU.add).then_inc(d_free, 1)
                    pairs((16 + 4 * j,), gates)
                    slot()
                    if j:
                        normed(j - 1)
                    pairs(range(17 + 4 * j, 20 + 4 * j), gates)
                slot()
                gated(B - 1)
                slot()
                normed(B - 1)
                done(n_row)
                for j in range(B):
                    slot()
                    if j == 0:
                        for v in range(2):
                            z_lo(k, "nT", v)
                    r = RES[:, j * D:(j + 1) * D]
                    filled(k, "out3", 6 * j)
                    V.tensor_tensor(r, dbank("out3", 6 * j)[:, 0:D], r, ALU.add).then_inc(d_free, 1)
                    V.drain()
                    filled(k, "out3", 6 * j + 1)
                    V.scalar_tensor_tensor(r, dbank("out3", 6 * j + 1)[:, 0:D], GE[:, j * 9 + E:j * 9 + E + 1], r,
                                           ALU.mult, ALU.add).then_inc(d_free, 1)
                    pairs(range(32 + 4 * j, 36 + 4 * j), gates)

            none = Slots(dve, None, 0, V.drain)
            a_part(-1, none)

            slot = Slots(dve, step, 0, V.drain)
            for m in range(0, GC, 4):
                slot()
                xp_half(0, 1, range(m, m + 4))
            slot.bare(1)
            for w3 in range(1, 3):
                factor_bias(w3)
            dve.wait_ge(raw_free, RS + SETUP_UNITS)
            for t in range(B, 3 * B):
                slot()
                matrix_sum(t)
                if t > B:
                    matrix_lo(t - 1)
            matrix_lo(3 * B - 1)

            def split_set(q):
                V.drain()
                V.tensor_copy(PG[:, :], at(GAIN, q * UPS, UPS))
                done(pg_ready)
                for u in range(UPS):
                    r = (SETUP_UNITS + u) % RS
                    for half in range(2):
                        slot()
                        dve.wait_ge(e_hi, q * (2 * UPS) + (2 * u + half + 1))
                        o = half * (RU // 2)
                        ins = V.scalar_tensor_tensor(STAGE[u][:, RU + o:RU + o + RU // 2], RAW[r][:, o:o + RU // 2],
                                                     PG[:, u:u + 1], STAGE[u][:, o:o + RU // 2], ALU.mult, ALU.subtract)
                        if half:
                            ins.then_inc(raw_free, 1)

            split_set(0)
            with slot.repeat(1, NEW, 2 * UPS) as q:
                split_set(q)
            slot.bare(BARE0)
            a_part(0, slot)
            with dve.Fori(1, NBLK - 1) as k:
                slot = Slots(dve, step, k, V.drain)
                c_part(k, slot, True)
                a_part(k, slot)
            slot = Slots(dve, step, NBLK - 1, V.drain)
            c_part(NBLK - 1, slot, True)
            slot.bare(TB - C_SLOTS)
            rows_in(NBLK - 1)
            V.drain()
            c_part(NBLK, none, False)

        @block.tensor
        def _(pe):
            def products(dst, terms, start=True, stop=True):
                n = len(terms) * 3
                i = 0
                for (ah_, al_), (bh_, bl_) in terms:
                    for l_, r_ in ((al_, bh_), (ah_, bl_), (ah_, bh_)):
                        ins = PE.matmul(dst, l_, r_, start=start and i == 0, stop=stop and i == n - 1)
                        i += 1
                return ins

            pe.sem_inc(a_free, AB)
            pe.wait_ge(s_gen, 6)
            pe.wait_ge(s_ln, 2)
            for c in range(C):
                ins = PE.transpose(DP[0][:, c * B:(c + 1) * B], LNX[:, c * P:(c + 1) * P], IDF[0:B, 0:B])
            ins.then_inc(s_lnT, 1)
            pe.wait_ge(s_tmpw, 32)
            pe.wait_ge(s_ae, 2 * C)
            for w in range(2):
                for m in range(C):
                    for c in range(C):
                        ins = PE.matmul(DP[1][:, (w * C + m) * B:(w * C + m + 1) * B],
                                        tmp("w1_3" if w else "w1_0", P, c * D + m * P),
                                        HC[:, (w * C + c) * B:(w * C + c + 1) * B], start=c == 0, stop=c == C - 1)
            ins.then_inc(s_hc, 1)
            pe.wait_ge(s_eq, 1)
            for k in range(NBLK):
                for i in range(4):
                    ins = PE.matmul(DP[3][:, k * B:(k + 1) * B], EQT[:, i * T + k * TB:i * T + (k + 1) * TB],
                                    EQB[:, i * B:(i + 1) * B], start=i == 0, stop=i == 3)
            ins.then_inc(s_in, 1)
            for m in range(C):
                for c in range(C):
                    ins = PE.matmul(DP[2][:, m * B:(m + 1) * B], tmp("WhhT", P, c * D + m * P), col("condT", B, c * B),
                                    start=c == 0, stop=c == C - 1)
            ins.then_inc(s_hbt, 1)
            pe.wait_ge(s_h, 2 * C)
            def factor(n):
                o, r = (0 if n < F_GROUP else C) * B, f_unit(n)
                pe.wait_ge(raw_in[r % RS], 16 * (r // RS + 1))
                if n >= 2:
                    pe.wait_ge(f_evac, n - 1)
                for kc in range(C):
                    ins = PE.matmul(GP[n % 2][0:B, :], HID[:, o + kc * B:o + (kc + 1) * B],
                                    RAW[r % RS][:, kc * 512:(kc + 1) * 512], start=kc == 0, stop=kc == C - 1)
                ins.then_inc(f_fill, 1)
                PE.drain().then_inc(raw_free, 1)

            def matrix(t):
                if t % B == 0:
                    pe.wait_ge(f_bias, t // B + 1)
                ftv = FT[t // B].rearrange("r (w b d) -> r w b d", w=2, b=B)
                if t >= 2:
                    pe.wait_ge(dw_sum, t - 1)
                for cc in range(C):
                    ins = PE.matmul(DP[2 + t % 2][:, cc * D:(cc + 1) * D], ftv[:, 0, t % B, cc * P:(cc + 1) * P],
                                    ftv[:, 1, t % B, :], start=True, stop=True)
                ins.then_inc(dw_fill, 1)

            for n in range(F_GROUP):
                factor(n)
            for t in range(B):
                matrix(t)
            pe.wait_ge(dw_lo, B)
            pe.wait_ge(res_lo, 1)

            def step(k, dyn, s):
                n, g, h = steps(k, dyn, s), GP[s % 2], H16[s % 2]
                PE.matmul(g[:, 0:64], IDH[:, :], at(XP, s * 64 if isinstance(dyn, int) else dyn * 64 + s * 64, 64),
                          start=True, stop=False)

                def wh(hi, c, m):
                    w = WH if hi else WL
                    o = OFF["Wh_ifo"] + c * 768 + m * P if m < 6 else OFF["Wh_g"] + c * 256 + (m - 6) * P
                    return w[:, o:o + P]
                pe.wait_ge(l_hi, n)
                for m in range(GC):
                    for c in range(C):
                        PE.matmul(g[:, m * 8:m * 8 + 4], wh(False, c, m), h[:, c * 8:c * 8 + 4], start=False, stop=False)
                pe.wait_ge(l_lo, n)
                for m in range(GC):
                    for c in range(C):
                        ins = PE.matmul(g[:, m * 8:m * 8 + 8], wh(True, c, m), h[:, c * 8:c * 8 + 8], start=False,
                                        stop=m == GC - 1 and c == C - 1)
                ins.then_inc(l_pe, 1)

            def d_wait(k, stage, i):
                pe.wait_ge(d_free, d_count(k, stage, i))

            def a_wait(k, stage, i):
                pe.wait_ge(a_free, a_count(k, stage, i))

            def all_freed(k, stage, i):
                pe.wait_ge(d_free, d_count(k, stage, i, DB))

            def a_lows(k, stage, i):
                pe.wait_ge(al, a_count(k, stage, i, 2))

            def transposes(k, stage, src):
                for c in range(C):
                    d_wait(k, stage, c)
                    for j in range(B):
                        ins = PE.transpose(dbank(stage, c)[:, j * P:(j + 1) * P],
                                           src[:, j * D + c * P:j * D + (c + 1) * P], IDF[:, :])
                    ins.then_inc(d_fill, 1)

            def gate_transposes(k, stage, i, src, n, js):
                d_wait(k, stage, i)
                for j in js:
                    ins = PE.transpose(dbank(stage, i)[0:n, (j - js[0]) * P:(j - js[0] + 1) * P], src[:, j * n:(j + 1) * n],
                                       IDF[:, :])
                ins.then_inc(d_fill, 1)

            def xp_half(k, half, ms):
                qv = [t[:, :].rearrange("p (c b s) -> p c b s", c=C, b=B) for t in (QH, QL)]
                hs = slice(half * (TB // 2), (half + 1) * (TB // 2))
                for m in ms:
                    a_wait(k, f"xp{half}", m)
                    products(abank(f"xp{half}", m)[:, 0:NT // 2],
                             [(res("Wx", c * GATES + m * P, P), (qv[0][:, c, :, hs], qv[1][:, c, :, hs]))
                              for c in range(C)]).then_inc(a_fill, 1)

            def a_part(k, slot):
                slot()
                pe.wait_ge(x_in, k * 16 + 32)
                transposes(k, "xT", RX)
                all_freed(k, "xT", C - 1)
                for m in range(C):
                    slot()
                    d_wait(k, "y0T", m)
                    for b in range(B):
                        ins = products(dbank("y0T", m)[:, b * TB:(b + 1) * TB],
                                       [(dwp(0, b, c, m * P, P), pair(QH, QL, c * NT + b * TB, TB)) for c in range(C)])
                    ins.then_inc(d_fill, 1)
                all_freed(k, "y0T", C - 1)
                d_wait(k, "log0", 0)
                for j in range(B):
                    ins = products(dbank("log0", 0)[:, j * E:(j + 1) * E],
                                   [(pair(ZH, ZL, c * NT + j * P, P), res("wgate", c * E, E)) for c in range(C)])
                ins.then_inc(d_fill, 1)
                slot()
                pe.wait_ge(g_mat, plus(k, "mat", "A", 1))
                gate_transposes(k, "g0T", 0, GT, E, range(B))

                def h0(j):
                    d_wait(k, "h0", j)
                    products(dbank("h0", j)[:, :],
                             [(pair(ZH, ZL, c * NT + j * P, P), res("Wd", c * 512, 512)) for c in range(C)]).then_inc(d_fill, 1)

                def h0T(j):
                    pe.wait_ge(h_row, plus(k, "hrow", "A", j + 1))
                    d_wait(k, "h0T", j)
                    for m in range(4):
                        ins = PE.transpose(dbank("h0T", j)[:, m * P:(m + 1) * P], HB[j % 2][:, m * P:(m + 1) * P], IDF[:, :])
                    ins.then_inc(d_fill, 1)

                slot()
                h0(0)
                h0(1)
                slot()
                h0T(0)
                h0(2)
                h0T(1)
                h0(3)
                slot()
                h0T(2)
                h0T(3)
                pe.wait_ge(gt_copy, plus(k, "mat", "A", 1))
                for j in range(B):
                    if j == 2:
                        slot()
                    d_wait(k, "out0", j)
                    all_freed(k, "h0T", j)
                    PE.matmul(dbank("out0", j)[:, 0:D], GTT[0:E, j * P:(j + 1) * P], RB[0:E, RBO["bu"]:RBO["bu"] + D],
                              start=True, stop=False)
                    products(dbank("out0", j)[:, 0:D],
                             [(pair(KH, KL, j * 512 + m * P, P), res("Wu", m * D, D)) for m in range(4)],
                             start=False).then_inc(d_fill, 1)
                slot()
                pe.wait_ge(r_row, plus(k, "rrow", "A", B))
                transposes(k, "x1T", RW)
                all_freed(k, "x1T", C - 1)
                for m in range(0, GC, 4):
                    slot()
                    xp_half(k, 0, range(m, m + 4))

            def up_chunk(k, p, par, m):
                if m == 0:
                    pe.wait_ge(w_in[0][par], p * 16 + ((k - 1) * (16 * (NEW // 2)) + 16))
                pe.wait_ge(a_free, base("a", k, "C") + p * (2 * M1) + (par * M1 + m + 1))
                products(abank("up", m)[:, :],
                         [(ew(0, par, c * H1 + m * P, P), pair(QH, QL, c * NT, NT)) for c in range(C)]).then_inc(a_fill, 1)

            def down(k, p, par, j, h):
                if j == 0 and h == 0:
                    pe.wait_ge(w_in[1][par], p * 16 + ((k - 1) * (16 * (NEW // 2)) + 16))
                if j == 0:
                    pe.wait_ge(al, base("a", k, "C") + p * (2 * M1) + (par * M1 + (h + 1) * (M1 // 2) + 2))
                if h == 0:
                    pe.wait_ge(d_free, base("d", k, "C") + p * (2 * B) + (PLACE["d", "down"][1] + par * B + j + 1))
                ins = products(dbank("down", j)[:, 0:D],
                               [(pair(GH[par], GL[par], m * NT + j * P, P), ew(1, par, m * D, D))
                                for m in range(h * (M1 // 2), (h + 1) * (M1 // 2))], start=h == 0, stop=h == 1)
                if h:
                    ins.then_inc(d_fill, 1)

            def set_in(k, par):
                for half in range(2):
                    pe.wait_ge(w_in[half][par], k * (16 * (NEW // 2)))

            def c_part(k, slot, x):
                pe.wait_ge(l_copy, k * TB + 2)
                for j in range(B):
                    d_wait(k, "log1", j)
                    for c in range(C):
                        ins = PE.matmul(dbank("log1", j)[:, 0:E], HT[:, c * NT + j * P:c * NT + (j + 1) * P],
                                        CENT[:, c * E:(c + 1) * E], start=c == 0, stop=c == C - 1)
                    ins.then_inc(d_fill, 1)
                for j in range(B):
                    d_wait(k, "uT", j)
                    for c in range(C):
                        ins = PE.transpose(dbank("uT", j)[:, c * P:(c + 1) * P], HT[:, c * NT + j * P:c * NT + (j + 1) * P],
                                           IDF[:, :])
                    ins.then_inc(d_fill, 1)
                if x:
                    pe.wait_ge(al, base("a", k, "X") + 2)
                    for m in range(0, GC, 4):
                        slot()
                        xp_half(k, 1, range(m, m + 4))
                slot()
                slot()
                pe.wait_ge(xn_row, k)
                transposes(k, "xnT", UT)
                slot()
                pe.wait_ge(g_mat, plus(k, "mat", "C", 1))
                for h in range(2):
                    gate_transposes(k, "g1T", h, GT, NE1, range(2 * h, 2 * h + 2))
                slot()
                pe.wait_ge(gt_copy, plus(k, "mat", "C", 1))
                for j in range(B):
                    d_wait(k, "bias1", j)
                    PE.matmul(dbank("bias1", j)[:, 0:D], GTT[0:NE1, j * P:(j + 1) * P], RB[0:NE1, RBO["b2"]:RBO["b2"] + D],
                              start=True, stop=True).then_inc(d_fill, 1)
                all_freed(k, "xnT", C - 1)
                for m in range(M1):
                    if m % 2 == 0:
                        slot()
                    up_chunk(k, 0, 0, m)
                with slot.repeat(0, 4, 2 * M1) as p:
                    for par in range(2):
                        for i in range(M1):
                            slot()
                            up_chunk(k, p + par, 1 - par, i)
                            down(k, p, par, i // 2, i % 2)
                for i in range(M1):
                    slot()
                    up_chunk(k, 4, 1, i)
                    down(k, 4, 0, i // 2, i % 2)
                for j in range(B):
                    slot()
                    down(k, 4, 1, j, 0)
                    down(k, 4, 1, j, 1)

                for m in range(C):
                    slot()
                    if m == 0:
                        pe.wait_ge(r_row, plus(k, "rrow", "C", B))
                        transposes(k, "x2T", RES)
                        all_freed(k, "x2T", C - 1)
                    a_wait(k, "z2", m)
                    products(abank("z2", m)[:, :],
                             [(res("Wih", c * D + m * P, P), pair(QH, QL, c * NT, NT)) for c in range(C)]).then_inc(a_fill, 1)
                a_lows(k, "z2", C - 1)
                d_wait(k, "log2", 0)
                for j in range(B):
                    ins = products(dbank("log2", 0)[:, j * E:(j + 1) * E],
                                   [(pair(ZH, ZL, c * NT + j * P, P), res("gatew", c * E, E)) for c in range(C)])
                ins.then_inc(d_fill, 1)
                slot()
                pe.wait_ge(g_mat, plus(k, "mat", "C", 2))
                for h in range(2):
                    gate_transposes(k, "g2T", h, GT, E, range(2 * h, 2 * h + 2))
                slot()
                pe.wait_ge(gt_copy, plus(k, "mat", "C", 2))
                for j in range(B):
                    d_wait(k, "bias2", j)
                    PE.matmul(dbank("bias2", j)[:, 0:D], GTT[0:E, j * P:(j + 1) * P], RB[0:E, RBO["eb"]:RBO["eb"] + D],
                              start=True, stop=True).then_inc(d_fill, 1)
                set_in(k, 0)
                for j in range(B):
                    for w in range(4):
                        if w % 2 == 0:
                            slot()
                        d_wait(k, "exp2", j * 4 + w)
                        products(dbank("exp2", j * 4 + w)[:, :],
                                 [(pair(ZH, ZL, c * NT + j * P, P), ew(c, 0, w * 512, 512))
                                  for c in range(C)]).then_inc(d_fill, 1)

                for m in range(C):
                    slot()
                    if m == 0:
                        pe.wait_ge(pair_add, gated_count(k, 15, 4))
                        transposes(k, "x3T", RES)
                        all_freed(k, "x3T", C - 1)
                    a_wait(k, "mid", m)
                    for b in range(B):
                        ins = products(abank("mid", m)[:, b * TB:(b + 1) * TB],
                                       [(dwp(1, b, c, m * P, P), pair(QH, QL, c * NT + b * TB, TB)) for c in range(C)])
                    ins.then_inc(a_fill, 1)
                slot()
                a_lows(k, "mid", C - 1)
                for m in range(C):
                    d_wait(k, "y3T", m)
                    for b in range(B):
                        ins = products(dbank("y3T", m)[:, b * TB:(b + 1) * TB],
                                       [(dwp(2, b, c, m * P, P), pair(ZH, ZL, c * NT + b * TB, TB)) for c in range(C)])
                    ins.then_inc(d_fill, 1)
                slot()
                pe.wait_ge(yl, k * C)
                d_wait(k, "log3", 0)
                for j in range(B):
                    ins = products(dbank("log3", 0)[:, j * 9:(j + 1) * 9],
                                   [(pair(QH, QL, c * NT + j * P, P), res("egsg", c * 9, 9)) for c in range(C)])
                ins.then_inc(d_fill, 1)
                slot()
                pe.wait_ge(g_mat, plus(k, "mat", "C", 3))
                gate_transposes(k, "g3T", 0, GT, 9, range(B))
                gate_transposes(k, "g3T", 1, GT2, 9, range(B))
                for j in range(B):
                    slot()
                    if j == 0:
                        pe.wait_ge(gt_copy, plus(k, "mat", "C", 3))
                        set_in(k, 1)
                    d_wait(k, "hid3", 6 * j)
                    PE.matmul(dbank("hid3", 6 * j)[:, :], GTT[0:9, j * P:(j + 1) * P], RB[0:9, RBO["eb12"]:RBO["eb12"] + 512],
                              start=True, stop=True).then_inc(d_fill, 1)
                    d_wait(k, "hid3", 6 * j + 1)
                    products(dbank("hid3", 6 * j + 1)[:, 0:256],
                             [(pair(QH, QL, c * NT + j * P, P), res("sw12", c * D, D)) for c in range(C)]).then_inc(d_fill, 1)
                    for w in range(4):
                        if w == 1:
                            slot()
                        d_wait(k, "hid3", 6 * j + 2 + w)
                        products(dbank("hid3", 6 * j + 2 + w)[:, :],
                                 [(pair(QH, QL, c * NT + j * P, P), ew(c, 1, w * 512, 512))
                                  for c in range(C)]).then_inc(d_fill, 1)
                slot()
                slot()
                pe.wait_ge(n_row, k)
                for v in range(2):
                    a_wait(k, "nT", v)
                    for j in range(B):
                        ins = PE.transpose(abank("nT", v)[:, j * P:(j + 1) * P], NTM[:, (v * B + j) * P:(v * B + j + 1) * P],
                                           IDF[:, :])
                    ins.then_inc(a_fill, 1)
                for j in range(B):
                    slot()
                    d_wait(k, "out3", 6 * j)
                    PE.matmul(dbank("out3", 6 * j)[:, 0:D], GTT[0:9, NT + j * P:NT + (j + 1) * P],
                              RB[0:9, RBO["b3"]:RBO["b3"] + D], start=True, stop=True).then_inc(d_fill, 1)
                    if j == 0:
                        a_lows(k, "nT", 1)
                    d_wait(k, "out3", 6 * j + 1)
                    products(dbank("out3", 6 * j + 1)[:, 0:D],
                             [(pair(ZH, ZL, NT + j * P, P), res("sw3", 0, D))]).then_inc(d_fill, 1)
                    for w in range(4):
                        d_wait(k, "out3", 6 * j + 2 + w)
                        products(dbank("out3", 6 * j + 2 + w)[:, :],
                                 [(pair(ZH, ZL, j * P, P), res("ew3", w * 512, 512))]).then_inc(d_fill, 1)

            def factors(k, dyn, s):
                first = F_GROUP + sum(F_SLOTS[:s])
                for n in range(first, first + F_SLOTS[s]):
                    factor(n)

            a_part(-1, Slots(pe, factors, -1))
            none = Slots(pe, None, 0)
            pe.wait_ge(f_evac, F_UNITS)
            pe.wait_ge(al, base("a", 0, "X") + 2)
            slot = Slots(pe, step, 0)
            for m in range(0, GC, 4):
                slot()
                xp_half(0, 1, range(m, m + 4))
            slot.bare(1)
            pe.wait_ge(al, base("a", 0, "A") + 2)
            for t in range(B, 3 * B):
                slot()
                matrix(t)
            pe.wait_ge(dw_lo, 3 * B)
            pe.sem_inc(s_mark, 1)
            slot.bare(NEW * 2 * UPS)
            slot.bare(BARE0)
            a_part(0, slot)
            with pe.Fori(1, NBLK - 1) as k:
                slot = Slots(pe, step, k)
                c_part(k, slot, True)
                a_part(k, slot)
            slot = Slots(pe, step, NBLK - 1)
            c_part(NBLK - 1, slot, True)
            slot.bare(TB - C_SLOTS)
            c_part(NBLK, none, False)


def host_layout(i):
    import numpy as np
    g = {k: np.asarray(v) for k, v in i.items()}

    def chunked(w):
        k, n = w.shape
        return w.reshape(k // P, P, n).transpose(1, 0, 2).reshape(P, -1)

    def column(v):
        return v.reshape(-1, P).T

    def factor(w, b):
        w = w.reshape(C, P, C, P, 2, R // 2).transpose(2, 4, 1, 0, 5, 3)
        return w.reshape(C * 2, P, RU), b.reshape(D, R).T

    n = D * R
    w0, b0 = g["L0_cond_w2"], g["L0_cond_b2"]
    w3, b3 = g["L3_cond_W2"], g["L3_cond_bias2"]
    facts = [factor(w0[:, s * n:(s + 1) * n], b0[s * n:(s + 1) * n]) for s in (0, 1)]
    facts += [factor(w3[:, s * n:(s + 1) * n], b3[s * n:(s + 1) * n]) for s in (2, 3, 1, 0)]

    wh = g["L1_cond_Wh"]
    ew3 = g["L3_ffn_ew3"].transpose(2, 0, 1).reshape(P, E * D)
    egsg = np.concatenate([g["L3_ffn_eg_w"], g["L3_ffn_sg_w"]], 0).T
    resident = {
        "Wh_ifo": chunked(wh[:, 0:768]), "Wh_g": chunked(wh[:, 768:1024]), "Wx": chunked(g["L1_cond_Wx"]), "ew3": ew3,
        "Wd": chunked(g["L0_ffn_Wd"].transpose(1, 0, 2).reshape(D, 512)),
        "Wu": chunked(g["L0_ffn_Wu"].reshape(512, D)), "Wih": chunked(g["L2_cond_W_ih"].T),
        "sw12": chunked(np.concatenate([g["L3_ffn_sw1"].T, g["L3_ffn_sw2"].T], 1)), "sw3": g["L3_ffn_sw3"].T,
        "wgate": chunked(g["L0_ffn_w_gate"]), "gatew": chunked(g["L2_ffn_gate_w"].T), "egsg": chunked(egsg),
    }
    w1 = np.concatenate([g["L1_ffn_W1_s"], g["L1_ffn_W1_r"]], 0)
    w2 = np.concatenate([g["L1_ffn_W2_s"], g["L1_ffn_W2_r"]], 0)
    sets = [np.concatenate([chunked(w1[e]), chunked(w2[e])], 1) for e in range(NE1)]
    sets.append(chunked(g["L2_ffn_expert_w"].transpose(1, 0, 2).reshape(D, E * D)))
    ew12 = np.concatenate([g["L3_ffn_ew1"].transpose(0, 2, 1), g["L3_ffn_ew2"].transpose(0, 2, 1)], 2)
    sets.append(chunked(ew12.transpose(1, 0, 2).reshape(D, E * D)))
    gains = [g["L1_ffn_g_shared"]] * 2 + [g["L1_ffn_g_routed"]] * 8
    b1 = np.concatenate([g["L1_ffn_b1_s"], g["L1_ffn_b1_r"]], 0)
    ones = np.ones((P, UPS), np.float32)
    gain = [np.concatenate([column(gains[e]), ones[:, C:]], 1) for e in range(NE1)] + [ones] * (NEW - NE1)
    cols = {"lstm_b": column(g["L1_cond_b"]), "g0": column(g["L0_cond_ln_g"]), "be0": column(g["L0_cond_ln_b"]),
            "b1_0": column(g["L0_cond_b1"]), "g3": column(g["L3_cond_ln_gamma"]), "be3": column(g["L3_cond_ln_beta"]),
            "b1_3": column(g["L3_cond_bias1"]), "bih": column(g["L2_cond_b_ih"]), "bhh": column(g["L2_cond_b_hh"]),
            "s_g": column(g["L3_ffn_s_ln_g"]), "s_b": column(g["L3_ffn_s_ln_b"]), "sel_g": column(g["L3_ffn_sel_ln_g"]),
            "sel_b": column(g["L3_ffn_sel_ln_b"]), "condT": chunked(g["cond_1024"].T)}
    rows = {"bd": g["L0_ffn_bd"].reshape(-1), "gate_b": g["L2_ffn_gate_b"],
            "egsg_b": np.concatenate([g["L3_ffn_eg_b"], g["L3_ffn_sg_b"]]), "exp_bias": g["L3_ffn_exp_bias"]}
    tmpw = {"w1_0": chunked(g["L0_cond_w1"]), "w1_3": chunked(g["L3_cond_W1"]), "base0": chunked(g["L0_cond_base_layer"]),
            "base_down": chunked(g["L3_cond_base_down"]), "base_upT": chunked(g["L3_cond_base_up"].T),
            "WhhT": chunked(g["L2_cond_W_hh"].T), "cent": chunked(g["L1_ffn_centroids"])}
    rb = np.zeros((16, 1536), np.float32)
    rb[0:E, 0:256] = g["L0_ffn_bu"]
    rb[0:2, 256:512] = g["L1_ffn_b2_s"]
    rb[2:NE1, 256:512] = g["L1_ffn_b2_r"]
    rb[0:E, 512:768] = g["L2_ffn_expert_b"]
    rb[0:E, 768:896] = g["L3_ffn_eb1"]
    rb[0:E, 896:1024] = g["L3_ffn_eb2"]
    rb[E, 1024:1152] = g["L3_ffn_sb1"]
    rb[E, 1152:1280] = g["L3_ffn_sb2"]
    rb[0:E, 1280:1536] = g["L3_ffn_eb3"]
    rb[E, 1280:1536] = g["L3_ffn_sb3"]
    idx = np.concatenate([g["L3_ffn_index_b"].reshape(4, P).T, g["L3_ffn_index_t"].reshape(4, P).T], 1)
    made = {
        "x": g["x"], "cond": g["cond_1024"],
        "factors": np.concatenate([w for w, _ in facts], 0),
        "factor_bias": np.concatenate([b for _, b in facts], 1),
        "resident": np.concatenate([resident[name] for name, _ in RESIDENT], 1),
        "stream": np.stack(sets), "b1": np.concatenate([column(v) for v in b1], 1),
        "gain": np.concatenate(gain, 1),
        "cols": np.concatenate([cols[name] for name, w in COLS if w], 1),
        "rows": np.broadcast_to(np.concatenate([rows[name] for name, _ in ROWS])[None], (P, NROWS)),
        "tmpw": np.concatenate([tmpw[name] for name, _ in TMPW], 1),
        "rb": rb, "idx": idx,
    }
    return {k: np.ascontiguousarray(v) for k, v in made.items()}


def build(nc, arrays):
    a = {k: nc.dram_tensor(f"in_{k}", v.shape, mybir.dt.from_np(v.dtype), kind="ExternalInput").ap()
         for k, v in arrays.items()}
    out = nc.dram_tensor("out_0", (B, T, D), F32, kind="ExternalOutput").ap()
    split = nc.dram_tensor("split_weights", (NEW, 2, P, 2 * HW), F16, kind="Internal").ap()
    turn = nc.dram_tensor("turned_factors", (NFACT, B, 2 * C * 512), F32, kind="Internal").ap()
    adaln_lstm_moe(nc, a, out, split, turn)


def kernel(**inputs):
    import concourse.bacc as bacc
    from concourse.bass_utils import run_bass_kernel_spmd

    nc = bacc.Bacc("TRN2", target_bir_lowering=False, num_devices=1)
    arrays = host_layout(inputs)
    build(nc, arrays)
    r = run_bass_kernel_spmd(nc, [{f"in_{k}": v for k, v in arrays.items()}], core_ids=[0])
    return r.results[0]["out_0"]
```
